# Optimizing a Trainium2 kernel written in Bass

```python
import numpy as np
import jax
import jax.numpy as jnp

def _softmax(x, axis=-1):
    return jax.nn.softmax(x, axis=axis)

def _gelu(x):
    return jax.nn.gelu(x, approximate=True)

def _silu(x):
    return jax.nn.silu(x)

def _sigmoid(x):
    return jax.nn.sigmoid(x)

def _layernorm(x, axis=-1, eps=1e-05):
    m = jnp.mean(x, axis=axis, keepdims=True)
    v = jnp.var(x, axis=axis, keepdims=True)
    return (x - m) / jnp.sqrt(v + eps)

def _scatter_add(tgt, idx, src, axis=0):
    return tgt.at[idx].add(src)

def _segment_sum(src, seg, n):
    return jax.ops.segment_sum(src, seg, n)
kernel_name = 'mk_audio_tower_d1_tok_audfeat256_r4_e2b839'

def setup_inputs(seed: int=0):
    np.random.seed(seed)
    _w = jnp.asarray

    def _rec_inputs():
        import jax
        import jax.numpy as jnp
        _rk = jax.random.key(seed)
        x = -0.00197248 + 1.00072 * jax.random.normal(jax.random.fold_in(_rk, 1), (64, 1, 10240), jnp.float32)
        return x
    x = _rec_inputs()

    def _L0_tok_setup():
        import jax, jax.numpy as jnp
        import numpy as np
        B, L = (4, 10240)
        C = 128
        DMLP = 512
        TEMP = 1e-05
        EPS = 1e-05
        FACTOR = 2

        def _conv(x, w, b, stride, pad):
            x = jnp.pad(x, ((0, 0), (0, 0), (pad, pad)), mode='reflect')
            y = jax.lax.conv_general_dilated(x, w, (stride,), 'VALID', dimension_numbers=('NCH', 'OIH', 'NCH'))
            return y + b[None, :, None]

        def _cnorm(x, g, b):
            m = jnp.mean(x, axis=1, keepdims=True)
            v = jnp.var(x, axis=1, keepdims=True, ddof=1)
            return (x - m) * jax.lax.rsqrt(v + EPS) * g[None, :, None] + b[None, :, None]

        def _forward(x, conv0_w, conv0_b, conv1_w, conv1_b, conv2_w, conv2_b, conv3_w, conv3_b, n0_w, n0_b, n1_w, n1_b, n2_w, n2_b, n3_w, n3_b, n4_w, n4_b, mlp_w1, mlp_b1, mlp_w2, mlp_b2, mlp_w3, mlp_b3):
            h = jax.nn.relu(_cnorm(_conv(x, conv0_w, conv0_b, 5, 3), n0_w, n0_b))
            h = jax.nn.relu(_cnorm(_conv(h, conv1_w, conv1_b, 4, 2), n1_w, n1_b))
            h = jax.nn.relu(_cnorm(_conv(h, conv2_w, conv2_b, 2, 1), n2_w, n2_b))
            h = jax.nn.relu(_cnorm(_conv(h, conv3_w, conv3_b, 2, 1), n3_w, n3_b))
            f = jnp.transpose(h, (0, 2, 1))
            T = f.shape[1]
            z = jax.nn.gelu(f @ mlp_w1 + mlp_b1, approximate=False)
            z = jax.nn.gelu(z @ mlp_w2 + mlp_b2, approximate=False)
            imp = jax.nn.sigmoid((z @ mlp_w3 + mlp_b3)[..., 0]) + TEMP
            imp = imp / jnp.sum(imp, axis=1, keepdims=True) * (T / FACTOR)
            Tn = T // FACTOR
            cs = jnp.cumsum(imp, axis=1)
            p = jnp.maximum(cs[:, :, None] - jnp.arange(Tn, dtype=cs.dtype)[None, None, :], 0.0)
            pc = jnp.pad(p, ((0, 0), (0, 0), (0, 1)))
            d = pc[:, :, :-1] - pc[:, :, 1:]
            wmat = d - jnp.pad(d, ((0, 0), (1, 0), (0, 0)))[:, :-1, :]
            pooled = jnp.einsum('btn,btc->bnc', wmat, f)
            out = jnp.transpose(pooled, (0, 2, 1))
            return jax.nn.relu(_cnorm(out, n4_w, n4_b))
        key = jax.random.key(seed)
        ks = jax.random.split(key, 8)

        def w(k, shape, fan_in):
            return jax.random.normal(k, shape, jnp.float32) / np.float32(np.sqrt(fan_in))
        inp = {'x': jax.random.normal(ks[0], (B, 1, L), jnp.float32), 'conv0_w': w(ks[1], (C, 1, 10), 10), 'conv0_b': jnp.zeros(C, jnp.float32), 'conv1_w': w(ks[2], (C, C, 8), C * 8), 'conv1_b': jnp.zeros(C, jnp.float32), 'conv2_w': w(ks[3], (C, C, 4), C * 4), 'conv2_b': jnp.zeros(C, jnp.float32), 'conv3_w': w(ks[4], (C, C, 4), C * 4), 'conv3_b': jnp.zeros(C, jnp.float32), 'mlp_w1': w(ks[5], (C, DMLP), C), 'mlp_b1': jnp.zeros(DMLP, jnp.float32), 'mlp_w2': w(ks[6], (DMLP, DMLP), DMLP), 'mlp_b2': jnp.zeros(DMLP, jnp.float32), 'mlp_w3': w(ks[7], (DMLP, 1), DMLP), 'mlp_b3': jnp.zeros(1, jnp.float32)}
        for i in range(5):
            inp[f'n{i}_w'] = jnp.ones(C, jnp.float32)
            inp[f'n{i}_b'] = jnp.zeros(C, jnp.float32)
        return inp
    _L0_tok_all = _L0_tok_setup()
    _L0_tok_in = {k: v for k, v in _L0_tok_all.items() if k in ('conv0_w', 'conv0_b', 'conv1_w', 'conv1_b', 'conv2_w', 'conv2_b', 'conv3_w', 'conv3_b', 'n0_w', 'n0_b', 'n1_w', 'n1_b', 'n2_w', 'n2_b', 'n3_w', 'n3_b', 'n4_w', 'n4_b', 'mlp_w1', 'mlp_b1', 'mlp_w2', 'mlp_b2', 'mlp_w3', 'mlp_b3')}
    del _L0_tok_all

    def _L0_attn_setup():
        import jax, jax.numpy as jnp
        import numpy as np
        key = jax.random.key(seed)
        ks = jax.random.split(key, 4)
        B, S, D = (4, 1024, 64)
        x = jax.random.normal(ks[0], (B, S, D), dtype=jnp.float32)
        Wq = jax.random.normal(ks[1], (D, D), dtype=jnp.float32) * 0.02
        Wk = jax.random.normal(ks[2], (D, D), dtype=jnp.float32) * 0.02
        Wv = jax.random.normal(ks[3], (D, D), dtype=jnp.float32) * 0.02
        bq = jnp.zeros((D,), dtype=jnp.float32)
        bk = jnp.zeros((D,), dtype=jnp.float32)
        bv = jnp.zeros((D,), dtype=jnp.float32)
        return {'x': x, 'Wq': Wq, 'bq': bq, 'Wk': Wk, 'bk': bk, 'Wv': Wv, 'bv': bv}
    _L0_attn_all = _L0_attn_setup()
    _L0_attn_in = {k: v for k, v in _L0_attn_all.items() if k in ('Wq', 'bq', 'Wk', 'bk', 'Wv', 'bv')}
    del _L0_attn_all

    def _L0_ffn_setup():
        import jax, jax.numpy as jnp
        import numpy as np
        B, T, IN_DIM = (64, 64, 64)
        HID, OUT_DIM = (128, 64)
        N_LAYERS, N_EXPERTS, N_SHARED = (2, 16, 1)
        key = jax.random.key(seed)
        ks = jax.random.split(key, 10)
        s = 0.02
        x = jax.random.normal(ks[0], (B, T, IN_DIM), dtype=jnp.float32)
        route_id = jax.random.randint(ks[1], (B,), 0, N_EXPERTS)
        Wi = jax.random.normal(ks[2], (HID, IN_DIM), dtype=jnp.float32) * s
        bi = jnp.zeros((HID,), dtype=jnp.float32)
        Wr = jax.random.normal(ks[3], (N_LAYERS, N_EXPERTS, HID, HID), dtype=jnp.float32) * s
        br = jax.random.normal(ks[4], (N_LAYERS, N_EXPERTS, HID), dtype=jnp.float32) * s
        Ws = jax.random.normal(ks[5], (N_LAYERS, N_SHARED, HID, HID), dtype=jnp.float32) * s
        bs = jax.random.normal(ks[6], (N_LAYERS, N_SHARED, HID), dtype=jnp.float32) * s
        Wo = jax.random.normal(ks[7], (OUT_DIM, HID), dtype=jnp.float32) * s
        bo = jnp.zeros((OUT_DIM,), dtype=jnp.float32)
        return {'x': x, 'route_id': route_id, 'Wi': Wi, 'bi': bi, 'Wr': Wr, 'br': br, 'Ws': Ws, 'bs': bs, 'Wo': Wo, 'bo': bo}
    _L0_ffn_all = _L0_ffn_setup()
    _L0_ffn_in = {k: v for k, v in _L0_ffn_all.items() if k in ('route_id', 'Wi', 'bi', 'Wr', 'br', 'Ws', 'bs', 'Wo', 'bo')}
    del _L0_ffn_all
    return {'x': x, 'L0_tok_conv0_w': _L0_tok_in['conv0_w'], 'L0_tok_conv0_b': _L0_tok_in['conv0_b'], 'L0_tok_conv1_w': _L0_tok_in['conv1_w'], 'L0_tok_conv1_b': _L0_tok_in['conv1_b'], 'L0_tok_conv2_w': _L0_tok_in['conv2_w'], 'L0_tok_conv2_b': _L0_tok_in['conv2_b'], 'L0_tok_conv3_w': _L0_tok_in['conv3_w'], 'L0_tok_conv3_b': _L0_tok_in['conv3_b'], 'L0_tok_n0_w': _L0_tok_in['n0_w'], 'L0_tok_n0_b': _L0_tok_in['n0_b'], 'L0_tok_n1_w': _L0_tok_in['n1_w'], 'L0_tok_n1_b': _L0_tok_in['n1_b'], 'L0_tok_n2_w': _L0_tok_in['n2_w'], 'L0_tok_n2_b': _L0_tok_in['n2_b'], 'L0_tok_n3_w': _L0_tok_in['n3_w'], 'L0_tok_n3_b': _L0_tok_in['n3_b'], 'L0_tok_n4_w': _L0_tok_in['n4_w'], 'L0_tok_n4_b': _L0_tok_in['n4_b'], 'L0_tok_mlp_w1': _L0_tok_in['mlp_w1'], 'L0_tok_mlp_b1': _L0_tok_in['mlp_b1'], 'L0_tok_mlp_w2': _L0_tok_in['mlp_w2'], 'L0_tok_mlp_b2': _L0_tok_in['mlp_b2'], 'L0_tok_mlp_w3': _L0_tok_in['mlp_w3'], 'L0_tok_mlp_b3': _L0_tok_in['mlp_b3'], 'L0_attn_Wq': _L0_attn_in['Wq'], 'L0_attn_bq': _L0_attn_in['bq'], 'L0_attn_Wk': _L0_attn_in['Wk'], 'L0_attn_bk': _L0_attn_in['bk'], 'L0_attn_Wv': _L0_attn_in['Wv'], 'L0_attn_bv': _L0_attn_in['bv'], 'L0_ffn_route_id': _L0_ffn_in['route_id'], 'L0_ffn_Wi': _L0_ffn_in['Wi'], 'L0_ffn_bi': _L0_ffn_in['bi'], 'L0_ffn_Wr': _L0_ffn_in['Wr'], 'L0_ffn_br': _L0_ffn_in['br'], 'L0_ffn_Ws': _L0_ffn_in['Ws'], 'L0_ffn_bs': _L0_ffn_in['bs'], 'L0_ffn_Wo': _L0_ffn_in['Wo'], 'L0_ffn_bo': _L0_ffn_in['bo']}

def reference(x, L0_tok_conv0_w, L0_tok_conv0_b, L0_tok_conv1_w, L0_tok_conv1_b, L0_tok_conv2_w, L0_tok_conv2_b, L0_tok_conv3_w, L0_tok_conv3_b, L0_tok_n0_w, L0_tok_n0_b, L0_tok_n1_w, L0_tok_n1_b, L0_tok_n2_w, L0_tok_n2_b, L0_tok_n3_w, L0_tok_n3_b, L0_tok_n4_w, L0_tok_n4_b, L0_tok_mlp_w1, L0_tok_mlp_b1, L0_tok_mlp_w2, L0_tok_mlp_b2, L0_tok_mlp_w3, L0_tok_mlp_b3, L0_attn_Wq, L0_attn_bq, L0_attn_Wk, L0_attn_bk, L0_attn_Wv, L0_attn_bv, L0_ffn_route_id, L0_ffn_Wi, L0_ffn_bi, L0_ffn_Wr, L0_ffn_br, L0_ffn_Ws, L0_ffn_bs, L0_ffn_Wo, L0_ffn_bo):
    import jax
    import jax.numpy as jnp

    def _L0_tok_ref(x, conv0_w, conv0_b, conv1_w, conv1_b, conv2_w, conv2_b, conv3_w, conv3_b, n0_w, n0_b, n1_w, n1_b, n2_w, n2_b, n3_w, n3_b, n4_w, n4_b, mlp_w1, mlp_b1, mlp_w2, mlp_b2, mlp_w3, mlp_b3):
        import jax, jax.numpy as jnp
        import numpy as np
        B, L = (4, 10240)
        C = 128
        DMLP = 512
        TEMP = 1e-05
        EPS = 1e-05
        FACTOR = 2

        def _conv(x, w, b, stride, pad):
            x = jnp.pad(x, ((0, 0), (0, 0), (pad, pad)), mode='reflect')
            y = jax.lax.conv_general_dilated(x, w, (stride,), 'VALID', dimension_numbers=('NCH', 'OIH', 'NCH'))
            return y + b[None, :, None]

        def _cnorm(x, g, b):
            m = jnp.mean(x, axis=1, keepdims=True)
            v = jnp.var(x, axis=1, keepdims=True, ddof=1)
            return (x - m) * jax.lax.rsqrt(v + EPS) * g[None, :, None] + b[None, :, None]

        def _forward(x, conv0_w, conv0_b, conv1_w, conv1_b, conv2_w, conv2_b, conv3_w, conv3_b, n0_w, n0_b, n1_w, n1_b, n2_w, n2_b, n3_w, n3_b, n4_w, n4_b, mlp_w1, mlp_b1, mlp_w2, mlp_b2, mlp_w3, mlp_b3):
            h = jax.nn.relu(_cnorm(_conv(x, conv0_w, conv0_b, 5, 3), n0_w, n0_b))
            h = jax.nn.relu(_cnorm(_conv(h, conv1_w, conv1_b, 4, 2), n1_w, n1_b))
            h = jax.nn.relu(_cnorm(_conv(h, conv2_w, conv2_b, 2, 1), n2_w, n2_b))
            h = jax.nn.relu(_cnorm(_conv(h, conv3_w, conv3_b, 2, 1), n3_w, n3_b))
            f = jnp.transpose(h, (0, 2, 1))
            T = f.shape[1]
            z = jax.nn.gelu(f @ mlp_w1 + mlp_b1, approximate=False)
            z = jax.nn.gelu(z @ mlp_w2 + mlp_b2, approximate=False)
            imp = jax.nn.sigmoid((z @ mlp_w3 + mlp_b3)[..., 0]) + TEMP
            imp = imp / jnp.sum(imp, axis=1, keepdims=True) * (T / FACTOR)
            Tn = T // FACTOR
            cs = jnp.cumsum(imp, axis=1)
            p = jnp.maximum(cs[:, :, None] - jnp.arange(Tn, dtype=cs.dtype)[None, None, :], 0.0)
            pc = jnp.pad(p, ((0, 0), (0, 0), (0, 1)))
            d = pc[:, :, :-1] - pc[:, :, 1:]
            wmat = d - jnp.pad(d, ((0, 0), (1, 0), (0, 0)))[:, :-1, :]
            pooled = jnp.einsum('btn,btc->bnc', wmat, f)
            out = jnp.transpose(pooled, (0, 2, 1))
            return jax.nn.relu(_cnorm(out, n4_w, n4_b))
        return _forward(x, conv0_w, conv0_b, conv1_w, conv1_b, conv2_w, conv2_b, conv3_w, conv3_b, n0_w, n0_b, n1_w, n1_b, n2_w, n2_b, n3_w, n3_b, n4_w, n4_b, mlp_w1, mlp_b1, mlp_w2, mlp_b2, mlp_w3, mlp_b3)

    def _L0_attn_ref(x, Wq, bq, Wk, bk, Wv, bv):
        import jax, jax.numpy as jnp
        import numpy as np
        Q = jnp.einsum('bsd,de->bse', x, Wq) + bq
        K = jnp.einsum('bsd,de,->bse'.replace(',->', '->'), x, Wk) + bk
        V = jnp.einsum('bsd,de->bse', x, Wv) + bv
        scale = 1.0 / jnp.sqrt(jnp.asarray(Q.shape[-1], dtype=jnp.float32))
        scores = jnp.einsum('bqd,bkd->bqk', Q, K) * scale
        weights = jax.nn.softmax(scores, axis=-1)
        return jnp.einsum('bqk,bkd->bqd', weights, V)

    def _L0_ffn_ref(x, route_id, Wi, bi, Wr, br, Ws, bs, Wo, bo):
        import jax, jax.numpy as jnp
        import numpy as np
        B, T, IN_DIM = (64, 64, 64)
        HID, OUT_DIM = (128, 64)
        N_LAYERS, N_EXPERTS, N_SHARED = (2, 16, 1)
        flat = x.reshape(-1, x.shape[-1])
        n_tok = flat.shape[0]
        route = jnp.repeat(route_id, n_tok // route_id.shape[0])
        h = jax.nn.relu(flat @ Wi.T + bi)
        n_layers, n_experts = (Wr.shape[0], Wr.shape[1])
        for l in range(n_layers):
            shared = (jnp.einsum('nd,shd->snh', h, Ws[l]) + bs[l][:, None, :]).mean(axis=0)
            routed = jnp.zeros_like(h)
            for e in range(n_experts):
                ye = h @ Wr[l, e].T + br[l, e]
                routed = routed + jnp.where((route == e)[:, None], ye, 0.0)
            h = jax.nn.relu(shared + routed + h)
        out = h @ Wo.T + bo
        return out.reshape(*x.shape[:-1], out.shape[-1])
    h = _L0_tok_ref(x, L0_tok_conv0_w, L0_tok_conv0_b, L0_tok_conv1_w, L0_tok_conv1_b, L0_tok_conv2_w, L0_tok_conv2_b, L0_tok_conv3_w, L0_tok_conv3_b, L0_tok_n0_w, L0_tok_n0_b, L0_tok_n1_w, L0_tok_n1_b, L0_tok_n2_w, L0_tok_n2_b, L0_tok_n3_w, L0_tok_n3_b, L0_tok_n4_w, L0_tok_n4_b, L0_tok_mlp_w1, L0_tok_mlp_b1, L0_tok_mlp_w2, L0_tok_mlp_b2, L0_tok_mlp_w3, L0_tok_mlp_b3)
    h = h + _L0_attn_ref(_layernorm(h, axis=-1), L0_attn_Wq, L0_attn_bq, L0_attn_Wk, L0_attn_bk, L0_attn_Wv, L0_attn_bv)
    h = h + _L0_ffn_ref(_layernorm(h, axis=-1), L0_ffn_route_id, L0_ffn_Wi, L0_ffn_bi, L0_ffn_Wr, L0_ffn_br, L0_ffn_Ws, L0_ffn_bs, L0_ffn_Wo, L0_ffn_bo)
    return h

_drawn_inputs = setup_inputs


def setup_inputs(seed=0):
    import zlib

    import numpy as np

    out = dict(_drawn_inputs(seed))
    spreads = {'L0_tok_conv0_b': (0.0, 0.1),
     'L0_tok_conv1_b': (0.0, 0.1),
     'L0_tok_conv2_b': (0.0, 0.1),
     'L0_tok_conv3_b': (0.0, 0.1),
     'L0_tok_n0_w': (1.0, 0.2),
     'L0_tok_n0_b': (0.0, 0.1),
     'L0_tok_n1_w': (1.0, 0.2),
     'L0_tok_n1_b': (0.0, 0.1),
     'L0_tok_n2_w': (1.0, 0.2),
     'L0_tok_n2_b': (0.0, 0.1),
     'L0_tok_n3_w': (1.0, 0.2),
     'L0_tok_n3_b': (0.0, 0.1),
     'L0_tok_n4_w': (1.0, 0.2),
     'L0_tok_n4_b': (0.0, 0.1),
     'L0_tok_mlp_b1': (0.0, 0.508),
     'L0_tok_mlp_b2': (0.0, 0.355),
     'L0_attn_bq': (0.0, 0.8),
     'L0_attn_bk': (0.0, 0.8),
     'L0_attn_bv': (0.0, 0.1),
     'L0_ffn_bi': (0.0, 0.43),
     'L0_ffn_bo': (0.0, 0.1)}
    factors = {'L0_attn_Wq': 8.0,
     'L0_attn_Wk': 8.0,
     'L0_attn_Wv': 5.172,
     'L0_ffn_Wr': 5.808,
     'L0_ffn_br': 8.0,
     'L0_ffn_Ws': 5.976,
     'L0_ffn_bs': 8.0}
    for name, (base, spread) in spreads.items():
        noise = np.random.default_rng([zlib.crc32(name.encode()), seed]).standard_normal(out[name].shape)
        drawn = base * np.exp(spread * noise) if base else spread * noise
        out[name] = jnp.asarray(drawn.astype(out[name].dtype))
    for name, factor in factors.items():
        out[name] = (out[name] * factor).astype(out[name].dtype)
    return out
```

```python
from contextlib import ExitStack

import concourse.bass as bass
from concourse import mybir

F32 = mybir.dt.float32
F32R = mybir.dt.float32r
BF16 = mybir.dt.bfloat16
I32 = mybir.dt.int32
ALU = mybir.AluOpType
ACT = mybir.ActivationFunctionType
AX = mybir.AxisListType

P = 128
B = 64
L = 10240
EPS = 1e-5
TEMP = 1e-5
T0, T1, T2, T3 = 2048, 512, 256, 128
K0, STR0 = 10, 5
LPAD = L + 6
GS = 4
NG = B // GS
HALF = T0 // 2
XW = STR0 * (HALF - 1) + K0 + 0
NTAP = K0 + 1
ROWS = 36
K0ROWS = 3 * ROWS
BLK = 8
BW = STR0 * (BLK - 1) + K0
NBLK = HALF // BLK
NB8 = 4 * BLK
NSTEP = NBLK // 4
DM = 512
KC = DM // P
NE = 16
EW = P + 1
D = 64

CB, CG, CN = 0, 3, 6
CG4, CN4, CM1, CM2, CW3, CBQ, CBK, CBI = 9, 10, 11, 15, 19, 23, 24, 25
NCOLS = 26
FAR = 1e30
W = 2

ROW1, ROW2, ROW3 = 0, 4, 6
NTILE = 7


def conv_tiles(g):
    return ([(1, s) for s in range(4)] if g < NG else []) + ([(3, 0)] if 0 <= g - 2 < NG else []) + \
        ([(2, 0), (2, 1)] if 0 <= g - 1 < NG else [])


def norm_tiles(g):
    return ([(2, 0), (2, 1)] if 0 <= g - 2 < NG else []) + \
        ([(1, s) for s in range(4)] if 0 <= g - 1 < NG else []) + ([(3, 0)] if 0 <= g - 3 < NG else [])


LOOP_FROM, LOOP_TO = 3, 15
LAST = NG + 2
FULL = conv_tiles(LOOP_FROM)
FULLN = norm_tiles(LOOP_FROM)


def before(g, tiles, full_from):
    if isinstance(g, int):
        return sum(len(tiles(i)) for i in range(g))
    return g * NTILE + (sum(len(tiles(i)) for i in range(full_from)) - NTILE * full_from)


def convs_before(g):
    return before(g, conv_tiles, 2)


def norms_before(g):
    return before(g, norm_tiles, 3)


def until(eng, sem, count):
    if isinstance(count, int) and count <= 0:
        return
    eng.wait_ge(sem, count)


def waits_behind(eng, sem, count, *others):
    others = [(s, c if isinstance(c, int) else eng.compute_val(c)) for s, c in others]
    eng.wait_ge(sem, count)
    for s, c in others:
        until(eng, s, c)


def each_iteration(eng, step):
    for g in range(LOOP_FROM):
        step(g, g % 2)
    with eng.Fori(0, (LOOP_TO - LOOP_FROM) // 2) as i:
        for d in range(2):
            step(i * 2 + (LOOP_FROM + d), (LOOP_FROM + d) % 2)
    for g in range(LOOP_TO, LAST + 1):
        step(g, g % 2)


def each_pair(eng, pair):
    pair(0)
    with eng.Fori(1, NSTEP // 2) as i:
        pair(i)


def has(g, what):
    if not isinstance(g, int):
        return True
    return {"conv1": g < NG, "conv2": 0 <= g - 1 < NG, "conv3": 0 <= g - 2 < NG, "next": g + 1 < NG,
            "batch": 0 <= g - 1 and g <= LAST}[what]


def tiles_of(g, tiles, full):
    return tiles(g) if isinstance(g, int) else full


def audio_kernel(nc, a, out):
    with ExitStack() as ctx:
        F = ctx.enter_context(nc.sbuf_tensor("F", [P, B * T3], F32))
        cols = ctx.enter_context(nc.sbuf_tensor("cols", [P, NCOLS], F32))
        ident = ctx.enter_context(nc.sbuf_tensor("ident", [P, P], F32))
        LG = ctx.enter_context(nc.sbuf_tensor("LG", [B, 2, T3], F32))
        bank = [ctx.enter_context(nc.psum_tensor(f"bank{i}", [P, 512], F32)) for i in range(8)]
        convolutions(nc, a, ctx, bank, F, cols, ident)
        importance_mlp(nc, a, ctx, bank, F, cols, LG)
        pool_attend_experts(nc, a, ctx, bank, F, cols, ident, LG, out)


def convolutions(nc, a, outer, bank, F, cols, ident):
    with ExitStack() as ctx:
        def sb(name, shape, dt=F32, at=None):
            return (at or ctx).enter_context(nc.sbuf_tensor(name, shape, dt))

        def sem(name):
            return outer.enter_context(nc.semaphore(name))

        convs = ctx.enter_context(ExitStack())
        wc = sb("wc", [P, 2, 16, P], F32R, convs)
        W0 = sb("W0", [K0ROWS, P], BF16, convs)
        selV = sb("selV", [P, NTILE, P], F32R, convs)
        selB = sb("selB", [96, NTILE, P], BF16, convs)
        bc = sb("bc", [P, 3], F32, convs)
        R = sb("R", [K0ROWS, 4, T0], BF16, convs)
        RS = sb("RS", [96, T1], BF16, convs)
        vs = sb("vs", [NTILE + 1, T1], F32, convs)
        iv = sb("iv", [NTILE + 1, T1], F32, convs)
        rs = sb("rs", [NTILE + 1, T1], F32, convs)
        rr = sb("rr", [NTILE + 1, T1], F32, convs)
        mt = sb("mt", [NTILE + 1, T1], BF16, convs)

        with ExitStack() as st:
            xs = sb("xs", [P, XW], F32, st)
            xst = sb("xst", [P, 2, 4 * BLK * STR0 + 5], F32, st)
            X45 = sb("X45", [64, 2, 4 * P], F32, st)
            TG = sb("TG", [BW + 1, BLK, NTAP], F32, st)
            Gs = sb("Gs", [NTAP, NTAP], F32, st)
            c0 = sb("c0", [P, NTAP], F32, st)
            c0c = sb("c0c", [P, NTAP], F32, st)
            onesC = sb("onesC", [P, P], F32, st)
            prod = sb("prod", [P, 2, 4 * BLK * K0], F32, st)
            red = sb("red", [P, 2, 4 * BLK], F32, st)
            var0 = sb("var0", [P, HALF], F32, st)
            rstd0 = sb("rstd0", [P, HALF], F32, st)
            ps = sb("ps", [P, 2, HALF], F32, st)
            rt = sb("rt", [P, 2, HALF], F32, st)
            S = sb("S", [P, 3, 3, HALF], BF16, st)
            ones_bf = sb("ones_bf", [P, HALF], BF16, st)
            wraw = sb("wraw", [P, 16, P], F32, st)
            wmean = sb("wmean", [P, 16], F32, st)
            w0 = sb("w0", [K0ROWS, 2, P], F32, st)
            w0k = sb("w0k", [K0ROWS, 4], F32, st)
            w0m = sb("w0m", [K0ROWS, 2], F32, st)
            w0t = sb("w0t", [K0ROWS, 2, P], F32, st)
            w0p = sb("w0p", [K0ROWS, 3, P], BF16, st)
            selBf = sb("selBf", [96, NTILE, P], F32, st)

        with ExitStack() as cv:
            A0 = sb("A0", [P, 2, 2, 4, T1 + 2], F32R, cv)
            A1 = sb("A1", [P, 2, 2, GS, T2 + 2], F32R, cv)
            A2 = sb("A2", [P, 2, 2, GS, T3 + 2], F32R, cv)
            Y = sb("Y", [P, 2, NTILE, T1], F32, cv)
            sqh = sb("sqh", [P, 2, T1], F32R, cv)
            sql = sb("sql", [P, 2, T1], F32R, cv)
            sqf = sb("sqf", [P, 2, T1], F32, cv)
            N = sb("N", [P, 2, T1], F32, cv)
            AF = sb("AF", [P, 2, T1], F32, cv)
        scratch = nc.dram_tensor("scratch", (ROWS, B * T0), BF16, kind="Internal").ap()

        P0, C1, V, RB, C2, C3 = bank[0:2], bank[2:4], bank[4], bank[5], bank[6], bank[7]

        x_in = sem("x_in")
        c0_in = sem("c0_in")
        w_in = sem("w_in")
        const_in = sem("const_in")
        ones_set = sem("ones_set")
        tg_clear = sem("tg_clear")
        gram_steps = sem("gram_steps")
        gram_act = sem("gram_act")
        tg_in = sem("tg_in")
        staged = sem("staged")
        turned = sem("turned")
        x45_ready = sem("x45_ready")
        quad_done = sem("quad_done")
        prod_done = sem("prod_done")
        red_done = sem("red_done")
        var_ready = sem("var_ready")
        inv_ready = sem("inv_ready")
        rstd_ready = sem("rstd_ready")
        scaled = sem("scaled")
        high_ready = sem("high_ready")
        rest_ready = sem("rest_ready")
        mid_ready = sem("mid_ready")
        low_ready = sem("low_ready")
        rows_out = [sem(f"rows_out{i}") for i in range(3)]
        ones_out = sem("ones_out")
        wsetup = sem("wsetup")
        psetup = sem("psetup")
        r_in = [sem(f"r_in{i}") for i in range(4)]
        conv0_done = sem("conv0_done")
        h0_high = sem("h0_high")
        h0_low = sem("h0_low")
        h0_pads = sem("h0_pads")
        conv1_done = sem("conv1_done")
        conv2_done = sem("conv2_done")
        conv3_done = sem("conv3_done")
        y_done = sem("y_done")
        sq_done = sem("sq_done")
        sql_done = sem("sql_done")
        var_done = sem("var_done")
        vs_done = sem("vs_done")
        iv_done = sem("iv_done")
        rs_done = sem("rs_done")
        parts_done = sem("parts_done")
        spread = sem("spread")
        n_done = sem("n_done")
        relu_done = sem("relu_done")
        ah_done = sem("ah_done")
        al_done = sem("al_done")
        a_pads = sem("a_pads")

        def phases(r0):
            return xs[:, r0:r0 + STR0 * (HALF - 1) + 1:STR0].rearrange("p (q r) -> p r q", r=4)

        block = ctx.enter_context(nc.Block())

        @block.sync
        def _(sp):
            for h in range(2):
                src = a["xpad"][:, STR0 * HALF * h:STR0 * HALF * h + XW]
                sp.dma_start(xs[64 * h:64 * h + 64, :], src).then_inc(x_in, 16)
            sp.dma_start(wraw[:, :, :], a["wconv"]).then_inc(w_in, 16)
            sp.wait_ge(tg_clear, 1)
            sp.wait_ge(gram_act, 1)
            for t in range(BLK):
                sp.dma_start(TG[STR0 * t:STR0 * t + K0, t, :], Gs[0:K0, :]).then_inc(tg_in, 16)
                sp.dma_start(TG[BW:BW + 1, t, :], Gs[K0:K0 + 1, :]).then_inc(tg_in, 16)
            sp.wait_ge(ones_set, 2)
            for i in range(3 * NTAP, ROWS):
                sp.dma_start(scratch[i, :].rearrange("(p t) -> p t", p=P), ones_bf[:, :]).then_inc(ones_out, 16)
            for k in range(NTAP):
                sp.wait_ge(low_ready, k + 1)
                for h in range(2):
                    for part in range(3):
                        dst = scratch[part * NTAP + k, :].rearrange("(b r e q) -> b r e q", b=B, r=4, e=2)
                        src = S[64 * h:64 * h + 64, k % 3, part, :].rearrange("b (r q) -> b r q", r=4)
                        sp.dma_start(dst[:, :, h, :], src).then_inc(rows_out[k % 3], 16)
            sp.wait_ge(ones_out, 16 * (ROWS - 3 * NTAP))
            for i in range(3):
                sp.wait_ge(rows_out[i], 96 * len(range(i, NTAP, 3)))

            def load(clip, slot):
                for q in range(3):
                    src = scratch[:, bass.ds(clip * T0, T0)]
                    sp.dma_start(R[ROWS * q:ROWS * (q + 1), slot, :], src).then_inc(r_in[slot], 16)

            for s in range(4):
                load(s, s)
            with sp.Fori(0, NG - 1) as i:
                for s in range(4):
                    sp.wait_ge(conv0_done, i * 16 + (4 * s + 4))
                    load(i * 4 + (4 + s), s)

        @block.gpsimd
        def _(pool):
            pool.wait_ge(x_in, 32)
            W = NB8 * STR0

            def stage(i):
                for d in range(2):
                    waits_behind(pool, x_in, 32, (turned, i * 2 + (d - 1)))
                    nc.gpsimd.tensor_copy(xst[:, d, 0:W + 5], xs[:, bass.ds(i * (2 * W) + d * W, W + 5)]).then_inc(staged, 1)

            each_pair(pool, stage)
            for k in range(NTAP):
                pool.wait_ge(mid_ready, k + 1)
                nc.gpsimd.tensor_tensor(S[:, k % 3, 2, :], rt[:, k % 2, :], S[:, k % 3, 1, :], ALU.subtract)\
                    .then_inc(low_ready, 1)

            def borders0(clip, slot):
                waits_behind(pool, x_in, 32, (h0_low, clip * 4 + 4), (conv1_done, clip - 1))
                t = A0[:, slot]
                for (r, c), (r1, c1) in (((2, 0), (2, 1)), ((3, 0), (1, 1)), ((0, T1 + 1), (2, T1)), ((1, T1 + 1), (1, T1))):
                    nc.gpsimd.tensor_copy(t[:, :, r, c:c + 1], t[:, :, r1, c1:c1 + 1].bitcast(F32))\
                        .then_inc(h0_pads, 1)

            def square(g, par, n, tile):
                at = convs_before(g) + n
                slot = (convs_par(g, par) + n) % 2
                y = Y[:, par, row_of(tile), :]
                pool.wait_ge(y_done, at + 1)
                nc.gpsimd.tensor_tensor(sqf[:, slot, :], y, y, ALU.mult).then_inc(sq_done, 1)
                pool.wait_ge(sq_done, at + 1)
                until(pool, var_done, at - 1)
                nc.gpsimd.tensor_tensor(sql[:, slot, :], sqf[:, slot, :], sqh[:, slot, :].bitcast(F32), ALU.subtract)\
                    .then_inc(sql_done, 1)

            def borders(g, n, tile):
                level, s = tile
                if level == 3:
                    return
                waits_behind(pool, x_in, 32, (al_done, splits_before(g) + n + 1))
                buf, w, c = (A1, T2, slice(s, s + 1)) if level == 1 else (A2, T3, slice(2 * s, 2 * s + 2))
                nc.gpsimd.tensor_copy(buf[:, :, 1, c, 0:1], buf[:, :, 1, c, 1:2].bitcast(F32)).then_inc(a_pads, 1)
                nc.gpsimd.tensor_copy(buf[:, :, 0, c, w + 1:w + 2], buf[:, :, 0, c, w:w + 1].bitcast(F32))\
                    .then_inc(a_pads, 1)

            borders0(0, 0)

            def step(g, par):
                tiles = tiles_of(g, conv_tiles, FULL)
                norms = tiles_of(g, norm_tiles, FULLN)
                if has(g, "conv1"):
                    for s in range(3):
                        borders0(g * 4 + (s + 1), (s + 1) % 2)
                        square(g, par, s, tiles[s])
                for n, tile in enumerate(norms[:2]):
                    borders(g, n, tile)
                if has(g, "next"):
                    borders0(g * 4 + 4, 0)
                for n, tile in enumerate(norms[2:]):
                    borders(g, n + 2, tile)
                if has(g, "conv1"):
                    square(g, par, 3, tiles[3])
                first = 4 if has(g, "conv1") else 0
                for n in range(first, len(tiles)):
                    square(g, par, n, tiles[n])

            each_iteration(pool, step)

        @block.scalar
        def _(act):
            act.dma_start(c0[:, :], a["c0"]).then_inc(c0_in, 16)
            for dst, name in ((w0[:, :, :], "w0"), (w0k[:, :], "w0k"), (selBf[:, :, :], "selB"), (cols[:, :], "cols"),
                              (ident[:, :], "ident")):
                act.dma_start(dst, a[name]).then_inc(const_in, 16)
            act.wait_ge(gram_steps, 3)
            nc.scalar.activation(Gs[:, :], bank[5][0:NTAP, 0:NTAP], ACT.Copy).then_inc(gram_act, 1)
            act.wait_ge(tg_clear, 1)

            def turned_out(i):
                for d in range(2):
                    act.wait_ge(turned, i * 2 + (d + 1))
                    until(act, quad_done, i * 2 + (d - 1))
                    nc.scalar.activation(X45[0:BW, d, :], bank[d][0:BW, :], ACT.Copy).then_inc(x45_ready, 1)

            each_pair(act, turned_out)
            act.wait_ge(inv_ready, 1)
            nc.scalar.activation(rstd0[:, :], var0[:, :], ACT.Sqrt).then_inc(rstd_ready, 1)
            for k in range(NTAP):
                act.wait_ge(scaled, k + 1)
                if k >= 3:
                    act.wait_ge(rows_out[k % 3], 96 * (k // 3))
                nc.scalar.activation(S[:, k % 3, 0, :], ps[:, k % 2, :], ACT.Copy).then_inc(high_ready, 1)
                act.wait_ge(rest_ready, k + 1)
                nc.scalar.activation(S[:, k % 3, 1, :], rt[:, k % 2, :], ACT.Copy).then_inc(mid_ready, 1)

            def relu0(clip, slot, r):
                act.wait_ge(conv0_done, clip * 4 + (r + 1))
                until(act, conv1_done, clip - 1)
                nc.scalar.activation(A0[:, slot, 0, r, 1:T1 + 1], P0[r % 2][:, :], ACT.Relu).then_inc(h0_high, 1)

            def centre(g, par, n, tile):
                level, s = tile
                at = convs_before(g) + n
                slot = (convs_par(g, par) + n) % 2
                src = C1[s % 2] if level == 1 else C2 if level == 2 else C3
                done, count = {1: (conv1_done, g * 4 + (s + 1)), 2: (conv2_done, (g - 1) * 2 + (s + 1)),
                               3: (conv3_done, g - 1)}[level]
                act.wait_ge(done, count)
                until(act, n_done, norms_before(g))
                bias = bc[:, level - 1:level]
                nc.scalar.activation(Y[:, par, row_of(tile), :], src[:, :], ACT.Identity, bias=bias)
                until(act, var_done, at - 1)
                nc.scalar.activation(sqh[:, slot, :], src[:, :], ACT.Square, bias=bias).then_inc(y_done, 1)

            def relu(g, par, n, tile):
                level, s = tile
                at = norms_before(g) + n
                slot = (norms_par(g, par) + n) % 2
                act.wait_ge(n_done, at + 1)
                src = N[:, slot, :]
                if level == 3:
                    dst = F[:, bass.ds((g - 3) * (GS * T3), GS * T3)]
                elif level == 1:
                    src = src.rearrange("p (q r) -> p r q", r=2)
                    dst = AF[:, slot, :].rearrange("p (r q) -> p r q", r=2)
                else:
                    src = src.rearrange("p (s q r) -> p r s q", r=2, s=2)
                    dst = AF[:, slot, :].rearrange("p (r s q) -> p r s q", r=2, s=2)
                if level != 3:
                    until(act, al_done, splits_before(g) + max(n - 1, 0))
                nc.scalar.activation(dst, src, ACT.Relu, scale=cols[:, CG + level - 1:CG + level],
                                     bias=cols[:, CN + level - 1:CN + level]).then_inc(relu_done, 1)

            act.wait_ge(psetup, 1)
            for r in range(4):
                relu0(0, 0, r)

            def step(g, par):
                tiles = tiles_of(g, conv_tiles, FULL)
                norms = tiles_of(g, norm_tiles, FULLN)
                conv1 = has(g, "conv1")
                if conv1:
                    for s in range(2):
                        for r in range(4):
                            relu0(g * 4 + (s + 1), (s + 1) % 2, r)
                        centre(g, par, s, tiles[s])
                if has(g, "batch"):
                    act.wait_ge(iv_done, g * 4)
                    until(act, parts_done, g * 5 - 8)
                    nc.scalar.activation(rs[:, :], iv[:, :], ACT.Sqrt).then_inc(rs_done, 1)
                if conv1:
                    for r in range(4):
                        relu0(g * 4 + 3, 1, r)
                    centre(g, par, 2, tiles[2])
                done = 0
                if conv1 and has(g, "next"):
                    for r in range(4):
                        relu0(g * 4 + 4, 0, r)
                        if done < len(norms):
                            relu(g, par, done, norms[done])
                            done += 1
                for n in range(done, len(norms)):
                    relu(g, par, n, norms[n])
                for n in range(3 if conv1 else 0, len(tiles)):
                    centre(g, par, n, tiles[n])

            each_iteration(act, step)

        @block.vector
        def _(dve):
            count = [0]

            def chain(ins):
                count[0] += 1
                ins.then_inc(wsetup, 1)
                dve.wait_ge(wsetup, count[0])

            nc.vector.memset(onesC[:, :], 1.0 / P).then_inc(ones_set, 1)
            nc.vector.memset(ones_bf[:, :], 1.0).then_inc(ones_set, 1)
            nc.vector.memset(X45[32:64, :, :], 1.0)
            nc.vector.memset(TG[:, :, :], 0.0).then_inc(tg_clear, 1)
            dve.wait_ge(c0_in, 16)
            dve.wait_ge(gram_steps, 1)
            nc.vector.tensor_tensor(c0c[:, :], c0[:, :], bank[4][:, 0:NTAP], ALU.subtract).then_inc(gram_steps, 1)
            dve.wait_ge(w_in, 16)
            chain(nc.vector.tensor_reduce(wmean[:, :], wraw[:, :, :], AX.X, ALU.add))
            chain(nc.vector.tensor_scalar(wmean[:, :], wmean[:, :], 1.0 / P, None, ALU.mult))
            mean = wmean[:, :].unsqueeze(2).broadcast_to([P, 16, P])
            chain(nc.vector.tensor_tensor(wraw[:, :, :], wraw[:, :, :], mean, ALU.subtract))
            chain(nc.vector.tensor_copy(wc[:, 0], wraw[:, :, :]))
            nc.vector.tensor_tensor(wc[:, 1], wraw[:, :, :], wc[:, 0].bitcast(F32), ALU.subtract)
            dve.wait_ge(const_in, 80)
            chain(nc.vector.tensor_reduce(w0m[:, 0:1], w0[:, 0, :], AX.X, ALU.add))
            chain(nc.vector.tensor_scalar(w0m[:, 1:2], w0m[:, 0:1], w0k[:, 0:1], 1.0 / P, ALU.mult, ALU.mult))
            chain(nc.vector.tensor_scalar(w0t[:, 0, :], w0[:, 0, :], w0m[:, 1:2], None, ALU.subtract))
            chain(nc.vector.tensor_tensor(w0t[:, 0, :], w0t[:, 0, :], w0[:, 1, :], ALU.mult))
            chain(nc.vector.tensor_copy(w0p[:, 0, :], w0t[:, 0, :]))
            chain(nc.vector.tensor_tensor(w0t[:, 1, :], w0t[:, 0, :], w0p[:, 0, :], ALU.subtract))
            chain(nc.vector.tensor_copy(w0p[:, 1, :], w0t[:, 1, :]))
            chain(nc.vector.tensor_tensor(w0p[:, 2, :], w0t[:, 1, :], w0p[:, 1, :], ALU.subtract))
            chain(nc.vector.tensor_scalar(w0t[:, 0, :], w0p[:, 0, :], w0k[:, 1:2], None, ALU.mult))
            chain(nc.vector.scalar_tensor_tensor(w0t[:, 1, :], w0p[:, 1, :], w0k[:, 2:3], w0t[:, 0, :], ALU.mult, ALU.add))
            chain(nc.vector.scalar_tensor_tensor(W0[:, :], w0p[:, 2, :], w0k[:, 3:4], w0t[:, 1, :], ALU.mult, ALU.add))
            nc.vector.tensor_copy(selB[:, :, :], selBf[:, :, :])
            chain(nc.vector.memset(selV[:, :, :].bitcast(F32), 0.0))
            for j in range(NTILE):
                nc.vector.memset(selV[:, j, j:j + 1].bitcast(F32), 1.0)
            nc.vector.memset(RS[:, :], 0.0)
            dve.wait_ge(gram_steps, 4)
            nc.vector.tensor_tensor(bc[:, :], cols[:, CB:CB + 3], bank[4][:, 16:19], ALU.subtract).then_inc(psetup, 1)

            def quadratic(i):
                for d in range(2):
                    dve.wait_ge(quad_done, i * 2 + (d + 1))
                    z = bank[2 + d][:, 0:NB8 * NTAP].rearrange("p (t k) -> p t k", k=NTAP)
                    nc.vector.tensor_tensor(prod[:, d, :].rearrange("p (t k) -> p t k", k=K0), z[:, :, 0:K0],
                                            patches(xs, i, d), ALU.mult).then_inc(prod_done, 1)
                    dve.wait_ge(prod_done, i * 2 + (d + 1))
                    nc.vector.tensor_reduce(red[:, d, :], prod[:, d, :].rearrange("p (t k) -> p t k", k=K0), AX.X,
                                            ALU.add).then_inc(red_done, 1)
                    dve.wait_ge(red_done, i * 2 + (d + 1))
                    nc.vector.tensor_tensor(var0[:, bass.ds(i * (2 * NB8) + d * NB8, NB8)], red[:, d, :],
                                            z[:, :, K0], ALU.add).then_inc(var_ready, 1)

            each_pair(dve, quadratic)
            dve.wait_ge(var_ready, NSTEP)
            chain(nc.vector.tensor_scalar(rstd0[:, :], var0[:, :], 1.0 / (P - 1), EPS, ALU.mult, ALU.add))
            nc.vector.reciprocal(var0[:, :], rstd0[:, :]).then_inc(inv_ready, 1)
            dve.wait_ge(rstd_ready, 1)
            rq = rstd0[:, :].rearrange("p (q r) -> p r q", r=4)
            for k in range(NTAP):
                o = ps[:, k % 2, :].rearrange("p (r q) -> p r q", r=4)
                if k < K0:
                    nc.vector.tensor_tensor(o, phases(k), rq, ALU.mult).then_inc(scaled, 1)
                else:
                    nc.vector.tensor_copy(o, rq).then_inc(scaled, 1)
                dve.wait_ge(high_ready, k + 1)
                if k >= 2:
                    dve.wait_ge(low_ready, k - 1)
                nc.vector.tensor_tensor(rt[:, k % 2, :], ps[:, k % 2, :], S[:, k % 3, 0, :], ALU.subtract)\
                    .then_inc(rest_ready, 1)

            def low0(clip, slot, r):
                dve.wait_ge(h0_high, clip * 4 + (r + 1))
                nc.vector.scalar_tensor_tensor(A0[:, slot, 1, r, 1:T1 + 1], P0[r % 2][:, :], 0.0,
                                               A0[:, slot, 0, r, 1:T1 + 1].bitcast(F32), ALU.max, ALU.subtract)\
                    .then_inc(h0_low, 1)

            def normalise(g, par, n, tile):
                at = norms_before(g) + n
                slot = (norms_par(g, par) + n) % 2
                dve.wait_ge(spread, at + 1)
                until(dve, relu_done, at - 1)
                nc.vector.tensor_tensor(N[:, slot, :], RB[:, :], Y[:, 1 - par, row_of(tile), :], ALU.mult)\
                    .then_inc(n_done, 1)

            def split(g, par, n, tile):
                level, s = tile
                if level == 3:
                    return
                at = norms_before(g) + n
                slot = (norms_par(g, par) + n) % 2
                dve.wait_ge(relu_done, at + 1)
                if level == 1:
                    src = AF[:, slot, :].rearrange("p (r q) -> p r q", r=2)
                    hi, lo = (A1[:, part, :, s, 1:T2 + 1] for part in range(2))
                    until(dve, conv2_done, (g - 1) * 2)
                else:
                    src = AF[:, slot, :].rearrange("p (r s q) -> p r s q", r=2, s=2)
                    hi, lo = (A2[:, part, :, 2 * s:2 * s + 2, 1:T3 + 1] for part in range(2))
                    until(dve, conv3_done, g - 2)
                nc.vector.tensor_copy(hi, src).then_inc(ah_done, 1)
                dve.wait_ge(ah_done, splits_before(g) + n + 1)
                nc.vector.tensor_tensor(lo, src, hi.bitcast(F32), ALU.subtract).then_inc(al_done, 1)

            for r in range(4):
                low0(0, 0, r)

            def step(g, par):
                norms = tiles_of(g, norm_tiles, FULLN)
                conv1 = has(g, "conv1")
                batch = has(g, "batch")
                if conv1:
                    for r in range(4):
                        low0(g * 4 + 1, 1, r)
                if batch:
                    dve.wait_ge(var_done, convs_before(g))
                    nc.vector.tensor_scalar(vs[:, :], V[0:NTILE + 1, :], 1.0 / (P - 1), EPS, ALU.mult, ALU.add)\
                        .then_inc(vs_done, 1)
                for r in range(4):
                    if conv1:
                        low0(g * 4 + 2, 0, r)
                    if batch:
                        if r == 0:
                            dve.wait_ge(vs_done, g)
                        c = slice(r * P, (r + 1) * P)
                        nc.vector.reciprocal(iv[:, c], vs[:, c]).then_inc(iv_done, 1)
                if conv1:
                    low0(g * 4 + 3, 1, 0)
                if batch:
                    dve.wait_ge(rs_done, g)
                    until(dve, spread, norms_before(g))
                    nc.vector.tensor_copy(RS[0:NTILE + 1, :], rs[:, :]).then_inc(parts_done, 1)
                    dve.wait_ge(parts_done, g * 5 - 4)
                    nc.vector.tensor_tensor(rr[:, :], rs[:, :], RS[0:NTILE + 1, :], ALU.subtract).then_inc(parts_done, 1)
                if conv1:
                    low0(g * 4 + 3, 1, 1)
                if batch:
                    dve.wait_ge(parts_done, g * 5 - 3)
                    nc.vector.tensor_copy(mt[:, :], rr[:, :]).then_inc(parts_done, 1)
                    dve.wait_ge(parts_done, g * 5 - 2)
                    nc.vector.tensor_tensor(RS[64:64 + NTILE + 1, :], rr[:, :], mt[:, :], ALU.subtract)\
                        .then_inc(parts_done, 1)
                    nc.vector.tensor_copy(RS[32:32 + NTILE + 1, :], mt[:, :]).then_inc(parts_done, 1)
                if conv1:
                    low0(g * 4 + 3, 1, 2)
                    low0(g * 4 + 3, 1, 3)
                last = len(norms)
                for n in range(last + 1):
                    if n < last:
                        normalise(g, par, n, norms[n])
                    if 1 <= n <= 4 and conv1 and has(g, "next"):
                        low0(g * 4 + 4, 0, n - 1)
                    if n >= 1:
                        split(g, par, n - 1, norms[n - 1])
                for n in range(last + 1, 5):
                    if conv1 and has(g, "next"):
                        low0(g * 4 + 4, 0, n - 1)

            each_iteration(dve, step)

        @block.tensor
        def _(pe):
            pe.wait_ge(c0_in, 16)
            pe.wait_ge(ones_set, 1)
            nc.tensor.matmul(bank[4][:, 0:NTAP], onesC[:, :], c0[:, :], start=True, stop=True).then_inc(gram_steps, 1)
            pe.wait_ge(gram_steps, 2)
            nc.tensor.matmul(bank[5][0:NTAP, 0:NTAP], c0c[:, :], c0c[:, :], start=True, stop=True).then_inc(gram_steps, 1)
            pe.wait_ge(const_in, 80)
            nc.tensor.matmul(bank[4][:, 16:19], onesC[:, :], cols[:, CB:CB + 3], start=True, stop=True)\
                .then_inc(gram_steps, 1)
            pe.wait_ge(tg_in, 16 * 2 * BLK)

            def turn(i, d):
                waits_behind(pe, const_in, 80, (staged, i * 2 + (d + 1)), (x45_ready, i * 2 + (d - 1)))
                for t in range(4):
                    mm = nc.tensor.transpose(bank[d][0:BW, t * P:(t + 1) * P],
                                             xst[:, d, t * BLK * STR0:t * BLK * STR0 + BW], ident[:, :])
                mm.then_inc(turned, 1)

            def quad(i, d):
                pe.wait_ge(x45_ready, i * 2 + (d + 1))
                until(pe, var_ready, i * 2 + (d - 1))
                for t in range(4):
                    c = slice(t * BLK * NTAP, (t + 1) * BLK * NTAP)
                    mm = nc.tensor.matmul(bank[2 + d][:, c], X45[0:BW + 1, d, t * P:(t + 1) * P],
                                          TG[:, :, :].rearrange("j t k -> j (t k)"), start=True, stop=True)
                mm.then_inc(quad_done, 1)

            def turn_and_quad(i):
                for d in range(2):
                    turn(i, d)
                    quad(i, d)

            each_pair(pe, turn_and_quad)

            def conv0(clip, r, slot):
                at = clip * 4 + r
                if r == 0:
                    pe.wait_ge(r_in[slot], clip * 12 + (48 - 12 * slot))
                until(pe, h0_low, at - 1)
                nc.tensor.matmul(P0[r % 2][:, :], W0[:, :], R[:, slot, r * T1:(r + 1) * T1], start=True, stop=True)\
                    .then_inc(conv0_done, 1)

            def conv1(g, s, fill):
                clip = g * 4 + s
                pe.wait_ge(h0_pads, clip * 4 + 4)
                if s >= 2:
                    until(pe, y_done, convs_before(g) + s - 1)
                elif not isinstance(g, int) or g >= 1:
                    until(pe, y_done, convs_before(g - 1) + s + 3)
                n = 0
                for tap in range(8):
                    m, phase = divmod(tap, 4)
                    r = (phase + 2) % 4
                    o = m + (1 if r < 2 else 0)
                    for w, x in PASSES:
                        mm = nc.tensor.matmul(C1[s % 2][:, :], wc[:, w, tap, :], A0[:, s % 2, x, r, o:o + T1],
                                              start=(n == 0), stop=(n == 23))
                        n += 1
                        if n == 24:
                            mm.then_inc(conv1_done, 1)
                        elif n in fill:
                            fill[n]()

            def conv_small(g, level, s):
                n = 0
                first, buf, w, dst = (8, A1, T2, C2) if level == 2 else (12, A2, T3, C3)
                cl = slice(2 * s, 2 * s + 2) if level == 2 else slice(0, 4)
                for tap in range(4):
                    m, phase = divmod(tap, 2)
                    psi = 1 - phase
                    o = m + (1 - psi)
                    for wp, x in PASSES:
                        mm = nc.tensor.matmul(dst[:, :], wc[:, wp, first + tap, :], buf[:, x, psi, cl, o:o + w],
                                              start=(n == 0), stop=(n == 11))
                        n += 1
                mm.then_inc(conv2_done if level == 2 else conv3_done, 1)

            def conv2(g, s):
                norms = tiles_of(g, norm_tiles, FULLN)
                pe.wait_ge(a_pads, 2 * (splits_before(g) + norms.index((1, 2 * s + 1)) + 1))
                if s == 1:
                    pe.wait_ge(y_done, convs_before(g) + tiles_of(g, conv_tiles, FULL).index((2, 0)) + 1)
                elif not isinstance(g, int) or g >= 2:
                    pe.wait_ge(y_done, convs_before(g))
                conv_small(g, 2, s)

            def conv3(g):
                norms = tiles_of(g, norm_tiles, FULLN)
                pe.wait_ge(a_pads, 2 * (splits_before(g) + norms.index((2, 1)) + 1))
                if not isinstance(g, int) or g >= 3:
                    pe.wait_ge(y_done, convs_before(g))
                conv_small(g, 3, 0)

            def variance(g, par, tile):
                tiles = tiles_of(g, conv_tiles, FULL)
                n = tiles.index(tile)
                at = convs_before(g) + n
                slot = (convs_par(g, par) + n) % 2
                pe.wait_ge(sql_done, at + 1)
                if n == 0:
                    until(pe, vs_done, g)
                nc.tensor.matmul(V[:, :], selV[:, row_of(tile), :], sqh[:, slot, :], start=(n == 0), stop=False)
                nc.tensor.matmul(V[:, :], selV[:, row_of(tile), :], sql[:, slot, :], start=False,
                                 stop=(n == len(tiles) - 1)).then_inc(var_done, 1)

            def bcast(g, n, tile):
                if n == 0:
                    pe.wait_ge(parts_done, g * 5)
                until(pe, n_done, norms_before(g) + n)
                nc.tensor.matmul(RB[:, :], selB[:, row_of(tile), :], RS[:, :], start=True, stop=True).then_inc(spread, 1)

            pe.wait_ge(psetup, 1)
            for r in range(4):
                conv0(0, r, 0)

            def step(g, par):
                tiles = tiles_of(g, conv_tiles, FULL)
                norms = tiles_of(g, norm_tiles, FULLN)
                conv1_on = has(g, "conv1")
                pending = list(enumerate(norms))

                def spread_next():
                    n, tile = pending.pop(0)
                    bcast(g, n, tile)

                def fills(s):
                    f = {}
                    if s < 3 or has(g, "next"):
                        for r in range(4):
                            f[3 + 5 * r] = lambda r=r: conv0(g * 4 + (s + 1), r, (s + 1) % 4)
                    if s == 2:
                        f.update({n: spread_next for n in (15, 20)[:len(pending)]})
                    if s == 3:
                        f.update({n: spread_next for n in (1, 5, 10, 15, 20)[:len(pending)]})
                    return f

                if conv1_on:
                    conv1(g, 0, fills(0))
                for tile in late(g - 1):
                    variance(g - 1, 1 - par, tile)
                if conv1_on:
                    conv1(g, 1, fills(1))
                    variance(g, par, (1, 0))
                    conv1(g, 2, fills(2))
                    variance(g, par, (1, 1))
                    conv1(g, 3, fills(3))
                while pending:
                    spread_next()
                if has(g, "conv3"):
                    conv3(g)
                if conv1_on:
                    variance(g, par, (1, 2))
                if has(g, "conv2"):
                    conv2(g, 0)
                if conv1_on:
                    variance(g, par, (1, 3))
                if has(g, "conv2"):
                    conv2(g, 1)
                if has(g, "conv3"):
                    variance(g, par, (3, 0))

            each_iteration(pe, step)


MLP_ORDER = ((2, 0), (1, 0), (1, 1), (2, 1), (1, 2), (1, 3), (2, 2), (2, 3))
PASSES = ((0, 0), (0, 1), (1, 0))


def mlp_order(i):
    return [t for t in MLP_ORDER if t[0] == 2 or not isinstance(i, int) or i + 1 < NG]


def mlp_before(i):
    return i * 8 + KC


def mlp_steps(eng, step):
    step(0, 0)
    step(1, 1)
    with eng.Fori(1, NG // 2 - 1) as i:
        for d in range(2):
            step(i * 2 + d, d)
    step(NG - 2, 0)
    step(NG - 1, 1)


def importance_mlp(nc, a, outer, bank, F, cols, LG):
    with ExitStack() as ctx:
        def sb(name, shape, dt=F32):
            return ctx.enter_context(nc.sbuf_tensor(name, shape, dt))

        def sem(name):
            return outer.enter_context(nc.semaphore(name))

        raw1 = sb("raw1", [P, DM])
        raw2 = sb("raw2", [P, KC, DM])
        W1 = sb("W1", [P, 2, DM], F32R)
        W2 = sb("W2", [P, 2, KC, DM], F32R)
        W3 = sb("W3", [P, KC, P], F32R)
        Fp = sb("Fp", [P, 2, 2, DM], F32R)
        Z = sb("Z", [P, KC, DM])
        Z1 = sb("Z1", [P, 2, 2, KC, DM], F32R)
        Z2 = sb("Z2", [P, 2, KC, DM], F32R)
        Lrow = sb("Lrow", [2, B * T3])
        mlp_in = sem("mlp_in")
        mlp_setup = sem("mlp_setup")
        f_high = sem("f_high")
        f_low = sem("f_low")
        z_sums = sem("z_sums")
        z_gelu = sem("z_gelu")
        z_high = sem("z_high")
        z_low = sem("z_low")
        logit_sums = sem("logit_sums")
        logit_rows = sem("logit_rows")
        logits_in = sem("logits_in")

        block = ctx.enter_context(nc.Block())

        @block.sync
        def _(sp):
            sp.dma_start(raw1[:, :], a["mlp1"]).then_inc(mlp_in, 16)
            sp.dma_start(raw2[:, :, :], a["mlp2"]).then_inc(mlp_in, 16)
            sp.wait_ge(logit_rows, NG)
            for r in range(2):
                sp.dma_start(LG[:, r, :], Lrow[r:r + 1, :].rearrange("p (b t) -> p b t", b=B)).then_inc(logits_in, 16)
            sp.wait_ge(logits_in, 32)

        @block.scalar
        def _(act):
            def gelu(n, at, layer, m):
                act.wait_ge(z_sums, n + 1)
                until(act, z_low, n - 3)
                b = CM1 + m if layer == 1 else CM2 + m
                nc.scalar.activation(Z[:, at, :], bank[at][:, :], ACT.Gelu, bias=cols[:, b:b + 1]).then_inc(z_gelu, 1)

            def logits(i, par):
                act.wait_ge(logit_sums, i * KC + KC)
                nc.scalar.activation(Lrow[:, bass.ds(i * DM, DM)], bank[4 + par][0:2, :], ACT.Copy).then_inc(logit_rows, 1)

            for m in range(KC):
                gelu(m, m, 1, m)

            def step(i, par):
                for j, (layer, m) in enumerate(mlp_order(i)):
                    gelu(mlp_before(i) + j, j % KC, layer, m)
                    if j == 1 and not (isinstance(i, int) and i == 0):
                        logits(i - 1, 1 - par)

            mlp_steps(act, step)
            logits(NG - 1, (NG - 1) % 2)

        @block.vector
        def _(dve):
            dve.wait_ge(mlp_in, 32)
            nc.vector.tensor_copy(W1[:, 0], raw1[:, :]).then_inc(mlp_setup, 1)
            nc.vector.tensor_copy(W2[:, 0], raw2[:, :, :]).then_inc(mlp_setup, 1)
            nc.vector.memset(W3[:, :, :].bitcast(F32), 0.0).then_inc(mlp_setup, 1)
            dve.wait_ge(mlp_setup, 3)
            nc.vector.tensor_tensor(W1[:, 1], raw1[:, :], W1[:, 0].bitcast(F32), ALU.subtract)
            nc.vector.tensor_tensor(W2[:, 1], raw2[:, :, :], W2[:, 0].bitcast(F32), ALU.subtract)
            w3 = cols[:, CW3:CW3 + KC]
            nc.vector.tensor_copy(W3[:, :, 0], w3).then_inc(mlp_setup, 1)
            dve.wait_ge(mlp_setup, 4)
            nc.vector.tensor_tensor(W3[:, :, 1], w3, W3[:, :, 0].bitcast(F32), ALU.subtract).then_inc(mlp_setup, 1)

            def split_f(i, par):
                nc.vector.tensor_copy(Fp[:, par, 0, :], F[:, bass.ds(i * DM, DM)]).then_inc(f_high, 1)
                dve.wait_ge(f_high, i + 1)
                nc.vector.tensor_tensor(Fp[:, par, 1, :], F[:, bass.ds(i * DM, DM)], Fp[:, par, 0, :].bitcast(F32),
                                        ALU.subtract).then_inc(f_low, 1)

            def split_z(n, at, hi, lo):
                dve.wait_ge(z_gelu, n + 1)
                nc.vector.tensor_copy(hi, Z[:, at, :]).then_inc(z_high, 1)
                dve.wait_ge(z_high, n + 1)
                nc.vector.tensor_tensor(lo, Z[:, at, :], hi.bitcast(F32), ALU.subtract).then_inc(z_low, 1)

            split_f(0, 0)
            split_f(1, 1)
            for m in range(KC):
                split_z(m, m, Z1[:, 0, 0, m, :], Z1[:, 0, 1, m, :])

            def step(i, par):
                for j, (layer, m) in enumerate(mlp_order(i)):
                    n = mlp_before(i) + j
                    if layer == 1:
                        split_z(n, j % KC, Z1[:, 1 - par, 0, m, :], Z1[:, 1 - par, 1, m, :])
                    else:
                        until(dve, logit_sums, i * KC + (m - 3))
                        split_z(n, j % KC, Z2[:, 0, m, :], Z2[:, 1, m, :])
                if not isinstance(i, int) or i + 2 < NG:
                    split_f(i + 2, par)

            mlp_steps(dve, step)

        @block.tensor
        def _(pe):
            def chunk(n, at, layer, m, par):
                until(pe, z_gelu, n - 3)
                k = 0
                depth = 1 if layer == 1 else KC
                for kc in range(depth):
                    for w, x in PASSES:
                        if layer == 1:
                            lhs, rhs = W1[:, w, m * P:(m + 1) * P], Fp[:, par, x, :]
                        else:
                            lhs, rhs = W2[:, w, kc, m * P:(m + 1) * P], Z1[:, par, x, kc, :]
                        mm = nc.tensor.matmul(bank[at][:, :], lhs, rhs, start=(k == 0), stop=(k == 3 * depth - 1))
                        k += 1
                mm.then_inc(z_sums, 1)

            def logits(i, par, m):
                pe.wait_ge(z_low, mlp_before(i) + mlp_order(i).index((2, m)) + 1)
                if m == 0:
                    until(pe, logit_rows, i - 1)
                for x in range(2):
                    mm = nc.tensor.matmul(bank[4 + par][:, :], W3[:, m, :], Z2[:, x, m, :], start=(m == 0 and x == 0),
                                          stop=(m == KC - 1 and x == 1))
                mm.then_inc(logit_sums, 1)

            pe.wait_ge(mlp_setup, 5)
            pe.wait_ge(f_low, 1)
            for m in range(KC):
                chunk(m, m, 1, m, 0)

            def step(i, par):
                order = mlp_order(i)
                for j, (layer, m) in enumerate(order):
                    n = mlp_before(i) + j
                    if j == 0:
                        pe.wait_ge(z_low, KC if isinstance(i, int) and i == 0 else i * 8 + 2)
                    if (layer, m) == (1, 0):
                        pe.wait_ge(f_low, i + 2)
                    chunk(n, j % KC, layer, m, par if layer == 2 else 1 - par)
                    if j == 0 and not (isinstance(i, int) and i == 0):
                        logits(i - 1, 1 - par, 3)
                    elif layer == 2 and m > 0:
                        logits(i, par, m - 1)

            mlp_steps(pe, step)
            logits(NG - 1, (NG - 1) % 2, 3)


def pool_attend_experts(nc, a, outer, bank, F, cols, ident, LG, out):
    with ExitStack() as ctx:
        def sb(name, shape, dt=F32):
            return ctx.enter_context(nc.sbuf_tensor(name, shape, dt))

        def sem(name):
            return outer.enter_context(nc.semaphore(name))

        NB = 8 // W
        H = T3
        route = sb("route", [1, B], I32)
        b3 = sb("b3", [B, 1])
        iota = sb("iota", [P, D + 1])
        wattn = sb("wattn", [P, 3, P])
        bv = sb("bv", [P, P])
        bo = sb("bo", [P, D])
        wi = sb("wi", [P, P])
        wo = sb("wo", [P, D])
        wx = sb("wx", [P, 2, NE, EW])
        wsh = sb("wsh", [P, 2, EW])
        imp = sb("imp", [B, T3])
        impn = sb("impn", [B, T3])
        isum = sb("isum", [B, 2])
        ones = sb("ones", [B, T3])
        cs = sb("cs", [B, T3 + 1])
        csT = sb("csT", [P, B, 2])
        Fs = sb("Fs", [P, W, GS, T3])
        zero = sb("zero", [P, 2 * GS])
        E1 = sb("E1", [P, 2 * GS, D + 1])
        E2 = sb("E2", [P, 2 * GS, D + 1])
        E3 = sb("E3", [P, GS, 2, D])
        WM = sb("WM", [P, W, GS, D])
        FT = sb("FT", [P, W, GS, P])
        st = sb("st", [P, W, 3, GS, 6])
        mv = sb("mv", [P, W, 3, GS, 2])
        sd = sb("sd", [P, W, 3, 3, GS])
        Xn = sb("Xn", [P, W, 2, P])
        H0 = sb("H0", [P, W, GS, D])
        Xc = sb("Xc", [P, W, 2, GS, D])
        Xa = sb("Xa", [P, W, 2, GS, D])
        XT = sb("XT", [P, W, 2, 2, P])
        QK = sb("QK", [P, W, 2, 2, P])
        Vt = sb("Vt", [P, W, 2, P])
        mx = sb("mx", [P, W, 2, GS])
        PR = sb("PR", [P, W, GS, P])
        psum_ = sb("prob_sums", [P, W, 2, GS])
        PT = sb("PT", [P, W, GS, P])
        H1 = sb("H1", [P, W, GS, D])
        H1b = sb("H1b", [P, W, GS, D])
        GW = sb("GW", [P, W, GS, 2, EW])
        HF = sb("HF", [P, W, 3, GS, P])
        O = sb("O", [P, W, GS, D])

        tail_in = sem("tail_in")
        experts_sum = sem("experts_sum")
        imp_steps = sem("imp_steps")
        cs_turned = sem("cs_turned")
        csT_ready = sem("csT_ready")
        f_staged = sem("f_staged")
        wm_steps = sem("wm_steps")
        wm_ready = sem("wm_ready")
        f_turned = sem("f_turned")
        ft_ready = sem("ft_ready")
        pooled = sem("pooled")
        stats = [sem(f"stats{i}") for i in range(3)]
        moments = [sem(f"moments{i}") for i in range(3)]
        var_eps = [sem(f"var_eps{i}") for i in range(3)]
        root = [sem(f"root{i}") for i in range(3)]
        invroot = [sem(f"invroot{i}") for i in range(3)]
        centred = [sem(f"centred{i}") for i in range(2)]
        normed = [sem(f"normed{i}") for i in range(3)]
        norm_turned = [sem(f"norm_turned{i}") for i in range(3)]
        h0_ready = sem("h0_ready")
        xt_ready = [sem(f"xt_ready{i}") for i in range(2)]
        qkv_done = sem("qkv_done")
        qk_ready = sem("qk_ready")
        v_ready = sem("v_ready")
        scores_done = sem("scores_done")
        max_done = sem("max_done")
        shift_ready = sem("shift_ready")
        probs_ready = sem("probs_ready")
        inv_sum = sem("inv_sum")
        probs_turned = sem("probs_turned")
        pt_ready = sem("pt_ready")
        attended = sem("attended")
        h1_ready = sem("h1_ready")
        h1b_ready = sem("h1b_ready")
        hidden_done = [sem(f"hidden_done{i}") for i in range(3)]
        hidden_ready = [sem(f"hidden_ready{i}") for i in range(3)]
        experts_in = [sem(f"experts_in{h}") for h in range(W)]
        out_done = sem("out_done")
        o_ready = sem("o_ready")
        stored = sem("stored")

        def groups(eng, steps):
            with eng.Fori(0, NG // W) as k:
                for step in steps:
                    for h in range(W):
                        step(k * W + h, h)

        def bk(h, i):
            return bank[h * NB + i]

        block = ctx.enter_context(nc.Block())

        @block.sync
        def _(sp):
            for dst, name in ((b3[:, :], "b3"), (iota[:, :], "iota"), (wattn[:, :, :], "attn"), (bv[:, :], "bv"),
                              (bo[:, :], "bo"), (wi[:, :], "wi"), (wo[:, :], "wo"), (wx[:, :, :, :], "wr"),
                              (wsh[:, :, :], "ws"), (route[:, :], "route")):
                sp.dma_start(dst, a[name]).then_inc(tail_in, 16)
            sp.wait_ge(experts_sum, 3)

            def fetch(k, h):
                sp.wait_ge(hidden_ready[2], k * W + (h + 1))
                for c in range(GS):
                    e = sp.value_load(route[0:1, bass.ds(k * (W * GS) + (h * GS + c), 1)], min_val=0, max_val=NE - 1)
                    for l in range(2):
                        sp.dma_start(GW[:, h, c, l, :], wx[:, l, bass.ds(e, 1), :].rearrange("p o w -> p (o w)"))\
                            .then_inc(experts_in[h], 16)

            with sp.Fori(0, NG // W) as k:
                for h in range(W):
                    fetch(k, h)
                for h in range(W):
                    sp.wait_ge(o_ready, k * W + (h + 1 + W))
                    dst = out[bass.ds(k * (W * GS) + h * GS, GS)].rearrange("b c d -> c b d")
                    sp.dma_start(dst, O[:, h]).then_inc(stored, 16)
            sp.wait_ge(stored, (NG + W) * 16)

        @block.gpsimd
        def _(pool):
            nc.gpsimd.memset(ones[:, :], 1.0).then_inc(imp_steps, 1)
            nc.gpsimd.memset(cs[:, 0:1], 0.0).then_inc(imp_steps, 1)
            nc.gpsimd.memset(E3[:, :, :, :], 0.0).then_inc(o_ready, W)
            nc.gpsimd.memset(O[:, :, 0, 0:1], 0.0).then_inc(stored, 16 * W)
            nc.gpsimd.memset(Fs[:, :, 0, 0:1], 0.0).then_inc(f_turned, W)
            nc.gpsimd.memset(WM[:, :, 0, 0:1], 0.0).then_inc(pooled, W)
            nc.gpsimd.memset(HF[:, :, 0, 0, 0:1], 0.0).then_inc(hidden_ready[2], W)
            nc.gpsimd.memset(zero[:, :], 0.0).then_inc(wm_steps, 1)
            pool.wait_ge(csT_ready, 2)
            pool.wait_ge(wm_steps, 1)

            def stage(q, h):
                pool.wait_ge(f_turned, q + 1)
                src = F[:, bass.ds(q * DM, DM)].rearrange("p (b t) -> p b t", b=GS)
                nc.gpsimd.tensor_tensor(Fs[:, h], src, zero[:, 0:GS].unsqueeze(2).broadcast_to([P, GS, T3]), ALU.add)\
                    .then_inc(f_staged, 1)

            def weights(q, h):
                c = csT[:, bass.ds(q * GS, GS), :].rearrange("p b s -> p (b s)")
                shape = [P, 2 * GS, D + 1]
                nc.gpsimd.tensor_tensor(E1[:, :, :], c.unsqueeze(2).broadcast_to(shape),
                                        iota[:, :].unsqueeze(1).broadcast_to(shape), ALU.subtract).then_inc(wm_steps, 1)
                waits_behind(pool, csT_ready, 2, (wm_steps, q * 3 + 2))
                nc.gpsimd.tensor_scalar(E2[:, :, :], E1[:, :, :], 0.0, None, ALU.max).then_inc(wm_steps, 1)
                pool.wait_ge(wm_steps, q * 3 + 3)
                nc.gpsimd.tensor_tensor(E3[:, :, :, :].rearrange("p b s n -> p (b s) n"), E2[:, :, 0:D], E2[:, :, 1:D + 1],
                                        ALU.subtract).then_inc(wm_steps, 1)
                pool.wait_ge(wm_steps, q * 3 + 4)
                pool.wait_ge(pooled, q + 1)
                nc.gpsimd.tensor_tensor(WM[:, h], E3[:, :, 0, :], E3[:, :, 1, :], ALU.subtract).then_inc(wm_ready, 1)

            groups(pool, [stage, weights])

        @block.scalar
        def _(act):
            act.wait_ge(imp_steps, 3)
            act.wait_ge(tail_in, 160)
            nc.scalar.activation(imp[:, :], impn[:, :], ACT.Sigmoid, bias=b3[:, :]).then_inc(imp_steps, 1)
            act.wait_ge(cs_turned, 2)
            for s in range(2):
                nc.scalar.activation(csT[:, :, s], bank[s][:, 0:B], ACT.Copy).then_inc(csT_ready, 1)

            def features(q, h):
                act.wait_ge(o_ready, q + 1)
                act.wait_ge(f_turned, q + (1 + W))
                nc.scalar.activation(FT[:, h], bk(h, 0)[:, :].rearrange("p (b c) -> p b c", b=GS), ACT.Copy)\
                    .then_inc(ft_ready, 1)

            def root_of(norm, n):
                def f(q, h):
                    act.wait_ge(var_eps[norm], q + 1)
                    nc.scalar.activation(sd[:, h, norm, 1, 0:n], sd[:, h, norm, 0, 0:n], ACT.Sqrt).then_inc(root[norm], 1)
                return f

            def first(q, h):
                act.wait_ge(norm_turned[0], q + 1)
                nc.scalar.activation(H0[:, h].rearrange("p b n -> p (b n)"), bk(h, 2)[:, 0:GS * D], ACT.Relu,
                                     scale=cols[:, CG4:CG4 + 1], bias=cols[:, CN4:CN4 + 1]).then_inc(h0_ready, 1)

            def turned(i):
                def f(q, h):
                    act.wait_ge(norm_turned[1 + i], q + 1)
                    nc.scalar.activation(XT[:, h, i].rearrange("p a c -> p (a c)"), bk(h, 0)[:, 0:2 * P], ACT.Copy)\
                        .then_inc(xt_ready[i], 1)
                return f

            def queries_keys(q, h):
                act.wait_ge(qkv_done, q + 1)
                for i, b in ((0, CBQ), (1, CBK)):
                    nc.scalar.activation(QK[:, h, i].rearrange("p a c -> p (a c)"), bk(h, 1)[:, i * 2 * P:(i + 1) * 2 * P],
                                         ACT.Identity, bias=cols[:, b:b + 1]).then_inc(qk_ready, 1)

            def probs(q, h):
                act.wait_ge(shift_ready, q + 1)
                for c in range(GS):
                    pair, one = divmod(c, 2)
                    nc.scalar.activation(PR[:, h, c, :], bk(h, 3 - 2 * one)[:, pair * P:(pair + 1) * P], ACT.Exp, scale=D ** -0.5,
                                         bias=mx[:, h, 1, c:c + 1], accum_out=psum_[:, h, 0, c:c + 1])\
                        .then_inc(probs_ready, 1)

            def probs_t(q, h):
                act.wait_ge(probs_turned, q + 1)
                nc.scalar.activation(PT[:, h], bk(h, 0)[:, :].rearrange("p (b c) -> p b c", b=GS), ACT.Copy)\
                    .then_inc(pt_ready, 1)

            def hidden0(q, h):
                act.wait_ge(hidden_done[0], q + 1)
                for one in range(2):
                    ins = nc.scalar.activation(HF[:, h, 0, 2 * one:2 * one + 2].rearrange("p b c -> p (b c)"),
                                               bk(h, 3 - 2 * one)[:, 0:2 * P], ACT.Relu, bias=cols[:, CBI:CBI + 1])
                ins.then_inc(hidden_ready[0], 1)

            def hidden(l):
                def f(q, h):
                    act.wait_ge(hidden_done[1 + l], q + 1)
                    for c in range(GS):
                        clip = (c % 2) * 2 + c // 2
                        ins = nc.scalar.activation(HF[:, h, 1 + l, c, :], bk(h, 3 - 2 * l)[:, c * P:(c + 1) * P], ACT.Relu,
                                                   bias=GW[:, h, clip, l, P:EW])
                    ins.then_inc(hidden_ready[1 + l], 1)
                return f

            groups(act, [features, root_of(0, 2), first, root_of(1, GS), turned(0), queries_keys, probs, probs_t,
                         root_of(2, GS), turned(1), hidden0, hidden(0), hidden(1)])

        @block.vector
        def _(dve):
            nc.vector.tensor_tensor(impn[:, :], LG[:, 0, :], LG[:, 1, :], ALU.add).then_inc(imp_steps, 1)
            dve.wait_ge(imp_steps, 4)
            nc.vector.tensor_scalar(impn[:, :], imp[:, :], TEMP, None, ALU.add).then_inc(imp_steps, 1)
            dve.wait_ge(imp_steps, 5)
            nc.vector.tensor_reduce(isum[:, 0:1], impn[:, :], AX.X, ALU.add).then_inc(imp_steps, 1)
            dve.wait_ge(imp_steps, 6)
            nc.vector.reciprocal(isum[:, 1:2], isum[:, 0:1]).then_inc(imp_steps, 1)
            dve.wait_ge(imp_steps, 7)
            nc.vector.tensor_scalar(imp[:, :], impn[:, :], isum[:, 1:2], float(D), ALU.mult, ALU.mult).then_inc(imp_steps, 1)
            dve.wait_ge(imp_steps, 8)
            nc.vector.tensor_tensor_scan(cs[:, 1:T3 + 1], ones[:, :], imp[:, :], 0.0, ALU.mult, ALU.add)\
                .then_inc(imp_steps, 1)
            dve.wait_ge(tail_in, 160)
            for l in range(2):
                nc.vector.tensor_tensor(wx[:, l], wx[:, l], wsh[:, l, :].unsqueeze(1).broadcast_to([P, NE, EW]), ALU.add)\
                    .then_inc(experts_sum, 1)
            dve.wait_ge(experts_sum, 2)
            mats = wx[:, :, :, 0:P].rearrange("p l e h -> p (l e) h")
            nc.vector.tensor_tensor(mats, mats, ident[:, :].unsqueeze(1).broadcast_to([P, 2 * NE, P]), ALU.add)\
                .then_inc(experts_sum, 1)

            def moments_of(norm, n, src, ready, unbias):
                def stat(q, h):
                    dve.wait_ge(ready, q + (1 + W if norm == 0 else 1))
                    for j in range(n):
                        nc.vector.bn_stats(st[:, h, norm, j, :], src(h, j)).then_inc(stats[norm], 1)

                def aggr(q, h):
                    waits_behind(dve, tail_in, 160, (stats[norm], q * n + n))
                    for j in range(n):
                        nc.vector.bn_aggr(mv[:, h, norm, j, :], st[:, h, norm, j, :]).then_inc(moments[norm], 1)

                def eps(q, h):
                    dve.wait_ge(moments[norm], q * n + n)
                    nc.vector.tensor_scalar(sd[:, h, norm, 0, 0:n], mv[:, h, norm, 0:n, 1], unbias, EPS, ALU.mult, ALU.add)\
                        .then_inc(var_eps[norm], 1)

                def inv(q, h):
                    dve.wait_ge(root[norm], q + 1)
                    nc.vector.reciprocal(sd[:, h, norm, 2, 0:n], sd[:, h, norm, 1, 0:n]).then_inc(invroot[norm], 1)

                return [stat, aggr, eps, inv]

            def norm_pooled(q, h):
                dve.wait_ge(invroot[0], q + 1)
                for j in range(2):
                    nc.vector.tensor_scalar(Xn[:, h, j, :], bk(h, 1)[:, j * P:(j + 1) * P], mv[:, h, 0, j, 0:1],
                                            sd[:, h, 0, 2, j:j + 1], ALU.subtract, ALU.mult).then_inc(normed[0], 1)

            def layer_norm(i, src):
                def centre(q, h):
                    nc.vector.tensor_tensor(Xc[:, h, i], src(h), mv[:, h, 1 + i, :, 0:1].broadcast_to([P, GS, D]),
                                            ALU.subtract).then_inc(centred[i], 1)

                def scale(q, h):
                    dve.wait_ge(invroot[1 + i], q + 1)
                    dve.wait_ge(centred[i], q + 1)
                    nc.vector.tensor_tensor(Xa[:, h, i], Xc[:, h, i],
                                            sd[:, h, 1 + i, 2, :].unsqueeze(2).broadcast_to([P, GS, D]), ALU.mult)\
                        .then_inc(normed[1 + i], 1)
                return centre, scale

            def values(q, h):
                dve.wait_ge(qkv_done, q + 1)
                nc.vector.tensor_tensor(Vt[:, h], bk(h, 2)[:, 0:2 * P].rearrange("p (a c) -> p a c", a=2),
                                        bv[:, :].unsqueeze(1).broadcast_to([P, 2, P]), ALU.add).then_inc(v_ready, 1)

            def maxima(q, h):
                dve.wait_ge(scores_done, q + 1)
                for one in range(2):
                    ins = nc.vector.tensor_reduce(mx[:, h, 0, one:GS:2],
                                                  bk(h, 3 - 2 * one)[:, 0:2 * P].rearrange("p (b c) -> p b c", b=2), AX.X, ALU.max)
                ins.then_inc(max_done, 1)

            def shift(q, h):
                dve.wait_ge(max_done, q + 1)
                nc.vector.tensor_scalar(mx[:, h, 1, :], mx[:, h, 0, :], -D ** -0.5, None, ALU.mult).then_inc(shift_ready, 1)

            def inv_sums(q, h):
                dve.wait_ge(probs_ready, q * GS + GS)
                nc.vector.reciprocal(psum_[:, h, 1, :], psum_[:, h, 0, :]).then_inc(inv_sum, 1)

            def residual(q, h):
                dve.wait_ge(attended, q + 1)
                dve.wait_ge(inv_sum, q + 1)
                for c in range(GS):
                    ins = nc.vector.scalar_tensor_tensor(H1[:, h, c, :], bk(h, 2)[:, c * D:(c + 1) * D],
                                                         psum_[:, h, 1, c:c + 1], H0[:, h, c, :], ALU.mult, ALU.add)
                ins.then_inc(h1_ready, 1)

            def with_bias(q, h):
                dve.wait_ge(h1_ready, q + 1)
                nc.vector.tensor_tensor(H1b[:, h], H1[:, h], bo[:, :].unsqueeze(1).broadcast_to([P, GS, D]), ALU.add)\
                    .then_inc(h1b_ready, 1)

            def outputs(q, h):
                dve.wait_ge(out_done, q + 1)
                dve.wait_ge(h1b_ready, q + 1)
                dve.wait_ge(stored, (q + 1) * 16)
                nc.vector.tensor_tensor(O[:, h].rearrange("p b d -> p (b d)"), bk(h, 2)[:, 0:GS * D],
                                        H1b[:, h].rearrange("p b d -> p (b d)"), ALU.add).then_inc(o_ready, 1)

            n0 = moments_of(0, 2, lambda h, j: bk(h, 1)[:, j * P:(j + 1) * P], pooled, P / (P - 1))
            n1 = moments_of(1, GS, lambda h, j: H0[:, h, j, :], h0_ready, 1.0)
            n2 = moments_of(2, GS, lambda h, j: H1[:, h, j, :], h1_ready, 1.0)
            c1, s1 = layer_norm(0, lambda h: H0[:, h])
            c2, s2 = layer_norm(1, lambda h: H1[:, h])
            groups(dve, n0 + [norm_pooled] + n1[:3] + [c1, n1[3], s1, values, maxima, shift, inv_sums, residual]
                   + n2[:3] + [c2, n2[3], s2, with_bias, outputs])

        @block.tensor
        def _(pe):
            pe.wait_ge(imp_steps, 9)
            for s in range(2):
                nc.tensor.transpose(bank[s][:, 0:B], cs[:, 1 - s:1 - s + T3], ident[0:B, 0:B]).then_inc(cs_turned, 1)
            pe.wait_ge(csT_ready, 2)
            pe.wait_ge(tail_in, 160)

            def turn_features(q, h):
                pe.wait_ge(o_ready, q + 1)
                pe.wait_ge(f_staged, q + 1)
                for c in range(GS):
                    mm = nc.tensor.transpose(bk(h, 0)[:, c * P:(c + 1) * P], Fs[:, h, c, :], ident[:, :])
                mm.then_inc(f_turned, 1)

            def pool_time(q, h):
                pe.wait_ge(ft_ready, q + 1)
                pe.wait_ge(wm_ready, q + 1)
                for c in range(GS):
                    pair, one = divmod(c, 2)
                    mm = nc.tensor.matmul(bk(h, 1)[one * D:(one + 1) * D, pair * P:(pair + 1) * P], WM[:, h, c, :],
                                          FT[:, h, c, :], start=True, stop=True)
                mm.then_inc(pooled, 1)

            def turn_pooled(q, h):
                pe.wait_ge(normed[0], q * 2 + 2)
                for j in range(2):
                    mm = nc.tensor.transpose(bk(h, 2)[:, j * P:(j + 1) * P], Xn[:, h, j, :], ident[:, :])
                mm.then_inc(norm_turned[0], 1)

            def turn_normed(i):
                def f(q, h):
                    pe.wait_ge(normed[1 + i], q + 1)
                    for j in range(2):
                        src = Xa[:, h, i, 2 * j:2 * j + 2, :].rearrange("p b d -> p (b d)")
                        mm = nc.tensor.transpose(bk(h, 0)[:, j * P:(j + 1) * P], src, ident[:, :])
                    mm.then_inc(norm_turned[1 + i], 1)
                return f

            def qkv(q, h):
                pe.wait_ge(xt_ready[0], q + 1)
                x = XT[:, h, 0].rearrange("p a c -> p (a c)")
                for i in range(2):
                    nc.tensor.matmul(bk(h, 1)[:, i * 2 * P:(i + 1) * 2 * P], wattn[:, i, :], x, start=True, stop=True)
                for j in range(2):
                    mm = nc.tensor.matmul(bk(h, 2)[:, j * P:(j + 1) * P], XT[:, h, 0, j, :], wattn[:, 2, :], start=True,
                                          stop=True)
                mm.then_inc(qkv_done, 1)

            def scores(q, h):
                pe.wait_ge(qk_ready, q * 2 + 2)
                for c in range(GS):
                    pair, one = divmod(c, 2)
                    r = slice(one * D, (one + 1) * D)
                    mm = nc.tensor.matmul(bk(h, 3 - 2 * one)[:, pair * P:(pair + 1) * P], QK[r, h, 0, pair, :],
                                          QK[r, h, 1, pair, :], start=True, stop=True)
                mm.then_inc(scores_done, 1)

            def turn_probs(q, h):
                pe.wait_ge(probs_ready, q * GS + GS)
                for c in range(GS):
                    mm = nc.tensor.transpose(bk(h, 0)[:, c * P:(c + 1) * P], PR[:, h, c, :], ident[:, :])
                mm.then_inc(probs_turned, 1)

            def attend(q, h):
                pe.wait_ge(pt_ready, q + 1)
                pe.wait_ge(v_ready, q + 1)
                for c in range(GS):
                    pair, one = divmod(c, 2)
                    mm = nc.tensor.matmul(bk(h, 2)[:, c * D:(c + 1) * D], PT[:, h, c, :],
                                          Vt[:, h, pair, one * D:(one + 1) * D], start=True, stop=True)
                mm.then_inc(attended, 1)

            def hidden0(q, h):
                pe.wait_ge(xt_ready[1], q + 1)
                for one in range(2):
                    r = slice(one * D, (one + 1) * D)
                    mm = nc.tensor.matmul(bk(h, 3 - 2 * one)[:, 0:2 * P], wi[r, :],
                                          XT[r, h, 1].rearrange("p a c -> p (a c)"), start=True, stop=True)
                mm.then_inc(hidden_done[0], 1)

            def hidden(l):
                def f(q, h, k=None):
                    pe.wait_ge(hidden_ready[l], q + 1)
                    for c in range(GS):
                        clip = (c % 2) * 2 + c // 2
                        mm = nc.tensor.matmul(bk(h, 3 - 2 * l)[:, c * P:(c + 1) * P], GW[:, h, clip, l, 0:P],
                                              HF[:, h, l, c, :], start=True, stop=True)
                    mm.then_inc(hidden_done[1 + l], 1)
                return f

            def outputs(q, h):
                pe.wait_ge(hidden_ready[2], q + (1 + W))
                for c in range(GS):
                    clip = (c % 2) * 2 + c // 2
                    mm = nc.tensor.matmul(bk(h, 2)[:, clip * D:(clip + 1) * D], HF[:, h, 2, c, :], wo[:, :], start=True,
                                          stop=True)
                mm.then_inc(out_done, 1)

            with pe.Fori(0, NG // W) as k:
                for step in [turn_features, pool_time, turn_pooled, turn_normed(0), qkv, scores, turn_probs, attend,
                             turn_normed(1), hidden0, "experts", hidden(0), hidden(1), outputs]:
                    for h in range(W):
                        if step == "experts":
                            pe.wait_ge(experts_in[h], k * (2 * GS * 16) + 2 * GS * 16)
                        else:
                            step(k * W + h, h)


def late(g):
    if isinstance(g, int):
        return [t for t in conv_tiles(g) if t[0] == 2] if g >= 0 else []
    return [(2, 0), (2, 1)]


def row_of(tile):
    return {1: ROW1, 2: ROW2, 3: ROW3}[tile[0]] + tile[1]


def convs_par(g, par):
    return convs_before(g) % 2 if isinstance(g, int) else (NTILE * par + convs_before(2)) % 2


def norms_par(g, par):
    return norms_before(g) % 2 if isinstance(g, int) else (NTILE * par + norms_before(3) - NTILE * 3) % 2


def splits_before(g):
    if isinstance(g, int):
        return sum(len([t for t in norm_tiles(i) if t[0] != 3]) for i in range(g))
    return g * 6 + (10 - 18)


def patches(xs, i, d):
    w = NB8 * STR0
    first = xs[:, bass.ds(i * (2 * w) + d * w, w + STR0)]
    return bass.AP(first.tensor, first.offset, [(XW, P), (STR0, NB8), (1, K0)])


def kernel(**x):
    import numpy as np
    import concourse.bacc as bacc
    from concourse.bass_utils import run_bass_kernel_spmd

    x = {k.replace("L0_", ""): np.asarray(v) for k, v in x.items()}
    f = np.float32

    def tap_major(w):
        return w.transpose(1, 2, 0)

    rows = np.zeros((K0ROWS, 2, P), f)
    kind = np.zeros((K0ROWS, 4), f)
    for q in range(3):
        for part in range(3):
            r = ROWS * q + NTAP * part
            rows[r:r + K0, 0] = x["tok_conv0_w"][:, 0, :].T
            rows[r + K0, 0] = x["tok_conv0_b"]
            rows[r:r + NTAP, 1] = x["tok_n0_w"]
            kind[r:r + NTAP, 0] = 1
        rows[ROWS * q + 3 * NTAP, 0] = x["tok_n0_b"]
        rows[ROWS * q + 3 * NTAP, 1] = 1
        kind[ROWS * q:ROWS * (q + 1), 1 + q] = 1
    sel = np.zeros((96, NTILE, P), f)
    for j in range(NTILE):
        sel[[j, 32 + j, 64 + j], j] = 1
    two = lambda v: np.concatenate([v, v])
    arrays = {
        "xpad": np.pad(x["x"][:, 0, :], ((0, 0), (3, 3)), mode="reflect"),
        "c0": np.concatenate([x["tok_conv0_w"][:, 0, :], x["tok_conv0_b"][:, None]], 1),
        "w0": rows, "w0k": kind, "selB": sel, "ident": np.eye(P, dtype=f),
        "wconv": np.concatenate([tap_major(x[f"tok_conv{i}_w"]) for i in (1, 2, 3)], 1),
        "cols": np.stack([x[f"tok_conv{i}_b"] for i in (1, 2, 3)] + [x[f"tok_n{i}_w"] for i in (1, 2, 3)]
                         + [x[f"tok_n{i}_b"] for i in (1, 2, 3)] + [x["tok_n4_w"], x["tok_n4_b"]]
                         + list(x["tok_mlp_b1"].reshape(KC, P)) + list(x["tok_mlp_b2"].reshape(KC, P))
                         + list(x["tok_mlp_w3"].reshape(KC, P)) + [two(x["attn_bq"]), two(x["attn_bk"]), x["ffn_bi"]], 1),
    }
    def pair(m):
        z = np.zeros((2, D, 2, D), f)
        z[0, :, 0] = z[1, :, 1] = m
        return z.reshape(P, P)

    arrays.update({
        "mlp1": x["tok_mlp_w1"], "mlp2": x["tok_mlp_w2"].reshape(KC, P, DM).transpose(1, 0, 2),
        "b3": np.repeat(x["tok_mlp_b3"][:, None], B, 0),
        "iota": np.tile(np.append(np.arange(D), FAR).astype(f), (P, 1)),
        "attn": np.stack([pair(x[f"attn_W{c}"]) for c in "qkv"], 1),
        "bv": np.tile(two(x["attn_bv"]), (P, 1)), "bo": np.tile(x["ffn_bo"], (P, 1)),
        "wi": two(x["ffn_Wi"].T), "wo": x["ffn_Wo"].T,
        "wr": np.concatenate([x["ffn_Wr"].transpose(3, 0, 1, 2), x["ffn_br"].transpose(2, 0, 1)[..., None]], 3),
        "ws": np.concatenate([x["ffn_Ws"].transpose(3, 0, 1, 2), x["ffn_bs"].transpose(2, 0, 1)[..., None]], 3)[:, :, 0],
        "route": x["ffn_route_id"][None, :],
    })
    arrays = {k: np.ascontiguousarray(v) for k, v in arrays.items()}
    nc = bacc.Bacc("TRN2", target_bir_lowering=False, num_devices=1)
    aps = {k: nc.dram_tensor("in_" + k, v.shape, mybir.dt.from_np(v.dtype), kind="ExternalInput").ap() for k, v in arrays.items()}
    out = nc.dram_tensor("out", (B, P, D), F32, kind="ExternalOutput").ap()
    audio_kernel(nc, aps, out)
    r = run_bass_kernel_spmd(nc, [{"in_" + k: v for k, v in arrays.items()}], core_ids=[0])
    return r.results[0]["out"]
```

```python
from contextlib import ExitStack

import concourse.bass as bass
from concourse import mybir

F32 = mybir.dt.float32
F32R = mybir.dt.float32r
BF16 = mybir.dt.bfloat16
I32 = mybir.dt.int32
ALU = mybir.AluOpType
ACT = mybir.ActivationFunctionType
AX = mybir.AxisListType

P = 128
B = 64
L = 10240
EPS = 1e-5
TEMP = 1e-5
T0, T1, T2, T3 = 2048, 512, 256, 128
K0, STR0 = 10, 5
LPAD = L + 6
GS = 4
NG = B // GS
HALF = T0 // 2
XW = STR0 * (HALF - 1) + K0 + 0
NTAP = K0 + 1
ROWS = 36
K0ROWS = 3 * ROWS
BLK = 8
BW = STR0 * (BLK - 1) + K0
NBLK = HALF // BLK
NB8 = 4 * BLK
NSTEP = NBLK // 4
DM = 512
KC = DM // P
NE = 16
EW = P + 1
D = 64

CB, CG, CN = 0, 3, 6
CG4, CN4, CM1, CM2, CW3, CBQ, CBK, CBI = 9, 10, 11, 15, 19, 23, 24, 25
NCOLS = 26
FAR = 1e30
W = 4

ROW1, ROW2, ROW3 = 0, 4, 6
NTILE = 7


def conv_tiles(g):
    return ([(1, s) for s in range(4)] if g < NG else []) + ([(3, 0)] if 0 <= g - 2 < NG else []) + \
        ([(2, 0), (2, 1)] if 0 <= g - 1 < NG else [])


def norm_tiles(g):
    return ([(2, 0), (2, 1)] if 0 <= g - 2 < NG else []) + \
        ([(1, s) for s in range(4)] if 0 <= g - 1 < NG else []) + ([(3, 0)] if 0 <= g - 3 < NG else [])


RING = 4
LOOP_FROM, LOOP_TO = 3, 15
LAST = NG + 2
FULL = conv_tiles(LOOP_FROM)
FULLN = norm_tiles(LOOP_FROM)


def before(g, tiles, full_from):
    if isinstance(g, int):
        return sum(len(tiles(i)) for i in range(g))
    return g * NTILE + (sum(len(tiles(i)) for i in range(full_from)) - NTILE * full_from)


def convs_before(g):
    return before(g, conv_tiles, 2)


def norms_before(g):
    return before(g, norm_tiles, 3)


def until(eng, sem, count):
    if isinstance(count, int) and count <= 0:
        return
    eng.wait_ge(sem, count)


def waits_behind(eng, sem, count, *others):
    others = [(s, c if isinstance(c, int) else eng.compute_val(c)) for s, c in others]
    eng.wait_ge(sem, count)
    for s, c in others:
        until(eng, s, c)


def each_iteration(eng, step):
    for g in range(LOOP_FROM):
        step(g, g % 2)
    with eng.Fori(0, (LOOP_TO - LOOP_FROM) // 2) as i:
        for d in range(2):
            step(i * 2 + (LOOP_FROM + d), (LOOP_FROM + d) % 2)
    for g in range(LOOP_TO, LAST + 1):
        step(g, g % 2)


def each_pair(eng, pair):
    pair(0)
    with eng.Fori(1, NSTEP // 2) as i:
        pair(i)


def has(g, what):
    if not isinstance(g, int):
        return True
    return {"conv1": g < NG, "conv2": 0 <= g - 1 < NG, "conv3": 0 <= g - 2 < NG, "next": g + 1 < NG,
            "batch": 0 <= g - 1 and g <= LAST}[what]


def tiles_of(g, tiles, full):
    return tiles(g) if isinstance(g, int) else full


def audio_kernel(nc, a, out):
    with ExitStack() as ctx:
        F = ctx.enter_context(nc.sbuf_tensor("F", [P, B * T3], F32))
        cols = ctx.enter_context(nc.sbuf_tensor("cols", [P, NCOLS], F32))
        ident = ctx.enter_context(nc.sbuf_tensor("ident", [P, P], F32))
        LG = ctx.enter_context(nc.sbuf_tensor("LG", [B, 2, T3], F32))
        bank = [ctx.enter_context(nc.psum_tensor(f"bank{i}", [P, 512], F32)) for i in range(8)]
        convolutions(nc, a, ctx, bank, F, cols, ident)
        importance_mlp(nc, a, ctx, bank, F, cols, LG)
        pool_attend_experts(nc, a, ctx, bank, F, cols, ident, LG, out)


def convolutions(nc, a, outer, bank, F, cols, ident):
    with ExitStack() as ctx:
        def sb(name, shape, dt=F32, at=None):
            return (at or ctx).enter_context(nc.sbuf_tensor(name, shape, dt))

        def sem(name):
            return outer.enter_context(nc.semaphore(name))

        convs = ctx.enter_context(ExitStack())
        wc = sb("wc", [P, 2, 16, P], F32R, convs)
        W0 = sb("W0", [K0ROWS, P], BF16, convs)
        selV = sb("selV", [P, NTILE, P], F32R, convs)
        selB = sb("selB", [96, NTILE, P], BF16, convs)
        bc = sb("bc", [P, 3], F32, convs)
        R = sb("R", [K0ROWS, 4, T0], BF16, convs)
        RS = sb("RS", [96, T1], BF16, convs)
        vs = sb("vs", [NTILE + 1, T1], F32, convs)
        iv = sb("iv", [NTILE + 1, T1], F32, convs)
        rs = sb("rs", [NTILE + 1, T1], F32, convs)
        rr = sb("rr", [NTILE + 1, T1], F32, convs)
        mt = sb("mt", [NTILE + 1, T1], BF16, convs)

        with ExitStack() as st:
            xs = sb("xs", [P, XW], F32, st)
            xst = sb("xst", [P, 2, 4 * BLK * STR0 + 5], F32, st)
            X45 = sb("X45", [64, 2, 4 * P], F32, st)
            TG = sb("TG", [BW + 1, BLK, NTAP], F32, st)
            Gs = sb("Gs", [NTAP, NTAP], F32, st)
            c0 = sb("c0", [P, NTAP], F32, st)
            c0c = sb("c0c", [P, NTAP], F32, st)
            onesC = sb("onesC", [P, P], F32, st)
            prod = sb("prod", [P, 2, 4 * BLK * K0], F32, st)
            red = sb("red", [P, 2, 4 * BLK], F32, st)
            var0 = sb("var0", [P, HALF], F32, st)
            rstd0 = sb("rstd0", [P, HALF], F32, st)
            ps = sb("ps", [P, 3, HALF], F32, st)
            rt = sb("rt", [P, 2, HALF], F32, st)
            S = sb("S", [P, 3, 3, HALF], BF16, st)
            ones_bf = sb("ones_bf", [P, HALF], BF16, st)
            wraw = sb("wraw", [P, 16, P], F32, st)
            wmean = sb("wmean", [P, 16], F32, st)
            w0 = sb("w0", [K0ROWS, 2, P], F32, st)
            w0k = sb("w0k", [K0ROWS, 4], F32, st)
            w0m = sb("w0m", [K0ROWS, 2], F32, st)
            w0t = sb("w0t", [K0ROWS, 2, P], F32, st)
            w0p = sb("w0p", [K0ROWS, 3, P], BF16, st)
            selBf = sb("selBf", [96, NTILE, P], F32, st)

        with ExitStack() as cv:
            A0 = sb("A0", [P, 2, 2, 4, T1 + 2], F32R, cv)
            A1 = sb("A1", [P, 2, 2, GS, T2 + 2], F32R, cv)
            A2 = sb("A2", [P, 2, 2, GS, T3 + 2], F32R, cv)
            Y = sb("Y", [P, 2, NTILE, T1], F32, cv)
            sqh = sb("sqh", [P, RING, T1], F32R, cv)
            sql = sb("sql", [P, RING, T1], F32R, cv)
            sqf = sb("sqf", [P, 2, T1], F32, cv)
            N = sb("N", [P, RING, T1], F32, cv)
            AF = sb("AF", [P, RING, T1], F32, cv)
        scratch = nc.dram_tensor("scratch", (ROWS, B * T0), BF16, kind="Internal").ap()

        P0, CONV, V, RB = bank[0:2], (bank[2], bank[3], bank[7]), bank[4], bank[5:7]

        x_in = sem("x_in")
        c0_in = sem("c0_in")
        w_in = sem("w_in")
        const_in = sem("const_in")
        ones_set = sem("ones_set")
        tg_clear = sem("tg_clear")
        gram_steps = sem("gram_steps")
        gram_act = sem("gram_act")
        tg_in = sem("tg_in")
        staged = sem("staged")
        turned = sem("turned")
        x45_ready = sem("x45_ready")
        quad_done = sem("quad_done")
        prod_done = sem("prod_done")
        red_done = sem("red_done")
        var_ready = sem("var_ready")
        inv_ready = sem("inv_ready")
        rstd_ready = sem("rstd_ready")
        scaled = sem("scaled")
        high_ready = sem("high_ready")
        rest_ready = sem("rest_ready")
        mid_ready = sem("mid_ready")
        low_ready = sem("low_ready")
        rows_out = [sem(f"rows_out{i}") for i in range(3)]
        ones_out = sem("ones_out")
        wsetup = sem("wsetup")
        psetup = sem("psetup")
        r_in = [sem(f"r_in{i}") for i in range(4)]
        conv0_done = sem("conv0_done")
        h0_high = sem("h0_high")
        h0_low = sem("h0_low")
        h0_pads = sem("h0_pads")
        conv1_done = sem("conv1_done")
        conv2_done = sem("conv2_done")
        conv3_done = sem("conv3_done")
        y_done = sem("y_done")
        sq_done = sem("sq_done")
        sql_done = sem("sql_done")
        var_done = sem("var_done")
        vs_done = sem("vs_done")
        iv_done = sem("iv_done")
        rs_done = sem("rs_done")
        parts_done = sem("parts_done")
        spread = sem("spread")
        n_done = sem("n_done")
        relu_done = sem("relu_done")
        ah_done = sem("ah_done")
        al_done = sem("al_done")
        a_pads = sem("a_pads")

        def phases(r0):
            return xs[:, r0:r0 + STR0 * (HALF - 1) + 1:STR0].rearrange("p (q r) -> p r q", r=4)

        block = ctx.enter_context(nc.Block())

        @block.sync
        def _(sp):
            x = a["xpad"]
            halves = bass.AP(x.tensor, x.offset, [(LPAD, B), (STR0 * HALF, 2), (1, XW)])
            sp.dma_start(xs[:, :], halves).then_inc(x_in, 16)
            sp.dma_start(wraw[:, :, :], a["wconv"]).then_inc(w_in, 16)
            sp.wait_ge(tg_clear, 1)
            sp.wait_ge(gram_act, 1)
            for t in range(BLK):
                sp.dma_start(TG[STR0 * t:STR0 * t + K0, t, :], Gs[0:K0, :]).then_inc(tg_in, 16)
            bias_row = Gs[K0:K0 + 1, :].unsqueeze(1).broadcast_to([1, BLK, NTAP])
            sp.dma_start(TG[BW:BW + 1, :, :], bias_row).then_inc(tg_in, 16)
            sp.wait_ge(ones_set, 2)
            for i in range(3 * NTAP, ROWS):
                sp.dma_start(scratch[i, :].rearrange("(p t) -> p t", p=P), ones_bf[:, :]).then_inc(ones_out, 16)
            for k in range(NTAP):
                sp.wait_ge(low_ready, k + 1)
                dst = scratch[k:3 * NTAP:NTAP, :].rearrange("i (p t) -> p i t", p=P)
                sp.dma_start(dst, S[:, k % 3, :, :]).then_inc(rows_out[k % 3], 16)
            sp.wait_ge(ones_out, 16 * (ROWS - 3 * NTAP))
            for i in range(3):
                sp.wait_ge(rows_out[i], 16 * len(range(i, NTAP, 3)))

            def load(clip, slot):
                for q in range(3):
                    src = scratch[:, bass.ds(clip * T0, T0)]
                    sp.dma_start(R[ROWS * q:ROWS * (q + 1), slot, :], src).then_inc(r_in[slot], 16)

            for s in range(4):
                load(s, s)
            with sp.Fori(0, NG - 1) as i:
                for s in range(4):
                    sp.wait_ge(conv0_done, i * 16 + (4 * s + 4))
                    load(i * 4 + (4 + s), s)

        @block.gpsimd
        def _(pool):
            pool.wait_ge(x_in, 16)
            W = NB8 * STR0

            def stage(i):
                for d in range(2):
                    waits_behind(pool, x_in, 16, (turned, i * 2 + (d - 1)))
                    nc.gpsimd.tensor_copy(xst[:, d, 0:W + 5], xs[:, bass.ds(i * (2 * W) + d * W, W + 5)]).then_inc(staged, 1)

            each_pair(pool, stage)
            for k in range(NTAP):
                pool.wait_ge(mid_ready, k + 1)
                nc.gpsimd.tensor_tensor(S[:, k % 3, 2, :], rt[:, k % 2, :], S[:, k % 3, 1, :], ALU.subtract)\
                    .then_inc(low_ready, 1)

            def borders0(clip, slot):
                waits_behind(pool, x_in, 16, (h0_low, clip * 4 + 4), (conv1_done, clip - 1))
                t = A0[:, slot]
                for (r, c), (r1, c1) in (((2, 0), (2, 1)), ((3, 0), (1, 1)), ((0, T1 + 1), (2, T1)), ((1, T1 + 1), (1, T1))):
                    nc.gpsimd.tensor_copy(t[:, :, r, c:c + 1], t[:, :, r1, c1:c1 + 1].bitcast(F32))\
                        .then_inc(h0_pads, 1)

            def square(g, par, n, tile):
                at = convs_before(g) + n
                slot = n % RING
                y = Y[:, par, row_of(tile), :]
                pool.wait_ge(y_done, at + 1)
                nc.gpsimd.tensor_tensor(sqf[:, n % 2, :], y, y, ALU.mult).then_inc(sq_done, 1)
                pool.wait_ge(sq_done, at + 1)
                until(pool, var_done, summed_before(g, n))
                nc.gpsimd.tensor_tensor(sql[:, slot, :], sqf[:, n % 2, :], sqh[:, slot, :].bitcast(F32), ALU.subtract)\
                    .then_inc(sql_done, 1)

            def borders(g, n, tile):
                level, s = tile
                if level == 3:
                    return
                waits_behind(pool, x_in, 16, (al_done, splits_before(g) + n + 1))
                buf, w, c = (A1, T2, slice(s, s + 1)) if level == 1 else (A2, T3, slice(2 * s, 2 * s + 2))
                nc.gpsimd.tensor_copy(buf[:, :, 1, c, 0:1], buf[:, :, 1, c, 1:2].bitcast(F32)).then_inc(a_pads, 1)
                nc.gpsimd.tensor_copy(buf[:, :, 0, c, w + 1:w + 2], buf[:, :, 0, c, w:w + 1].bitcast(F32))\
                    .then_inc(a_pads, 1)

            borders0(0, 0)

            def step(g, par):
                tiles = tiles_of(g, conv_tiles, FULL)
                norms = tiles_of(g, norm_tiles, FULLN)
                if has(g, "conv1"):
                    for s in range(3):
                        borders0(g * 4 + (s + 1), (s + 1) % 2)
                        square(g, par, s, tiles[s])
                first = 3 if has(g, "conv1") else 0
                squares = [lambda n=n: square(g, par, n, tiles[n]) for n in range(first, len(tiles))]
                edges = [lambda n=n: borders(g, n, norms[n]) for n in range(len(norms))]
                for f in edges[:2]:
                    f()
                if has(g, "conv1"):
                    order = edges[2:4] + squares[:1] + edges[4:]
                    if has(g, "next"):
                        order += [lambda: borders0(g * 4 + 4, 0)]
                    order += squares[1:]
                else:
                    order = edges[2:] + squares
                for work in order:
                    work()

            each_iteration(pool, step)

        @block.scalar
        def _(act):
            act.dma_start(c0[:, :], a["c0"]).then_inc(c0_in, 16)
            for dst, name in ((w0[:, :, :], "w0"), (w0k[:, :], "w0k"), (selBf[:, :, :], "selB"), (cols[:, :], "cols"),
                              (ident[:, :], "ident")):
                act.dma_start(dst, a[name]).then_inc(const_in, 16)
            act.wait_ge(gram_steps, 3)
            nc.scalar.activation(Gs[:, :], bank[5][0:NTAP, 0:NTAP], ACT.Copy).then_inc(gram_act, 1)
            act.wait_ge(tg_clear, 1)

            def turned_out(i):
                for d in range(2):
                    act.wait_ge(turned, i * 2 + (d + 1))
                    until(act, quad_done, i * 2 + (d - 1))
                    nc.scalar.activation(X45[0:BW, d, :], bank[d][0:BW, :], ACT.Copy).then_inc(x45_ready, 1)

            each_pair(act, turned_out)
            act.wait_ge(inv_ready, 1)
            nc.scalar.activation(rstd0[:, :], var0[:, :], ACT.Sqrt).then_inc(rstd_ready, 1)

            def high(k):
                act.wait_ge(scaled, k + 1)
                if k >= 3:
                    act.wait_ge(rows_out[k % 3], 16 * (k // 3))
                nc.scalar.activation(S[:, k % 3, 0, :], ps[:, k % 3, :], ACT.Copy).then_inc(high_ready, 1)

            high(0)
            for k in range(NTAP):
                if k + 1 < NTAP:
                    high(k + 1)
                act.wait_ge(rest_ready, k + 1)
                nc.scalar.activation(S[:, k % 3, 1, :], rt[:, k % 2, :], ACT.Copy).then_inc(mid_ready, 1)

            def relu0(clip, slot, r):
                act.wait_ge(conv0_done, clip * 4 + (r + 1))
                until(act, conv1_done, clip - 1)
                nc.scalar.activation(A0[:, slot, 0, r, 1:T1 + 1], P0[r % 2][:, :], ACT.Relu).then_inc(h0_high, 1)

            def centre(g, par, n, tile):
                level, s = tile
                at = convs_before(g) + n
                slot = n % RING
                src = CONV[bank_of(tile)]
                done, count = {1: (conv1_done, g * 4 + (s + 1)), 2: (conv2_done, (g - 1) * 2 + (s + 1)),
                               3: (conv3_done, g - 1)}[level]
                act.wait_ge(done, count)
                until(act, n_done, norms_before(g))
                bias = bc[:, level - 1:level]
                nc.scalar.activation(Y[:, par, row_of(tile), :], src[:, :], ACT.Identity, bias=bias)
                until(act, var_done, summed_before(g, n))
                nc.scalar.activation(sqh[:, slot, :], src[:, :], ACT.Square, bias=bias).then_inc(y_done, 1)

            def relu(g, par, n, tile):
                level, s = tile
                at = norms_before(g) + n
                slot = n % RING
                act.wait_ge(n_done, at + 1)
                src = N[:, slot, :]
                if level == 3:
                    dst = F[:, bass.ds((g - 3) * (GS * T3), GS * T3)]
                elif level == 1:
                    src = src.rearrange("p (q r) -> p r q", r=2)
                    dst = AF[:, slot, :].rearrange("p (r q) -> p r q", r=2)
                else:
                    src = src.rearrange("p (s q r) -> p r s q", r=2, s=2)
                    dst = AF[:, slot, :].rearrange("p (r s q) -> p r s q", r=2, s=2)
                if level != 3:
                    until(act, al_done, splits_before(g) + max(n - RING + 1, 0))
                nc.scalar.activation(dst, src, ACT.Relu, scale=cols[:, CG + level - 1:CG + level],
                                     bias=cols[:, CN + level - 1:CN + level]).then_inc(relu_done, 1)

            act.wait_ge(psetup, 1)
            for r in range(4):
                relu0(0, 0, r)

            def step(g, par):
                tiles = tiles_of(g, conv_tiles, FULL)
                norms = tiles_of(g, norm_tiles, FULLN)
                conv1 = has(g, "conv1")
                if conv1:
                    for s in range(2):
                        for r in range(4):
                            relu0(g * 4 + (s + 1), (s + 1) % 2, r)
                        centre(g, par, s, tiles[s])
                if has(g, "batch"):
                    act.wait_ge(iv_done, g * 4)
                    until(act, parts_done, g * 5 - 8)
                    nc.scalar.activation(rs[:, :], iv[:, :], ACT.Sqrt).then_inc(rs_done, 1)
                if conv1:
                    for r in range(4):
                        relu0(g * 4 + 3, 1, r)
                    centre(g, par, 2, tiles[2])
                relus = [lambda n=n: relu(g, par, n, norms[n]) for n in range(len(norms))]
                centres = [lambda n=n: centre(g, par, n, tiles[n]) for n in range(3 if conv1 else 0, len(tiles))]
                ahead = [lambda r=r: relu0(g * 4 + 4, 0, r) for r in range(4)] if conv1 and has(g, "next") else []
                if conv1:
                    order = relus[:4] + centres[:1] + ahead[:1] + relus[4:5] + ahead[1:2] + relus[5:6] + centres[1:2] \
                        + relus[6:] + ahead[2:] + centres[2:]
                else:
                    order = relus + centres
                for work in order:
                    work()

            each_iteration(act, step)

        @block.vector
        def _(dve):
            count = [0]

            def chain(ins):
                count[0] += 1
                ins.then_inc(wsetup, 1)
                dve.wait_ge(wsetup, count[0])

            nc.vector.memset(onesC[:, :], 1.0 / P).then_inc(ones_set, 1)
            nc.vector.memset(ones_bf[:, :], 1.0).then_inc(ones_set, 1)
            nc.vector.memset(X45[32:64, :, :], 1.0)
            nc.vector.memset(TG[:, :, :], 0.0).then_inc(tg_clear, 1)
            dve.wait_ge(c0_in, 16)
            dve.wait_ge(gram_steps, 1)
            nc.vector.tensor_tensor(c0c[:, :], c0[:, :], bank[4][:, 0:NTAP], ALU.subtract).then_inc(gram_steps, 1)
            def quadratic(i):
                for d in range(2):
                    dve.wait_ge(quad_done, i * 2 + (d + 1))
                    z = bank[2 + d][:, 0:NB8 * NTAP].rearrange("p (t k) -> p t k", k=NTAP)
                    nc.vector.tensor_tensor(prod[:, d, :].rearrange("p (t k) -> p t k", k=K0), z[:, :, 0:K0],
                                            patches(xs, i, d), ALU.mult).then_inc(prod_done, 1)
                    dve.wait_ge(prod_done, i * 2 + (d + 1))
                    nc.vector.tensor_reduce(red[:, d, :], prod[:, d, :].rearrange("p (t k) -> p t k", k=K0), AX.X,
                                            ALU.add).then_inc(red_done, 1)
                    dve.wait_ge(red_done, i * 2 + (d + 1))
                    nc.vector.tensor_tensor(var0[:, bass.ds(i * (2 * NB8) + d * NB8, NB8)], red[:, d, :],
                                            z[:, :, K0], ALU.add).then_inc(var_ready, 1)

            each_pair(dve, quadratic)
            dve.wait_ge(var_ready, NSTEP)
            chain(nc.vector.tensor_scalar(rstd0[:, :], var0[:, :], 1.0 / (P - 1), EPS, ALU.mult, ALU.add))
            nc.vector.reciprocal(var0[:, :], rstd0[:, :]).then_inc(inv_ready, 1)
            dve.wait_ge(rstd_ready, 1)
            rq = rstd0[:, :].rearrange("p (q r) -> p r q", r=4)

            def scale(k):
                if k >= 3:
                    dve.wait_ge(rest_ready, k - 2)
                o = ps[:, k % 3, :].rearrange("p (r q) -> p r q", r=4)
                if k < K0:
                    nc.vector.tensor_tensor(o, phases(k), rq, ALU.mult).then_inc(scaled, 1)
                else:
                    nc.vector.tensor_copy(o, rq).then_inc(scaled, 1)

            scale(0)
            for k in range(NTAP):
                if k + 1 < NTAP:
                    scale(k + 1)
                dve.wait_ge(high_ready, k + 1)
                if k >= 2:
                    dve.wait_ge(low_ready, k - 1)
                nc.vector.tensor_tensor(rt[:, k % 2, :], ps[:, k % 3, :], S[:, k % 3, 0, :], ALU.subtract)\
                    .then_inc(rest_ready, 1)

            dve.wait_ge(w_in, 16)
            chain(nc.vector.tensor_reduce(wmean[:, :], wraw[:, :, :], AX.X, ALU.add))
            chain(nc.vector.tensor_scalar(wmean[:, :], wmean[:, :], 1.0 / P, None, ALU.mult))
            mean = wmean[:, :].unsqueeze(2).broadcast_to([P, 16, P])
            chain(nc.vector.tensor_tensor(wraw[:, :, :], wraw[:, :, :], mean, ALU.subtract))
            chain(nc.vector.tensor_copy(wc[:, 0], wraw[:, :, :]))
            nc.vector.tensor_tensor(wc[:, 1], wraw[:, :, :], wc[:, 0].bitcast(F32), ALU.subtract)
            dve.wait_ge(const_in, 80)
            chain(nc.vector.tensor_reduce(w0m[:, 0:1], w0[:, 0, :], AX.X, ALU.add))
            chain(nc.vector.tensor_scalar(w0m[:, 1:2], w0m[:, 0:1], w0k[:, 0:1], 1.0 / P, ALU.mult, ALU.mult))
            chain(nc.vector.tensor_scalar(w0t[:, 0, :], w0[:, 0, :], w0m[:, 1:2], None, ALU.subtract))
            chain(nc.vector.tensor_tensor(w0t[:, 0, :], w0t[:, 0, :], w0[:, 1, :], ALU.mult))
            chain(nc.vector.tensor_copy(w0p[:, 0, :], w0t[:, 0, :]))
            chain(nc.vector.tensor_tensor(w0t[:, 1, :], w0t[:, 0, :], w0p[:, 0, :], ALU.subtract))
            chain(nc.vector.tensor_copy(w0p[:, 1, :], w0t[:, 1, :]))
            chain(nc.vector.tensor_tensor(w0p[:, 2, :], w0t[:, 1, :], w0p[:, 1, :], ALU.subtract))
            chain(nc.vector.tensor_scalar(w0t[:, 0, :], w0p[:, 0, :], w0k[:, 1:2], None, ALU.mult))
            chain(nc.vector.scalar_tensor_tensor(w0t[:, 1, :], w0p[:, 1, :], w0k[:, 2:3], w0t[:, 0, :], ALU.mult, ALU.add))
            chain(nc.vector.scalar_tensor_tensor(W0[:, :], w0p[:, 2, :], w0k[:, 3:4], w0t[:, 1, :], ALU.mult, ALU.add))
            nc.vector.tensor_copy(selB[:, :, :], selBf[:, :, :])
            chain(nc.vector.memset(selV[:, :, :].bitcast(F32), 0.0))
            for j in range(NTILE):
                nc.vector.memset(selV[:, j, j:j + 1].bitcast(F32), 1.0)
            nc.vector.memset(RS[:, :], 0.0)
            dve.wait_ge(gram_steps, 4)
            nc.vector.tensor_tensor(bc[:, :], cols[:, CB:CB + 3], bank[4][:, 16:19], ALU.subtract).then_inc(psetup, 1)

            def low0(clip, slot, r):
                dve.wait_ge(h0_high, clip * 4 + (r + 1))
                nc.vector.scalar_tensor_tensor(A0[:, slot, 1, r, 1:T1 + 1], P0[r % 2][:, :], 0.0,
                                               A0[:, slot, 0, r, 1:T1 + 1].bitcast(F32), ALU.max, ALU.subtract)\
                    .then_inc(h0_low, 1)

            def normalise(g, par, n, tile):
                at = norms_before(g) + n
                slot = n % RING
                dve.wait_ge(spread, at + 1)
                until(dve, relu_done, norms_before(g) + max(n - RING + 1, 0))
                nc.vector.tensor_tensor(N[:, slot, :], RB[norms_par(g, par, n)][:, :], Y[:, 1 - par, row_of(tile), :], ALU.mult)\
                    .then_inc(n_done, 1)

            def split(g, par, n, tile):
                level, s = tile
                if level == 3:
                    return
                at = norms_before(g) + n
                slot = n % RING
                dve.wait_ge(relu_done, at + 1)
                if level == 1:
                    src = AF[:, slot, :].rearrange("p (r q) -> p r q", r=2)
                    hi, lo = (A1[:, part, :, s, 1:T2 + 1] for part in range(2))
                    until(dve, conv2_done, (g - 1) * 2)
                else:
                    src = AF[:, slot, :].rearrange("p (r s q) -> p r s q", r=2, s=2)
                    hi, lo = (A2[:, part, :, 2 * s:2 * s + 2, 1:T3 + 1] for part in range(2))
                    until(dve, conv3_done, g - 2)
                nc.vector.tensor_copy(hi, src).then_inc(ah_done, 1)
                dve.wait_ge(ah_done, splits_before(g) + n + 1)
                nc.vector.tensor_tensor(lo, src, hi.bitcast(F32), ALU.subtract).then_inc(al_done, 1)

            for r in range(4):
                low0(0, 0, r)

            def step(g, par):
                norms = tiles_of(g, norm_tiles, FULLN)
                conv1 = has(g, "conv1")
                batch = has(g, "batch")
                if conv1:
                    for r in range(4):
                        low0(g * 4 + 1, 1, r)
                if batch:
                    dve.wait_ge(var_done, convs_before(g))
                    nc.vector.tensor_scalar(vs[:, :], V[0:NTILE + 1, :], 1.0 / (P - 1), EPS, ALU.mult, ALU.add)\
                        .then_inc(vs_done, 1)
                for part, r in ((0, 0), (1, 1), (None, 2), (2, 3), (3, None)):
                    if conv1 and r is not None:
                        low0(g * 4 + 2, 0, r)
                    if batch and part is not None:
                        if part == 0:
                            dve.wait_ge(vs_done, g)
                        c = slice(part * P, (part + 1) * P)
                        nc.vector.reciprocal(iv[:, c], vs[:, c]).then_inc(iv_done, 1)
                if conv1:
                    low0(g * 4 + 3, 1, 0)
                if batch:
                    dve.wait_ge(rs_done, g)
                    until(dve, spread, norms_before(g))
                    nc.vector.tensor_copy(RS[0:NTILE + 1, :], rs[:, :]).then_inc(parts_done, 1)
                    dve.wait_ge(parts_done, g * 5 - 4)
                    nc.vector.tensor_tensor(rr[:, :], rs[:, :], RS[0:NTILE + 1, :], ALU.subtract).then_inc(parts_done, 1)
                if conv1:
                    low0(g * 4 + 3, 1, 1)
                if batch:
                    dve.wait_ge(parts_done, g * 5 - 3)
                    nc.vector.tensor_copy(mt[:, :], rr[:, :]).then_inc(parts_done, 1)
                    dve.wait_ge(parts_done, g * 5 - 2)
                    nc.vector.tensor_tensor(RS[64:64 + NTILE + 1, :], rr[:, :], mt[:, :], ALU.subtract)\
                        .then_inc(parts_done, 1)
                    nc.vector.tensor_copy(RS[32:32 + NTILE + 1, :], mt[:, :]).then_inc(parts_done, 1)
                if conv1:
                    low0(g * 4 + 3, 1, 2)
                    low0(g * 4 + 3, 1, 3)
                for n in range(9):
                    if n < len(norms):
                        normalise(g, par, n, norms[n])
                    if 0 <= n - 2 < len(norms):
                        split(g, par, n - 2, norms[n - 2])
                    if n >= 5 and conv1 and has(g, "next"):
                        low0(g * 4 + 4, 0, n - 5)

            each_iteration(dve, step)

        @block.tensor
        def _(pe):
            pe.wait_ge(c0_in, 16)
            pe.wait_ge(ones_set, 1)
            nc.tensor.matmul(bank[4][:, 0:NTAP], onesC[:, :], c0[:, :], start=True, stop=True).then_inc(gram_steps, 1)
            pe.wait_ge(gram_steps, 2)
            nc.tensor.matmul(bank[5][0:NTAP, 0:NTAP], c0c[:, :], c0c[:, :], start=True, stop=True).then_inc(gram_steps, 1)
            pe.wait_ge(const_in, 80)
            nc.tensor.matmul(bank[4][:, 16:19], onesC[:, :], cols[:, CB:CB + 3], start=True, stop=True)\
                .then_inc(gram_steps, 1)
            pe.wait_ge(tg_in, 16 * (BLK + 1))

            def turn(i, d):
                waits_behind(pe, const_in, 80, (staged, i * 2 + (d + 1)), (x45_ready, i * 2 + (d - 1)))
                for t in range(4):
                    mm = nc.tensor.transpose(bank[d][0:BW, t * P:(t + 1) * P],
                                             xst[:, d, t * BLK * STR0:t * BLK * STR0 + BW], ident[:, :])
                mm.then_inc(turned, 1)

            def quad(i, d):
                pe.wait_ge(x45_ready, i * 2 + (d + 1))
                until(pe, var_ready, i * 2 + (d - 1))
                for t in range(4):
                    c = slice(t * BLK * NTAP, (t + 1) * BLK * NTAP)
                    mm = nc.tensor.matmul(bank[2 + d][:, c], X45[0:BW + 1, d, t * P:(t + 1) * P],
                                          TG[:, :, :].rearrange("j t k -> j (t k)"), start=True, stop=True)
                mm.then_inc(quad_done, 1)

            def quad_behind_turn(i, last=False):
                turn(i, 1)
                quad(i, 0)
                if not last:
                    turn(i + 1, 0)
                quad(i, 1)

            turn(0, 0)
            quad_behind_turn(0)
            with pe.Fori(1, NSTEP // 2 - 1) as i:
                quad_behind_turn(i)
            quad_behind_turn(NSTEP // 2 - 1, True)

            def conv0(clip, r, slot):
                at = clip * 4 + r
                if r == 0:
                    pe.wait_ge(r_in[slot], clip * 12 + (48 - 12 * slot))
                until(pe, h0_low, at - 1)
                nc.tensor.matmul(P0[r % 2][:, :], W0[:, :], R[:, slot, :].rearrange("p (e r q) -> p r e q", e=2, r=4)[:, r], start=True, stop=True)\
                    .then_inc(conv0_done, 1)

            def conv1(g, s, fill):
                clip = g * 4 + s
                pe.wait_ge(h0_pads, clip * 4 + 4)
                until(pe, y_done, left_before(g, s))
                n = 0
                for tap in range(8):
                    m, phase = divmod(tap, 4)
                    r = (phase + 2) % 4
                    o = m + (1 if r < 2 else 0)
                    for w, x in PASSES:
                        mm = nc.tensor.matmul(CONV[s % 2][:, :], wc[:, w, tap, :], A0[:, s % 2, x, r, o:o + T1],
                                              start=(n == 0), stop=(n == 23))
                        n += 1
                        if n == 24:
                            mm.then_inc(conv1_done, 1)
                        elif n in fill:
                            fill[n]()

            def conv_small(g, level, s, fill):
                tile = (level, s)
                until(pe, y_done, left_before(g, tiles_of(g, conv_tiles, FULL).index(tile)))
                n = 0
                first, buf, w = (8, A1, T2) if level == 2 else (12, A2, T3)
                dst = CONV[bank_of(tile)]
                cl = slice(2 * s, 2 * s + 2) if level == 2 else slice(0, 4)
                for tap in range(4):
                    m, phase = divmod(tap, 2)
                    psi = 1 - phase
                    o = m + (1 - psi)
                    for wp, x in PASSES:
                        mm = nc.tensor.matmul(dst[:, :], wc[:, wp, first + tap, :], buf[:, x, psi, cl, o:o + w],
                                              start=(n == 0), stop=(n == 11))
                        n += 1
                        if n in fill:
                            fill[n]()
                mm.then_inc(conv2_done if level == 2 else conv3_done, 1)

            def conv2(g, s, fill):
                norms = tiles_of(g, norm_tiles, FULLN)
                pe.wait_ge(a_pads, 2 * (splits_before(g) + norms.index((1, 2 * s + 1)) + 1))
                conv_small(g, 2, s, fill)

            def conv3(g, fill):
                norms = tiles_of(g, norm_tiles, FULLN)
                pe.wait_ge(a_pads, 2 * (splits_before(g) + norms.index((2, 1)) + 1))
                conv_small(g, 3, 0, fill)

            def variance(g, par, tile):
                tiles = tiles_of(g, conv_tiles, FULL)
                n = tiles.index(tile)
                at = convs_before(g) + n
                slot = n % RING
                pe.wait_ge(sql_done, at + 1)
                if n == 0:
                    until(pe, vs_done, g)
                nc.tensor.matmul(V[:, :], selV[:, row_of(tile), :], sqh[:, slot, :], start=(n == 0), stop=False)
                nc.tensor.matmul(V[:, :], selV[:, row_of(tile), :], sql[:, slot, :], start=False,
                                 stop=(n == len(tiles) - 1)).then_inc(var_done, 1)

            def bcast(g, par, n, tile):
                if n == 0:
                    pe.wait_ge(parts_done, g * 5)
                until(pe, n_done, norms_before(g) + (n - 1))
                nc.tensor.matmul(RB[norms_par(g, par, n)][:, :], selB[:, row_of(tile), :], RS[:, :], start=True, stop=True).then_inc(spread, 1)

            pe.wait_ge(psetup, 1)
            for r in range(4):
                conv0(0, r, 0)

            def step(g, par):
                tiles = tiles_of(g, conv_tiles, FULL)
                norms = tiles_of(g, norm_tiles, FULLN)
                conv1_on = has(g, "conv1")
                pending = list(enumerate(norms))

                def spread_next():
                    if pending:
                        n, tile = pending.pop(0)
                        bcast(g, par, n, tile)

                def patch(r):
                    if conv1_on and has(g, "next"):
                        conv0(g * 4 + 4, r, 0)

                def fills(s):
                    if s == 3:
                        return dict.fromkeys((2, 8, 14, 20), spread_next)
                    f = {1 + 5 * r: lambda r=r: conv0(g * 4 + (s + 1), r, (s + 1) % 4) for r in range(4)}
                    if s == 2:
                        f[20] = spread_next
                    return f

                in_conv3 = {2: spread_next, 4: lambda: patch(0), 9: lambda: patch(1), 10: spread_next}
                in_conv2 = {3: lambda: patch(2), 8: lambda: patch(3)}
                if conv1_on:
                    conv1(g, 0, fills(0))
                for tile in late(g - 1):
                    variance(g - 1, 1 - par, tile)
                if conv1_on:
                    conv1(g, 1, fills(1))
                    variance(g, par, (1, 0))
                    conv1(g, 2, fills(2))
                    variance(g, par, (1, 1))
                    conv1(g, 3, fills(3))
                else:
                    while pending:
                        spread_next()
                if has(g, "conv3"):
                    conv3(g, in_conv3)
                else:
                    for work in in_conv3.values():
                        work()
                if conv1_on:
                    variance(g, par, (1, 2))
                if has(g, "conv2"):
                    conv2(g, 0, in_conv2)
                    conv2(g, 1, {})
                else:
                    for work in in_conv2.values():
                        work()
                while pending:
                    spread_next()
                if conv1_on:
                    variance(g, par, (1, 3))

            each_iteration(pe, step)


MLP_ORDER = ((2, 0), (1, 0), (1, 1), (2, 1), (1, 2), (1, 3), (2, 2), (2, 3))
PASSES = ((0, 0), (0, 1), (1, 0))


def mlp_order(i):
    return [t for t in MLP_ORDER if t[0] == 2 or not isinstance(i, int) or i + 1 < NG]


def mlp_before(i):
    return i * 8 + KC


def mlp_steps(eng, step):
    step(0, 0)
    step(1, 1)
    with eng.Fori(1, NG // 2 - 1) as i:
        for d in range(2):
            step(i * 2 + d, d)
    step(NG - 2, 0)
    step(NG - 1, 1)


def importance_mlp(nc, a, outer, bank, F, cols, LG):
    with ExitStack() as ctx:
        def sb(name, shape, dt=F32):
            return ctx.enter_context(nc.sbuf_tensor(name, shape, dt))

        def sem(name):
            return outer.enter_context(nc.semaphore(name))

        raw1 = sb("raw1", [P, DM])
        raw2 = sb("raw2", [P, KC, DM])
        W1 = sb("W1", [P, 2, DM], F32R)
        W2 = sb("W2", [P, 2, KC, DM], F32R)
        W3 = sb("W3", [P, KC, P], F32R)
        Fp = sb("Fp", [P, 2, 2, DM], F32R)
        Z = sb("Z", [P, KC, DM])
        Z1 = sb("Z1", [P, 2, 2, KC, DM], F32R)
        Z2 = sb("Z2", [P, 2, KC, DM], F32R)
        Lrow = sb("Lrow", [2, B * T3])
        mlp_in = sem("mlp_in")
        mlp_setup = sem("mlp_setup")
        f_high = sem("f_high")
        f_low = sem("f_low")
        z_sums = sem("z_sums")
        z_gelu = sem("z_gelu")
        z_high = sem("z_high")
        z_low = sem("z_low")
        logit_sums = sem("logit_sums")
        logit_rows = sem("logit_rows")
        logits_in = sem("logits_in")

        block = ctx.enter_context(nc.Block())

        @block.sync
        def _(sp):
            sp.dma_start(raw1[:, :], a["mlp1"]).then_inc(mlp_in, 16)
            sp.dma_start(raw2[:, :, :], a["mlp2"]).then_inc(mlp_in, 16)
            sp.wait_ge(logit_rows, NG)
            for r in range(2):
                sp.dma_start(LG[:, r, :], Lrow[r:r + 1, :].rearrange("p (b t) -> p b t", b=B)).then_inc(logits_in, 16)
            sp.wait_ge(logits_in, 32)

        @block.scalar
        def _(act):
            def gelu(n, at, layer, m):
                act.wait_ge(z_sums, n + 1)
                until(act, z_low, n - 3)
                b = CM1 + m if layer == 1 else CM2 + m
                nc.scalar.activation(Z[:, at, :], bank[at][:, :], ACT.Gelu, bias=cols[:, b:b + 1]).then_inc(z_gelu, 1)

            def logits(i, par):
                act.wait_ge(logit_sums, i * KC + KC)
                nc.scalar.activation(Lrow[:, bass.ds(i * DM, DM)], bank[4 + par][0:2, :], ACT.Copy).then_inc(logit_rows, 1)

            for m in range(KC):
                gelu(m, m, 1, m)

            def step(i, par):
                for j, (layer, m) in enumerate(mlp_order(i)):
                    gelu(mlp_before(i) + j, j % KC, layer, m)
                    if j == 1 and not (isinstance(i, int) and i == 0):
                        logits(i - 1, 1 - par)

            mlp_steps(act, step)
            logits(NG - 1, (NG - 1) % 2)

        @block.vector
        def _(dve):
            dve.wait_ge(mlp_in, 32)
            nc.vector.tensor_copy(W1[:, 0], raw1[:, :]).then_inc(mlp_setup, 1)
            nc.vector.tensor_copy(W2[:, 0], raw2[:, :, :]).then_inc(mlp_setup, 1)
            nc.vector.memset(W3[:, :, :].bitcast(F32), 0.0).then_inc(mlp_setup, 1)
            dve.wait_ge(mlp_setup, 3)
            nc.vector.tensor_tensor(W1[:, 1], raw1[:, :], W1[:, 0].bitcast(F32), ALU.subtract)
            nc.vector.tensor_tensor(W2[:, 1], raw2[:, :, :], W2[:, 0].bitcast(F32), ALU.subtract)
            w3 = cols[:, CW3:CW3 + KC]
            nc.vector.tensor_copy(W3[:, :, 0], w3).then_inc(mlp_setup, 1)
            dve.wait_ge(mlp_setup, 4)
            nc.vector.tensor_tensor(W3[:, :, 1], w3, W3[:, :, 0].bitcast(F32), ALU.subtract).then_inc(mlp_setup, 1)

            def split_f(i, par):
                nc.vector.tensor_copy(Fp[:, par, 0, :], F[:, bass.ds(i * DM, DM)]).then_inc(f_high, 1)
                dve.wait_ge(f_high, i + 1)
                nc.vector.tensor_tensor(Fp[:, par, 1, :], F[:, bass.ds(i * DM, DM)], Fp[:, par, 0, :].bitcast(F32),
                                        ALU.subtract).then_inc(f_low, 1)

            def split_z(n, at, hi, lo):
                dve.wait_ge(z_gelu, n + 1)
                nc.vector.tensor_copy(hi, Z[:, at, :]).then_inc(z_high, 1)
                dve.wait_ge(z_high, n + 1)
                nc.vector.tensor_tensor(lo, Z[:, at, :], hi.bitcast(F32), ALU.subtract).then_inc(z_low, 1)

            split_f(0, 0)
            split_f(1, 1)
            for m in range(KC):
                split_z(m, m, Z1[:, 0, 0, m, :], Z1[:, 0, 1, m, :])

            def step(i, par):
                for j, (layer, m) in enumerate(mlp_order(i)):
                    n = mlp_before(i) + j
                    if layer == 1:
                        split_z(n, j % KC, Z1[:, 1 - par, 0, m, :], Z1[:, 1 - par, 1, m, :])
                    else:
                        until(dve, logit_sums, i * KC + (m - 3))
                        split_z(n, j % KC, Z2[:, 0, m, :], Z2[:, 1, m, :])
                if not isinstance(i, int) or i + 2 < NG:
                    split_f(i + 2, par)

            mlp_steps(dve, step)

        @block.tensor
        def _(pe):
            def chunk(n, at, layer, m, par):
                until(pe, z_gelu, n - 3)
                k = 0
                depth = 1 if layer == 1 else KC
                for kc in range(depth):
                    for w, x in PASSES:
                        if layer == 1:
                            lhs, rhs = W1[:, w, m * P:(m + 1) * P], Fp[:, par, x, :]
                        else:
                            lhs, rhs = W2[:, w, kc, m * P:(m + 1) * P], Z1[:, par, x, kc, :]
                        mm = nc.tensor.matmul(bank[at][:, :], lhs, rhs, start=(k == 0), stop=(k == 3 * depth - 1))
                        k += 1
                mm.then_inc(z_sums, 1)

            def logits(i, par, m):
                pe.wait_ge(z_low, mlp_before(i) + mlp_order(i).index((2, m)) + 1)
                if m == 0:
                    until(pe, logit_rows, i - 1)
                for x in range(2):
                    mm = nc.tensor.matmul(bank[4 + par][:, :], W3[:, m, :], Z2[:, x, m, :], start=(m == 0 and x == 0),
                                          stop=(m == KC - 1 and x == 1))
                mm.then_inc(logit_sums, 1)

            pe.wait_ge(mlp_setup, 5)
            pe.wait_ge(f_low, 1)
            for m in range(KC):
                chunk(m, m, 1, m, 0)

            def step(i, par):
                order = mlp_order(i)
                for j, (layer, m) in enumerate(order):
                    n = mlp_before(i) + j
                    if j == 0:
                        pe.wait_ge(z_low, KC if isinstance(i, int) and i == 0 else i * 8 + 2)
                    if (layer, m) == (1, 0):
                        pe.wait_ge(f_low, i + 2)
                    chunk(n, j % KC, layer, m, par if layer == 2 else 1 - par)
                    if j == 0 and not (isinstance(i, int) and i == 0):
                        logits(i - 1, 1 - par, 3)
                    elif layer == 2 and m > 0:
                        logits(i, par, m - 1)

            mlp_steps(pe, step)
            logits(NG - 1, (NG - 1) % 2, 3)


def pool_attend_experts(nc, a, outer, bank, F, cols, ident, LG, out):
    with ExitStack() as ctx:
        def sb(name, shape, dt=F32):
            return ctx.enter_context(nc.sbuf_tensor(name, shape, dt))

        def sem(name):
            return outer.enter_context(nc.semaphore(name))

        NB = 8 // W
        H = T3
        route = sb("route", [1, B], I32)
        b3 = sb("b3", [B, 1])
        iota = sb("iota", [P, D + 1])
        wattn = sb("wattn", [P, 3, P])
        bv = sb("bv", [P, P])
        bo = sb("bo", [P, D])
        wi = sb("wi", [P, P])
        wo = sb("wo", [P, D])
        wx = sb("wx", [P, 2, NE, EW])
        wsh = sb("wsh", [P, 2, EW])
        imp = sb("imp", [B, T3])
        impn = sb("impn", [B, T3])
        isum = sb("isum", [B, 2])
        ones = sb("ones", [B, T3])
        cs = sb("cs", [B, T3 + 1])
        csT = sb("csT", [P, B, 2])
        Fs = sb("Fs", [P, W, GS, T3])
        zero = sb("zero", [P, 2 * GS])
        E1 = sb("E1", [P, 2 * GS, D + 1])
        E2 = sb("E2", [P, 2 * GS, D + 1])
        E3 = sb("E3", [P, GS, 2, D])
        WM = sb("WM", [P, W, GS, D])
        FT = sb("FT", [P, W, GS, P])
        st = sb("st", [P, W, 3, GS, 6])
        mv = sb("mv", [P, W, 3, GS, 2])
        sd = sb("sd", [P, W, 3, 3, GS])
        Xn = sb("Xn", [P, W, 2, P])
        H0 = sb("H0", [P, W, GS, D])
        Xc = sb("Xc", [P, W, 2, GS, D])
        Xa = sb("Xa", [P, W, 2, GS, D])
        XT = sb("XT", [P, W, 2, 2, P])
        QK = sb("QK", [P, W, 2, 2, P])
        Vt = sb("Vt", [P, W, 2, P])
        mx = sb("mx", [P, W, 2, GS])
        PR = sb("PR", [P, W, GS, P])
        psum_ = sb("prob_sums", [P, W, 2, GS])
        PT = sb("PT", [P, W, GS, P])
        H1 = sb("H1", [P, W, GS, D])
        H1b = sb("H1b", [P, W, GS, D])
        GW = sb("GW", [P, W, GS, 2, EW])
        HF = sb("HF", [P, W, 3, GS, P])
        O = sb("O", [P, W, GS, D])

        tail_in = sem("tail_in")
        experts_sum = sem("experts_sum")
        imp_steps = sem("imp_steps")
        cs_turned = sem("cs_turned")
        csT_ready = sem("csT_ready")
        f_staged = sem("f_staged")
        wm_steps = sem("wm_steps")
        wm_ready = sem("wm_ready")
        f_turned = sem("f_turned")
        ft_ready = sem("ft_ready")
        pooled = sem("pooled")
        stats = [sem(f"stats{i}") for i in range(3)]
        moments = [sem(f"moments{i}") for i in range(3)]
        var_eps = [sem(f"var_eps{i}") for i in range(3)]
        root = [sem(f"root{i}") for i in range(3)]
        invroot = [sem(f"invroot{i}") for i in range(3)]
        centred = [sem(f"centred{i}") for i in range(2)]
        normed = [sem(f"normed{i}") for i in range(3)]
        norm_turned = [sem(f"norm_turned{i}") for i in range(3)]
        h0_ready = sem("h0_ready")
        xt_ready = [sem(f"xt_ready{i}") for i in range(2)]
        qkv_done = sem("qkv_done")
        qk_ready = sem("qk_ready")
        v_ready = sem("v_ready")
        scores_done = sem("scores_done")
        max_done = sem("max_done")
        shift_ready = sem("shift_ready")
        probs_ready = sem("probs_ready")
        inv_sum = sem("inv_sum")
        probs_turned = sem("probs_turned")
        pt_ready = sem("pt_ready")
        attended = sem("attended")
        h1_ready = sem("h1_ready")
        h1b_ready = sem("h1b_ready")
        hidden_done = [sem(f"hidden_done{i}") for i in range(3)]
        hidden_ready = [sem(f"hidden_ready{i}") for i in range(3)]
        experts_in = [sem(f"experts_in{h}") for h in range(W)]
        out_done = sem("out_done")
        o_ready = sem("o_ready")
        stored = sem("stored")

        def groups(eng, steps):
            with eng.Fori(0, NG // W) as k:
                for step in steps:
                    for h in range(W):
                        step(k * W + h, h)

        def bk(h, i):
            return bank[h * NB + i]

        block = ctx.enter_context(nc.Block())

        @block.sync
        def _(sp):
            for dst, name in ((b3[:, :], "b3"), (iota[:, :], "iota"), (wattn[:, :, :], "attn"), (bv[:, :], "bv"),
                              (bo[:, :], "bo"), (wi[:, :], "wi"), (wo[:, :], "wo"), (wx[:, :, :, :], "wr"),
                              (wsh[:, :, :], "ws"), (route[:, :], "route")):
                sp.dma_start(dst, a[name]).then_inc(tail_in, 16)
            sp.wait_ge(experts_sum, 3)

            def fetch(k, h):
                sp.wait_ge(hidden_ready[2], k * W + (h + 1))
                for c in range(GS):
                    e = sp.value_load(route[0:1, bass.ds(k * (W * GS) + (h * GS + c), 1)], min_val=0, max_val=NE - 1)
                    for l in range(2):
                        sp.dma_start(GW[:, h, c, l, :], wx[:, l, bass.ds(e, 1), :].rearrange("p o w -> p (o w)"))\
                            .then_inc(experts_in[h], 16)

            with sp.Fori(0, NG // W) as k:
                for h in range(W):
                    fetch(k, h)
                for h in range(W):
                    sp.wait_ge(o_ready, k * W + (h + 1 + W))
                    dst = out[bass.ds(k * (W * GS) + h * GS, GS)].rearrange("b c d -> c b d")
                    sp.dma_start(dst, O[:, h]).then_inc(stored, 16)
            sp.wait_ge(stored, (NG + W) * 16)

        @block.gpsimd
        def _(pool):
            nc.gpsimd.memset(ones[:, :], 1.0).then_inc(imp_steps, 1)
            nc.gpsimd.memset(cs[:, 0:1], 0.0).then_inc(imp_steps, 1)
            nc.gpsimd.memset(E3[:, :, :, :], 0.0).then_inc(o_ready, W)
            nc.gpsimd.memset(O[:, :, 0, 0:1], 0.0).then_inc(stored, 16 * W)
            nc.gpsimd.memset(Fs[:, :, 0, 0:1], 0.0).then_inc(f_turned, W)
            nc.gpsimd.memset(WM[:, :, 0, 0:1], 0.0).then_inc(pooled, W)
            nc.gpsimd.memset(HF[:, :, 0, 0, 0:1], 0.0).then_inc(hidden_ready[2], W)
            nc.gpsimd.memset(zero[:, :], 0.0).then_inc(wm_steps, 1)
            pool.wait_ge(csT_ready, 2)
            pool.wait_ge(wm_steps, 1)

            def stage(q, h):
                pool.wait_ge(f_turned, q + 1)
                src = F[:, bass.ds(q * DM, DM)].rearrange("p (b t) -> p b t", b=GS)
                nc.gpsimd.tensor_tensor(Fs[:, h], src, zero[:, 0:GS].unsqueeze(2).broadcast_to([P, GS, T3]), ALU.add)\
                    .then_inc(f_staged, 1)

            def weights(q, h):
                c = csT[:, bass.ds(q * GS, GS), :].rearrange("p b s -> p (b s)")
                shape = [P, 2 * GS, D + 1]
                nc.gpsimd.tensor_tensor(E1[:, :, :], c.unsqueeze(2).broadcast_to(shape),
                                        iota[:, :].unsqueeze(1).broadcast_to(shape), ALU.subtract).then_inc(wm_steps, 1)
                waits_behind(pool, csT_ready, 2, (wm_steps, q * 3 + 2))
                nc.gpsimd.tensor_scalar(E2[:, :, :], E1[:, :, :], 0.0, None, ALU.max).then_inc(wm_steps, 1)
                pool.wait_ge(wm_steps, q * 3 + 3)
                nc.gpsimd.tensor_tensor(E3[:, :, :, :].rearrange("p b s n -> p (b s) n"), E2[:, :, 0:D], E2[:, :, 1:D + 1],
                                        ALU.subtract).then_inc(wm_steps, 1)
                pool.wait_ge(wm_steps, q * 3 + 4)
                pool.wait_ge(pooled, q + 1)
                nc.gpsimd.tensor_tensor(WM[:, h], E3[:, :, 0, :], E3[:, :, 1, :], ALU.subtract).then_inc(wm_ready, 1)

            groups(pool, [stage, weights])

        @block.scalar
        def _(act):
            act.wait_ge(imp_steps, 3)
            act.wait_ge(tail_in, 160)
            nc.scalar.activation(imp[:, :], impn[:, :], ACT.Sigmoid, bias=b3[:, :]).then_inc(imp_steps, 1)
            act.wait_ge(cs_turned, 2)
            for s in range(2):
                nc.scalar.activation(csT[:, :, s], bank[s][:, 0:B], ACT.Copy).then_inc(csT_ready, 1)

            def features(q, h):
                act.wait_ge(o_ready, q + 1)
                act.wait_ge(f_turned, q + (1 + W))
                nc.scalar.activation(FT[:, h], bk(h, 0)[:, :].rearrange("p (b c) -> p b c", b=GS), ACT.Copy)\
                    .then_inc(ft_ready, 1)

            def root_of(norm, n):
                def f(q, h):
                    act.wait_ge(var_eps[norm], q + 1)
                    nc.scalar.activation(sd[:, h, norm, 1, 0:n], sd[:, h, norm, 0, 0:n], ACT.Sqrt).then_inc(root[norm], 1)
                return f

            def first(q, h):
                act.wait_ge(norm_turned[0], q + 1)
                nc.scalar.activation(H0[:, h].rearrange("p b n -> p (b n)"), bk(h, 0)[:, 0:GS * D], ACT.Relu,
                                     scale=cols[:, CG4:CG4 + 1], bias=cols[:, CN4:CN4 + 1]).then_inc(h0_ready, 1)

            def turned(i):
                def f(q, h):
                    act.wait_ge(norm_turned[1 + i], q + 1)
                    nc.scalar.activation(XT[:, h, i].rearrange("p a c -> p (a c)"), bk(h, 1 - i)[:, 0:2 * P], ACT.Copy)\
                        .then_inc(xt_ready[i], 1)
                return f

            def queries_keys(q, h):
                act.wait_ge(qkv_done, q + 1)
                for i, b in ((0, CBQ), (1, CBK)):
                    nc.scalar.activation(QK[:, h, i].rearrange("p a c -> p (a c)"), bk(h, 0)[:, i * 2 * P:(i + 1) * 2 * P],
                                         ACT.Identity, bias=cols[:, b:b + 1]).then_inc(qk_ready, 1)

            def probs(q, h):
                act.wait_ge(shift_ready, q + 1)
                for c in range(GS):
                    pair, one = divmod(c, 2)
                    nc.scalar.activation(PR[:, h, c, :], bk(h, one)[:, pair * P:(pair + 1) * P], ACT.Exp, scale=D ** -0.5,
                                         bias=mx[:, h, 1, c:c + 1], accum_out=psum_[:, h, 0, c:c + 1])\
                        .then_inc(probs_ready, 1)

            def probs_t(q, h):
                act.wait_ge(probs_turned, q + 1)
                nc.scalar.activation(PT[:, h], bk(h, 0)[:, :].rearrange("p (b c) -> p b c", b=GS), ACT.Copy)\
                    .then_inc(pt_ready, 1)

            def hidden0(q, h):
                act.wait_ge(hidden_done[0], q + 1)
                for one in range(2):
                    ins = nc.scalar.activation(HF[:, h, 0, 2 * one:2 * one + 2].rearrange("p b c -> p (b c)"),
                                               bk(h, one)[:, 0:2 * P], ACT.Relu, bias=cols[:, CBI:CBI + 1])
                ins.then_inc(hidden_ready[0], 1)

            def hidden(l):
                def f(q, h):
                    act.wait_ge(hidden_done[1 + l], q + 1)
                    for c in range(GS):
                        clip = (c % 2) * 2 + c // 2
                        ins = nc.scalar.activation(HF[:, h, 1 + l, c, :], bk(h, l)[:, c * P:(c + 1) * P], ACT.Relu,
                                                   bias=GW[:, h, clip, l, P:EW])
                    ins.then_inc(hidden_ready[1 + l], 1)
                return f

            groups(act, [features, root_of(0, 2), first, root_of(1, GS), turned(0), queries_keys, probs, probs_t,
                         root_of(2, GS), turned(1), hidden0, hidden(0), hidden(1)])

        @block.vector
        def _(dve):
            nc.vector.tensor_tensor(impn[:, :], LG[:, 0, :], LG[:, 1, :], ALU.add).then_inc(imp_steps, 1)
            dve.wait_ge(imp_steps, 4)
            nc.vector.tensor_scalar(impn[:, :], imp[:, :], TEMP, None, ALU.add).then_inc(imp_steps, 1)
            dve.wait_ge(imp_steps, 5)
            nc.vector.tensor_reduce(isum[:, 0:1], impn[:, :], AX.X, ALU.add).then_inc(imp_steps, 1)
            dve.wait_ge(imp_steps, 6)
            nc.vector.reciprocal(isum[:, 1:2], isum[:, 0:1]).then_inc(imp_steps, 1)
            dve.wait_ge(imp_steps, 7)
            nc.vector.tensor_scalar(imp[:, :], impn[:, :], isum[:, 1:2], float(D), ALU.mult, ALU.mult).then_inc(imp_steps, 1)
            dve.wait_ge(imp_steps, 8)
            nc.vector.tensor_tensor_scan(cs[:, 1:T3 + 1], ones[:, :], imp[:, :], 0.0, ALU.mult, ALU.add)\
                .then_inc(imp_steps, 1)
            dve.wait_ge(tail_in, 160)
            for l in range(2):
                nc.vector.tensor_tensor(wx[:, l], wx[:, l], wsh[:, l, :].unsqueeze(1).broadcast_to([P, NE, EW]), ALU.add)\
                    .then_inc(experts_sum, 1)
            dve.wait_ge(experts_sum, 2)
            mats = wx[:, :, :, 0:P].rearrange("p l e h -> p (l e) h")
            nc.vector.tensor_tensor(mats, mats, ident[:, :].unsqueeze(1).broadcast_to([P, 2 * NE, P]), ALU.add)\
                .then_inc(experts_sum, 1)

            def moments_of(norm, n, src, ready, unbias):
                def stat(q, h):
                    dve.wait_ge(ready, q + (1 + W if norm == 0 else 1))
                    for j in range(n):
                        nc.vector.bn_stats(st[:, h, norm, j, :], src(h, j)).then_inc(stats[norm], 1)

                def aggr(q, h):
                    waits_behind(dve, tail_in, 160, (stats[norm], q * n + n))
                    for j in range(n):
                        nc.vector.bn_aggr(mv[:, h, norm, j, :], st[:, h, norm, j, :]).then_inc(moments[norm], 1)

                def eps(q, h):
                    dve.wait_ge(moments[norm], q * n + n)
                    nc.vector.tensor_scalar(sd[:, h, norm, 0, 0:n], mv[:, h, norm, 0:n, 1], unbias, EPS, ALU.mult, ALU.add)\
                        .then_inc(var_eps[norm], 1)

                def inv(q, h):
                    dve.wait_ge(root[norm], q + 1)
                    nc.vector.reciprocal(sd[:, h, norm, 2, 0:n], sd[:, h, norm, 1, 0:n]).then_inc(invroot[norm], 1)

                return [stat, aggr, eps, inv]

            def norm_pooled(q, h):
                dve.wait_ge(invroot[0], q + 1)
                for j in range(2):
                    nc.vector.tensor_scalar(Xn[:, h, j, :], bk(h, 1)[:, j * P:(j + 1) * P], mv[:, h, 0, j, 0:1],
                                            sd[:, h, 0, 2, j:j + 1], ALU.subtract, ALU.mult).then_inc(normed[0], 1)

            def layer_norm(i, src):
                def centre(q, h):
                    nc.vector.tensor_tensor(Xc[:, h, i], src(h), mv[:, h, 1 + i, :, 0:1].broadcast_to([P, GS, D]),
                                            ALU.subtract).then_inc(centred[i], 1)

                def scale(q, h):
                    dve.wait_ge(invroot[1 + i], q + 1)
                    dve.wait_ge(centred[i], q + 1)
                    nc.vector.tensor_tensor(Xa[:, h, i], Xc[:, h, i],
                                            sd[:, h, 1 + i, 2, :].unsqueeze(2).broadcast_to([P, GS, D]), ALU.mult)\
                        .then_inc(normed[1 + i], 1)
                return centre, scale

            def values(q, h):
                dve.wait_ge(qkv_done, q + 1)
                nc.vector.tensor_tensor(Vt[:, h], bk(h, 1)[:, 0:2 * P].rearrange("p (a c) -> p a c", a=2),
                                        bv[:, :].unsqueeze(1).broadcast_to([P, 2, P]), ALU.add).then_inc(v_ready, 1)

            def maxima(q, h):
                dve.wait_ge(scores_done, q + 1)
                for one in range(2):
                    ins = nc.vector.tensor_reduce(mx[:, h, 0, one:GS:2],
                                                  bk(h, one)[:, 0:2 * P].rearrange("p (b c) -> p b c", b=2), AX.X, ALU.max)
                ins.then_inc(max_done, 1)

            def shift(q, h):
                dve.wait_ge(max_done, q + 1)
                nc.vector.tensor_scalar(mx[:, h, 1, :], mx[:, h, 0, :], -D ** -0.5, None, ALU.mult).then_inc(shift_ready, 1)

            def inv_sums(q, h):
                dve.wait_ge(probs_ready, q * GS + GS)
                nc.vector.reciprocal(psum_[:, h, 1, :], psum_[:, h, 0, :]).then_inc(inv_sum, 1)

            def residual(q, h):
                dve.wait_ge(attended, q + 1)
                dve.wait_ge(inv_sum, q + 1)
                for c in range(GS):
                    ins = nc.vector.scalar_tensor_tensor(H1[:, h, c, :], bk(h, 1)[:, c * D:(c + 1) * D],
                                                         psum_[:, h, 1, c:c + 1], H0[:, h, c, :], ALU.mult, ALU.add)
                ins.then_inc(h1_ready, 1)

            def with_bias(q, h):
                dve.wait_ge(h1_ready, q + 1)
                nc.vector.tensor_tensor(H1b[:, h], H1[:, h], bo[:, :].unsqueeze(1).broadcast_to([P, GS, D]), ALU.add)\
                    .then_inc(h1b_ready, 1)

            def outputs(q, h):
                dve.wait_ge(out_done, q + 1)
                dve.wait_ge(h1b_ready, q + 1)
                dve.wait_ge(stored, (q + 1) * 16)
                nc.vector.tensor_tensor(O[:, h].rearrange("p b d -> p (b d)"), bk(h, 0)[:, 0:GS * D],
                                        H1b[:, h].rearrange("p b d -> p (b d)"), ALU.add).then_inc(o_ready, 1)

            n0 = moments_of(0, 2, lambda h, j: bk(h, 1)[:, j * P:(j + 1) * P], pooled, P / (P - 1))
            n1 = moments_of(1, GS, lambda h, j: H0[:, h, j, :], h0_ready, 1.0)
            n2 = moments_of(2, GS, lambda h, j: H1[:, h, j, :], h1_ready, 1.0)
            c1, s1 = layer_norm(0, lambda h: H0[:, h])
            c2, s2 = layer_norm(1, lambda h: H1[:, h])
            groups(dve, n0 + [norm_pooled] + n1[:3] + [c1, n1[3], s1, values, maxima, shift, inv_sums, residual]
                   + n2[:3] + [c2, n2[3], s2, with_bias, outputs])

        @block.tensor
        def _(pe):
            pe.wait_ge(imp_steps, 9)
            for s in range(2):
                nc.tensor.transpose(bank[s][:, 0:B], cs[:, 1 - s:1 - s + T3], ident[0:B, 0:B]).then_inc(cs_turned, 1)
            pe.wait_ge(csT_ready, 2)
            pe.wait_ge(tail_in, 160)

            def turn_features(q, h):
                pe.wait_ge(o_ready, q + 1)
                pe.wait_ge(f_staged, q + 1)
                for c in range(GS):
                    mm = nc.tensor.transpose(bk(h, 0)[:, c * P:(c + 1) * P], Fs[:, h, c, :], ident[:, :])
                mm.then_inc(f_turned, 1)

            def pool_time(q, h):
                pe.wait_ge(ft_ready, q + 1)
                pe.wait_ge(wm_ready, q + 1)
                for c in range(GS):
                    pair, one = divmod(c, 2)
                    mm = nc.tensor.matmul(bk(h, 1)[one * D:(one + 1) * D, pair * P:(pair + 1) * P], WM[:, h, c, :],
                                          FT[:, h, c, :], start=True, stop=True)
                mm.then_inc(pooled, 1)

            def turn_pooled(q, h):
                pe.wait_ge(normed[0], q * 2 + 2)
                for j in range(2):
                    mm = nc.tensor.transpose(bk(h, 0)[:, j * P:(j + 1) * P], Xn[:, h, j, :], ident[:, :])
                mm.then_inc(norm_turned[0], 1)

            def turn_normed(i):
                def f(q, h):
                    pe.wait_ge(normed[1 + i], q + 1)
                    for j in range(2):
                        src = Xa[:, h, i, 2 * j:2 * j + 2, :].rearrange("p b d -> p (b d)")
                        mm = nc.tensor.transpose(bk(h, 1 - i)[:, j * P:(j + 1) * P], src, ident[:, :])
                    mm.then_inc(norm_turned[1 + i], 1)
                return f

            def qkv(q, h):
                pe.wait_ge(xt_ready[0], q + 1)
                x = XT[:, h, 0].rearrange("p a c -> p (a c)")
                for i in range(2):
                    nc.tensor.matmul(bk(h, 0)[:, i * 2 * P:(i + 1) * 2 * P], wattn[:, i, :], x, start=True, stop=True)
                for j in range(2):
                    mm = nc.tensor.matmul(bk(h, 1)[:, j * P:(j + 1) * P], XT[:, h, 0, j, :], wattn[:, 2, :], start=True,
                                          stop=True)
                mm.then_inc(qkv_done, 1)

            def scores(q, h):
                pe.wait_ge(qk_ready, q * 2 + 2)
                pe.wait_ge(v_ready, q + 1)
                for c in range(GS):
                    pair, one = divmod(c, 2)
                    r = slice(one * D, (one + 1) * D)
                    mm = nc.tensor.matmul(bk(h, one)[:, pair * P:(pair + 1) * P], QK[r, h, 0, pair, :],
                                          QK[r, h, 1, pair, :], start=True, stop=True)
                mm.then_inc(scores_done, 1)

            def turn_probs(q, h):
                pe.wait_ge(probs_ready, q * GS + GS)
                for c in range(GS):
                    mm = nc.tensor.transpose(bk(h, 0)[:, c * P:(c + 1) * P], PR[:, h, c, :], ident[:, :])
                mm.then_inc(probs_turned, 1)

            def attend(q, h):
                pe.wait_ge(pt_ready, q + 1)
                pe.wait_ge(v_ready, q + 1)
                for c in range(GS):
                    pair, one = divmod(c, 2)
                    mm = nc.tensor.matmul(bk(h, 1)[:, c * D:(c + 1) * D], PT[:, h, c, :],
                                          Vt[:, h, pair, one * D:(one + 1) * D], start=True, stop=True)
                mm.then_inc(attended, 1)

            def hidden0(q, h):
                pe.wait_ge(xt_ready[1], q + 1)
                for one in range(2):
                    r = slice(one * D, (one + 1) * D)
                    mm = nc.tensor.matmul(bk(h, one)[:, 0:2 * P], wi[r, :],
                                          XT[r, h, 1].rearrange("p a c -> p (a c)"), start=True, stop=True)
                mm.then_inc(hidden_done[0], 1)

            def hidden(l):
                def f(q, h, k=None):
                    pe.wait_ge(hidden_ready[l], q + 1)
                    for c in range(GS):
                        clip = (c % 2) * 2 + c // 2
                        mm = nc.tensor.matmul(bk(h, l)[:, c * P:(c + 1) * P], GW[:, h, clip, l, 0:P],
                                              HF[:, h, l, c, :], start=True, stop=True)
                    mm.then_inc(hidden_done[1 + l], 1)
                return f

            def outputs(q, h):
                pe.wait_ge(hidden_ready[2], q + (1 + W))
                for c in range(GS):
                    clip = (c % 2) * 2 + c // 2
                    mm = nc.tensor.matmul(bk(h, 0)[:, clip * D:(clip + 1) * D], HF[:, h, 2, c, :], wo[:, :], start=True,
                                          stop=True)
                mm.then_inc(out_done, 1)

            with pe.Fori(0, NG // W) as k:
                for step in [turn_features, pool_time, turn_pooled, turn_normed(0), qkv, scores, turn_probs, attend,
                             turn_normed(1), hidden0, "experts", hidden(0), hidden(1), outputs]:
                    for h in range(W):
                        if step == "experts":
                            pe.wait_ge(experts_in[h], k * (2 * GS * 16) + 2 * GS * 16)
                        else:
                            step(k * W + h, h)


def bank_of(tile):
    return 2 if tile[0] == 3 else tile[1] % 2


def left_before(g, n):
    bank = bank_of(tiles_of(g, conv_tiles, FULL)[n])
    for back in range(4):
        tiles = FULL if not isinstance(g, int) else conv_tiles(g - back) if g >= back else []
        for m in reversed(range(n if back == 0 else len(tiles))):
            if bank_of(tiles[m]) == bank:
                return convs_before(g - back) + (m + 1)
    return 0


def late(g):
    return [t for t in tiles_of(g, conv_tiles, FULL) if t[0] != 1] if not isinstance(g, int) or g >= 0 else []


def row_of(tile):
    return {1: ROW1, 2: ROW2, 3: ROW3}[tile[0]] + tile[1]


def summed_before(g, n):
    return convs_before(g) + max(n - RING + 1, 0)


def norms_par(g, par, n):
    return (norms_before(g) + n) % 2 if isinstance(g, int) else (NTILE * par + norms_before(3) - NTILE * 3 + n) % 2


def splits_before(g):
    if isinstance(g, int):
        return sum(len([t for t in norm_tiles(i) if t[0] != 3]) for i in range(g))
    return g * 6 + (10 - 18)


def patches(xs, i, d):
    w = NB8 * STR0
    first = xs[:, bass.ds(i * (2 * w) + d * w, w + STR0)]
    return bass.AP(first.tensor, first.offset, [(XW, P), (STR0, NB8), (1, K0)])


def kernel(**x):
    import numpy as np
    import concourse.bacc as bacc
    from concourse.bass_utils import run_bass_kernel_spmd

    x = {k.replace("L0_", ""): np.asarray(v) for k, v in x.items()}
    f = np.float32

    def tap_major(w):
        return w.transpose(1, 2, 0)

    rows = np.zeros((K0ROWS, 2, P), f)
    kind = np.zeros((K0ROWS, 4), f)
    for q in range(3):
        for part in range(3):
            r = ROWS * q + NTAP * part
            rows[r:r + K0, 0] = x["tok_conv0_w"][:, 0, :].T
            rows[r + K0, 0] = x["tok_conv0_b"]
            rows[r:r + NTAP, 1] = x["tok_n0_w"]
            kind[r:r + NTAP, 0] = 1
        rows[ROWS * q + 3 * NTAP, 0] = x["tok_n0_b"]
        rows[ROWS * q + 3 * NTAP, 1] = 1
        kind[ROWS * q:ROWS * (q + 1), 1 + q] = 1
    sel = np.zeros((96, NTILE, P), f)
    for j in range(NTILE):
        sel[[j, 32 + j, 64 + j], j] = 1
    two = lambda v: np.concatenate([v, v])
    arrays = {
        "xpad": np.pad(x["x"][:, 0, :], ((0, 0), (3, 3)), mode="reflect"),
        "c0": np.concatenate([x["tok_conv0_w"][:, 0, :], x["tok_conv0_b"][:, None]], 1),
        "w0": rows, "w0k": kind, "selB": sel, "ident": np.eye(P, dtype=f),
        "wconv": np.concatenate([tap_major(x[f"tok_conv{i}_w"]) for i in (1, 2, 3)], 1),
        "cols": np.stack([x[f"tok_conv{i}_b"] for i in (1, 2, 3)] + [x[f"tok_n{i}_w"] for i in (1, 2, 3)]
                         + [x[f"tok_n{i}_b"] for i in (1, 2, 3)] + [x["tok_n4_w"], x["tok_n4_b"]]
                         + list(x["tok_mlp_b1"].reshape(KC, P)) + list(x["tok_mlp_b2"].reshape(KC, P))
                         + list(x["tok_mlp_w3"].reshape(KC, P)) + [two(x["attn_bq"]), two(x["attn_bk"]), x["ffn_bi"]], 1),
    }
    def pair(m):
        z = np.zeros((2, D, 2, D), f)
        z[0, :, 0] = z[1, :, 1] = m
        return z.reshape(P, P)

    arrays.update({
        "mlp1": x["tok_mlp_w1"], "mlp2": x["tok_mlp_w2"].reshape(KC, P, DM).transpose(1, 0, 2),
        "b3": np.repeat(x["tok_mlp_b3"][:, None], B, 0),
        "iota": np.tile(np.append(np.arange(D), FAR).astype(f), (P, 1)),
        "attn": np.stack([pair(x[f"attn_W{c}"]) for c in "qkv"], 1),
        "bv": np.tile(two(x["attn_bv"]), (P, 1)), "bo": np.tile(x["ffn_bo"], (P, 1)),
        "wi": two(x["ffn_Wi"].T), "wo": x["ffn_Wo"].T,
        "wr": np.concatenate([x["ffn_Wr"].transpose(3, 0, 1, 2), x["ffn_br"].transpose(2, 0, 1)[..., None]], 3),
        "ws": np.concatenate([x["ffn_Ws"].transpose(3, 0, 1, 2), x["ffn_bs"].transpose(2, 0, 1)[..., None]], 3)[:, :, 0],
        "route": x["ffn_route_id"][None, :],
    })
    arrays = {k: np.ascontiguousarray(v) for k, v in arrays.items()}
    nc = bacc.Bacc("TRN2", target_bir_lowering=False, num_devices=1)
    aps = {k: nc.dram_tensor("in_" + k, v.shape, mybir.dt.from_np(v.dtype), kind="ExternalInput").ap() for k, v in arrays.items()}
    out = nc.dram_tensor("out", (B, P, D), F32, kind="ExternalOutput").ap()
    audio_kernel(nc, aps, out)
    r = run_bass_kernel_spmd(nc, [{"in_" + k: v for k, v in arrays.items()}], core_ids=[0])
    return r.results[0]["out"]
```

```python
from contextlib import ExitStack

import concourse.bass as bass
from concourse import mybir

F32 = mybir.dt.float32
F32R = mybir.dt.float32r
BF16 = mybir.dt.bfloat16
I32 = mybir.dt.int32
ALU = mybir.AluOpType
ACT = mybir.ActivationFunctionType
AX = mybir.AxisListType

P = 128
B = 64
L = 10240
EPS = 1e-5
TEMP = 1e-5
T0, T1, T2, T3 = 2048, 512, 256, 128
K0, STR0 = 10, 5
LPAD = L + 6
GS = 4
NG = B // GS
HALF = T0 // 2
XW = STR0 * (HALF - 1) + K0
NTAP = K0 + 1
ROWS = 36
K0ROWS = 3 * ROWS
BLK = 16
BW = STR0 * (BLK - 1) + K0
SBLK = 2
STEP_T = SBLK * BLK
NSTEP = HALF // STEP_T
ONES = BW // 32 * 32
DM = 512
KC = DM // P
NE = 16
EW = P + 1
D = 64

CB, CG, CN = 0, 3, 6
CG4, CN4, CM1, CM2, CW3, CBQ, CBK, CBI = 9, 10, 11, 15, 19, 23, 24, 25
NCOLS = 26
FAR = 1e30
W = 4

ROW1, ROW2, ROW3 = 0, 4, 6
NTILE = 7


def conv_tiles(g):
    return ([(1, s) for s in range(4)] if g < NG else []) + ([(3, 0)] if 0 <= g - 2 < NG else []) + \
        ([(2, 0), (2, 1)] if 0 <= g - 1 < NG else [])


def norm_tiles(g):
    return ([(2, 0), (2, 1)] if 0 <= g - 2 < NG else []) + \
        ([(1, s) for s in range(4)] if 0 <= g - 1 < NG else []) + ([(3, 0)] if 0 <= g - 3 < NG else [])


RING = 4
NRING = 3
LOOP_FROM, LOOP_TO = 3, 15
LAST = NG + 2
FULL = conv_tiles(LOOP_FROM)
FULLN = norm_tiles(LOOP_FROM)


def before(g, tiles, full_from):
    if isinstance(g, int):
        return sum(len(tiles(i)) for i in range(g))
    return g * NTILE + (sum(len(tiles(i)) for i in range(full_from)) - NTILE * full_from)


def convs_before(g):
    return before(g, conv_tiles, 2)


def norms_before(g):
    return before(g, norm_tiles, 3)


def until(eng, sem, count):
    if isinstance(count, int) and count <= 0:
        return
    eng.wait_ge(sem, count)


def waits_behind(eng, sem, count, *others):
    others = [(s, c if isinstance(c, int) else eng.compute_val(c)) for s, c in others]
    eng.wait_ge(sem, count)
    for s, c in others:
        until(eng, s, c)


def each_iteration(eng, step, before_last=None):
    for g in range(LOOP_FROM):
        step(g, g % 2)
    with eng.Fori(0, (LOOP_TO - LOOP_FROM) // 2) as i:
        for d in range(2):
            step(i * 2 + (LOOP_FROM + d), (LOOP_FROM + d) % 2)
    for g in range(LOOP_TO, LAST + 1):
        if g == LAST and before_last:
            before_last()
        step(g, g % 2)


CHUNKS = 4
CH = HALF // CHUNKS
SR = 6
PAIRS = NSTEP // 2 // CHUNKS


def statistics(eng, pair, begin, tap, ahead=0):
    pair(0)
    with eng.Fori(1, PAIRS + ahead) as i:
        pair(i)
    for c in range(CHUNKS):
        begin(c)
        done = 0
        if c + 1 < CHUNKS:
            for j in range(PAIRS):
                if (c + 1) * PAIRS + j + ahead < NSTEP // 2:
                    pair((c + 1) * PAIRS + j + ahead)
                due = NTAP * (j + 1) // PAIRS
                for k in range(done, due):
                    tap(c, k)
                done = due
        for k in range(done, NTAP):
            tap(c, k)


def has(g, what):
    if not isinstance(g, int):
        return True
    return {"conv1": g < NG, "conv2": 0 <= g - 1 < NG, "conv3": 0 <= g - 2 < NG, "next": g + 1 < NG,
            "batch": 0 <= g - 1 and g <= LAST}[what]


def tiles_of(g, tiles, full):
    return tiles(g) if isinstance(g, int) else full


def audio_kernel(nc, a, out):
    with ExitStack() as ctx:
        F = ctx.enter_context(nc.sbuf_tensor("F", [P, B * T3], F32))
        cols = ctx.enter_context(nc.sbuf_tensor("cols", [P, NCOLS], F32))
        ident = ctx.enter_context(nc.sbuf_tensor("ident", [P, P], F32))
        LG = ctx.enter_context(nc.sbuf_tensor("LG", [B, 2, T3], F32))
        b3 = ctx.enter_context(nc.sbuf_tensor("b3", [B, 1], F32))
        iota = ctx.enter_context(nc.sbuf_tensor("iota", [P, D + 1], F32))
        csT = ctx.enter_context(nc.sbuf_tensor("csT", [P, B, 2], F32))
        WM = ctx.enter_context(nc.sbuf_tensor("WM", [P, W, GS, D], F32))
        wm_ready = ctx.enter_context(nc.semaphore("wm_ready"))
        halves = [Half(nc, ctx, i) for i in range(2)]
        shared = (LG, b3, iota, csT, WM, wm_ready, halves)
        bank = [ctx.enter_context(nc.psum_tensor(f"bank{i}", [P, 512], F32)) for i in range(8)]
        with ExitStack() as mlp:
            weights = [mlp.enter_context(nc.sbuf_tensor(*x)) for x in
                       (("R", [P, 4, T0], BF16), ("W1", [P, 2, DM], F32R), ("W3", [P, KC, P], F32R))]
            convolutions(nc, a, ctx, bank, F, cols, ident, weights)
            importance_mlp(nc, a, ctx, bank, F, cols, ident, shared, weights)
        pool_attend_experts(nc, a, ctx, bank, F, cols, ident, shared, out)


def convolutions(nc, a, outer, bank, F, cols, ident, mlp_weights):
    R, W1, W3 = mlp_weights
    raw1, raw2 = raw_weights(R)
    with ExitStack() as ctx:
        def sb(name, shape, dt=F32, at=None):
            return (at or ctx).enter_context(nc.sbuf_tensor(name, shape, dt))

        def sem(name):
            return outer.enter_context(nc.semaphore(name))

        convs = ctx.enter_context(ExitStack())
        wc = sb("wc", [P, 2, 16, P], F32R, convs)
        W0 = sb("W0", [K0ROWS, P], BF16, convs)
        selV = sb("selV", [P, NTILE, P], F32R, convs)
        selB = sb("selB", [96, NTILE, P], BF16, convs)
        bc = sb("bc", [P, 3], F32, convs)
        RS = sb("RS", [96, T1], BF16, convs)
        vs = sb("vs", [NTILE + 1, T1], F32, convs)
        iv = sb("iv", [NTILE + 1, T1], F32, convs)
        rs = sb("rs", [NTILE + 1, T1], F32, convs)
        rr = sb("rr", [NTILE + 1, T1], F32, convs)
        mt = sb("mt", [NTILE + 1, T1], BF16, convs)

        with ExitStack() as st:
            xs = sb("xs", [P, XW], F32, st)
            xst = sb("xst", [P, 2, STEP_T * STR0 + 5], F32, st)
            XT0 = sb("XT0", [ONES + 32, 2, SBLK * P], F32, st)
            TG = sb("TG", [BW + 1, BLK, NTAP], F32, st)
            Gs = sb("Gs", [NTAP, NTAP], F32, st)
            c0 = sb("c0", [P, NTAP], F32, st)
            c0c = sb("c0c", [P, NTAP], F32, st)
            onesC = sb("onesC", [P, P], F32, st)
            prod = sb("prod", [P, 2, STEP_T * K0], F32, st)
            red = sb("red", [P, 2, STEP_T], F32, st)
            var0 = sb("var0", [P, HALF], F32, st)
            rstd0 = sb("rstd0", [P, HALF], F32, st)
            ps = sb("ps", [P, 3, CH], F32, st)
            rt = sb("rt", [P, 2, CH], F32, st)
            S = sb("S", [P, SR, 3, CH], BF16, st)
            ones_bf = sb("ones_bf", [P, HALF], BF16, st)
            wraw = sb("wraw", [P, 16, P], F32, st)
            wmean = sb("wmean", [P, 16], F32, st)
            w0 = sb("w0", [K0ROWS, 2, P], F32, st)
            w0k = sb("w0k", [K0ROWS, 4], F32, st)
            w0m = sb("w0m", [K0ROWS, 2], F32, st)
            w0t = sb("w0t", [K0ROWS, 2, P], F32, st)
            w0p = sb("w0p", [K0ROWS, 3, P], BF16, st)
            selBf = sb("selBf", [96, NTILE, P], F32, st)

        with ExitStack() as cv:
            A0 = sb("A0", [P, 2, 2, 4, T1 + 2], F32R, cv)
            A1 = sb("A1", [P, 2, 2, GS, T2 + 2], F32R, cv)
            A2 = sb("A2", [P, 2, 2, GS, T3 + 2], F32R, cv)
            Y = sb("Y", [P, 2, NTILE, T1], F32, cv)
            sqh = sb("sqh", [P, RING, T1], F32R, cv)
            sql = sb("sql", [P, RING, T1], F32R, cv)
            sqf = sb("sqf", [P, T1], F32, cv)
            N = sb("N", [P, NRING, T1], F32, cv)
            AF = sb("AF", [P, NRING, T1], F32, cv)
        scratch = nc.dram_tensor("scratch", (ROWS, B * T0), BF16, kind="Internal").ap()

        P0, CONV, V, RB = bank[0:2], (bank[2], bank[3], bank[7]), bank[4], bank[5:7]

        x_in = sem("x_in")
        c0_in = sem("c0_in")
        w_in = sem("w_in")
        const_in = sem("const_in")
        ones_set = sem("ones_set")
        tg_clear = sem("tg_clear")
        gram_steps = sem("gram_steps")
        gram_act = sem("gram_act")
        tg_in = sem("tg_in")
        staged = sem("staged")
        turned = sem("turned")
        xt0_ready = sem("xt0_ready")
        quad_done = sem("quad_done")
        prod_done = sem("prod_done")
        red_done = sem("red_done")
        var_ready = sem("var_ready")
        inv_ready = sem("inv_ready")
        rstd_ready = sem("rstd_ready")
        scaled = sem("scaled")
        high_ready = sem("high_ready")
        rest_ready = sem("rest_ready")
        mid_ready = sem("mid_ready")
        low_ready = sem("low_ready")
        rows_out = [sem(f"rows_out{i}") for i in range(SR)]
        ones_out = sem("ones_out")
        wsetup = sem("wsetup")
        mlp_in = sem("mlp_in")
        psetup = sem("psetup")
        r_in = [sem(f"r_in{i}") for i in range(4)]
        conv0_done = sem("conv0_done")
        h0_high = sem("h0_high")
        h0_low = sem("h0_low")
        h0_pads = sem("h0_pads")
        conv1_done = sem("conv1_done")
        conv2_done = sem("conv2_done")
        conv3_done = sem("conv3_done")
        y_done = sem("y_done")
        sq_done = sem("sq_done")
        sql_done = sem("sql_done")
        var_done = sem("var_done")
        vs_done = sem("vs_done")
        iv_done = sem("iv_done")
        rs_done = sem("rs_done")
        parts_done = sem("parts_done")
        spread = sem("spread")
        n_done = sem("n_done")
        relu_done = sem("relu_done")
        ah_done = sem("ah_done")
        al_done = sem("al_done")
        a_pads = sem("a_pads")

        def phases(c, k):
            o = STR0 * CH * c + k
            return xs[:, o:o + STR0 * (CH - 1) + 1:STR0].rearrange("p (q r) -> p r q", r=4)

        block = ctx.enter_context(nc.Block())

        @block.sync
        def _(sp):
            sp.dma_start(wraw[:, :, :], a["wconv"]).then_inc(w_in, 16)
            x = a["xpad"]
            halves = bass.AP(x.tensor, x.offset, [(LPAD, B), (STR0 * HALF, 2), (1, XW)])
            sp.dma_start(xs[:, :], halves).then_inc(x_in, 16)
            sp.wait_ge(tg_clear, 1)
            sp.wait_ge(gram_act, 1)
            for t in range(0, BLK, 2):
                sp.dma_start(TG[STR0 * t:STR0 * t + K0, t, :], Gs[0:K0, :]).then_inc(tg_in, 16)
            bias_row = Gs[K0:K0 + 1, :].unsqueeze(1).broadcast_to([1, BLK, NTAP])
            sp.dma_start(TG[BW:BW + 1, :, :], bias_row).then_inc(tg_in, 16)
            sp.wait_ge(ones_set, 2)
            for i in range(3 * NTAP, ROWS):
                sp.dma_start(scratch[i, :].rearrange("(p t) -> p t", p=P), ones_bf[:, :]).then_inc(ones_out, 16)
            for m in range(CHUNKS * NTAP):
                c, k = divmod(m, NTAP)
                sp.wait_ge(low_ready, m + 1)
                dst = scratch[k:3 * NTAP:NTAP, :].rearrange("i (p c t) -> c p i t", p=P, c=CHUNKS)[c]
                sp.dma_start(dst, S[:, m % SR, :, :]).then_inc(rows_out[m % SR], 16)
            sp.wait_ge(ones_out, 16 * (ROWS - 3 * NTAP))
            for i in range(SR):
                sp.wait_ge(rows_out[i], 16 * len(range(i, CHUNKS * NTAP, SR)))

            def load(clip, slot):
                for q in range(3):
                    src = scratch[:, bass.ds(clip * T0, T0)]
                    sp.dma_start(R[ROWS * q:ROWS * (q + 1), slot, :], src).then_inc(r_in[slot], 16)

            for s in range(4):
                load(s, s)
            with sp.Fori(0, NG - 1) as i:
                for s in range(4):
                    sp.wait_ge(conv0_done, i * 16 + (4 * s + 4))
                    load(i * 4 + (4 + s), s)
            sp.wait_ge(conv0_done, B * 4)
            for dst, name in ((raw1, "mlp1"), (raw2, "mlp2")):
                sp.dma_start(dst, a[name]).then_inc(mlp_in, 16)

        @block.gpsimd
        def _(pool):
            pool.wait_ge(x_in, 16)
            W = STEP_T * STR0

            def stage(i):
                for d in range(2):
                    waits_behind(pool, x_in, 16, (turned, i * 2 + (d - 1)))
                    nc.gpsimd.tensor_copy(xst[:, d, 0:W + 5], xs[:, bass.ds(i * (2 * W) + d * W, W + 5)]).then_inc(staged, 1)

            def low(c, k):
                m = c * NTAP + k
                pool.wait_ge(mid_ready, m + 1)
                nc.gpsimd.tensor_tensor(S[:, m % SR, 2, :], rt[:, m % 2, :], S[:, m % SR, 1, :], ALU.subtract)\
                    .then_inc(low_ready, 1)

            statistics(pool, stage, lambda c: None, low, 2)

            def borders0(clip, slot):
                waits_behind(pool, x_in, 16, (h0_low, clip * 4 + 4), (conv1_done, clip - 1))
                t = A0[:, slot]
                for (r, c), (r1, c1) in (((2, 0), (2, 1)), ((3, 0), (1, 1)), ((0, T1 + 1), (2, T1)), ((1, T1 + 1), (1, T1))):
                    nc.gpsimd.tensor_copy(t[:, :, r, c:c + 1], t[:, :, r1, c1:c1 + 1].bitcast(F32))\
                        .then_inc(h0_pads, 1)

            def square(g, par, n, tile):
                at = convs_before(g) + n
                slot = n % RING
                y = Y[:, par, row_of(tile), :]
                pool.wait_ge(y_done, at + 1)
                until(pool, sql_done, at)
                nc.gpsimd.tensor_tensor(sqf[:, :], y, y, ALU.mult).then_inc(sq_done, 1)
                pool.wait_ge(sq_done, at + 1)
                until(pool, var_done, summed_before(g, n))
                nc.gpsimd.tensor_tensor(sql[:, slot, :], sqf[:, :], sqh[:, slot, :].bitcast(F32), ALU.subtract)\
                    .then_inc(sql_done, 1)

            def borders(g, n, tile):
                level, s = tile
                if level == 3:
                    return
                waits_behind(pool, x_in, 16, (al_done, splits_before(g) + n + 1))
                buf, w, c = (A1, T2, slice(s, s + 1)) if level == 1 else (A2, T3, slice(2 * s, 2 * s + 2))
                nc.gpsimd.tensor_copy(buf[:, :, 1, c, 0:1], buf[:, :, 1, c, 1:2].bitcast(F32)).then_inc(a_pads, 1)
                nc.gpsimd.tensor_copy(buf[:, :, 0, c, w + 1:w + 2], buf[:, :, 0, c, w:w + 1].bitcast(F32))\
                    .then_inc(a_pads, 1)

            borders0(0, 0)

            def step(g, par):
                tiles = tiles_of(g, conv_tiles, FULL)
                norms = tiles_of(g, norm_tiles, FULLN)
                if has(g, "conv1"):
                    for s in range(3):
                        borders0(g * 4 + (s + 1), (s + 1) % 2)
                        square(g, par, s, tiles[s])
                first = 3 if has(g, "conv1") else 0
                squares = [lambda n=n: square(g, par, n, tiles[n]) for n in range(first, len(tiles))]
                edges = [lambda n=n: borders(g, n, norms[n]) for n in range(len(norms))]
                for f in edges[:2]:
                    f()
                if has(g, "conv1"):
                    order = edges[2:4] + squares[:1] + edges[4:]
                    if has(g, "next"):
                        order += [lambda: borders0(g * 4 + 4, 0)]
                    order += squares[1:]
                else:
                    order = edges[2:] + squares
                for work in order:
                    work()

            each_iteration(pool, step)

        @block.scalar
        def _(act):
            act.dma_start(c0[:, :], a["c0"]).then_inc(c0_in, 16)
            for dst, name in ((w0[:, :, :], "w0"), (w0k[:, :], "w0k"), (selBf[:, :, :], "selB"), (cols[:, :], "cols"),
                              (ident[:, :], "ident")):
                act.dma_start(dst, a[name]).then_inc(const_in, 16)
            act.wait_ge(gram_steps, 3)
            nc.scalar.activation(Gs[:, :], bank[5][0:NTAP, 0:NTAP], ACT.Copy).then_inc(gram_act, 1)
            act.wait_ge(tg_clear, 1)
            act.wait_ge(gram_act, 1)
            for t in range(1, BLK, 2):
                act.dma_start(TG[STR0 * t:STR0 * t + K0, t, :], Gs[0:K0, :]).then_inc(tg_in, 16)

            def turned_out(i):
                for d in range(2):
                    act.wait_ge(turned, i * 2 + (d + 1))
                    until(act, quad_done, i * 2 + (d - 1))
                    nc.scalar.activation(XT0[0:BW, d, :], bank[d][0:BW, 0:SBLK * P], ACT.Copy).then_inc(xt0_ready, 1)

            def high(m):
                act.wait_ge(scaled, m + 1)
                if m >= SR:
                    act.wait_ge(rows_out[m % SR], 16 * (m // SR))
                nc.scalar.activation(S[:, m % SR, 0, :], ps[:, m % 3, :], ACT.Copy).then_inc(high_ready, 1)

            def roots(c):
                act.wait_ge(inv_ready, c + 1)
                part = slice(c * CH, (c + 1) * CH)
                nc.scalar.activation(rstd0[:, part], var0[:, part], ACT.Sqrt).then_inc(rstd_ready, 1)
                high(c * NTAP)

            def middle(c, k):
                m = c * NTAP + k
                if k + 1 < NTAP:
                    high(m + 1)
                act.wait_ge(rest_ready, m + 1)
                nc.scalar.activation(S[:, m % SR, 1, :], rt[:, m % 2, :], ACT.Copy).then_inc(mid_ready, 1)

            statistics(act, turned_out, roots, middle, 1)

            def relu0(clip, slot, r):
                act.wait_ge(conv0_done, clip * 4 + (r + 1))
                until(act, conv1_done, clip - 1)
                nc.scalar.activation(A0[:, slot, 0, r, 1:T1 + 1], P0[r % 2][:, :], ACT.Relu).then_inc(h0_high, 1)

            def centre(g, par, n, tile):
                level, s = tile
                at = convs_before(g) + n
                slot = n % RING
                src = CONV[bank_of(tile)]
                done, count = {1: (conv1_done, g * 4 + (s + 1)), 2: (conv2_done, (g - 1) * 2 + (s + 1)),
                               3: (conv3_done, g - 1)}[level]
                act.wait_ge(done, count)
                until(act, n_done, norms_before(g))
                bias = bc[:, level - 1:level]
                nc.scalar.activation(Y[:, par, row_of(tile), :], src[:, :], ACT.Identity, bias=bias)
                until(act, var_done, summed_before(g, n))
                nc.scalar.activation(sqh[:, slot, :], src[:, :], ACT.Square, bias=bias).then_inc(y_done, 1)

            def relu(g, par, n, tile):
                level, s = tile
                at = norms_before(g) + n
                slot = n % NRING
                act.wait_ge(n_done, at + 1)
                src = N[:, slot, :]
                if level == 3:
                    dst = F[:, bass.ds((g - 3) * (GS * T3), GS * T3)]
                elif level == 1:
                    src = src.rearrange("p (q r) -> p r q", r=2)
                    dst = AF[:, slot, :].rearrange("p (r q) -> p r q", r=2)
                else:
                    src = src.rearrange("p (s q r) -> p r s q", r=2, s=2)
                    dst = AF[:, slot, :].rearrange("p (r s q) -> p r s q", r=2, s=2)
                if level != 3:
                    until(act, al_done, splits_before(g) + max(n - NRING + 1, 0))
                nc.scalar.activation(dst, src, ACT.Relu, scale=cols[:, CG + level - 1:CG + level],
                                     bias=cols[:, CN + level - 1:CN + level]).then_inc(relu_done, 1)

            act.wait_ge(psetup, 1)
            for r in range(4):
                relu0(0, 0, r)

            def step(g, par):
                tiles = tiles_of(g, conv_tiles, FULL)
                norms = tiles_of(g, norm_tiles, FULLN)
                conv1 = has(g, "conv1")
                if conv1:
                    for s in range(2):
                        for r in range(4):
                            relu0(g * 4 + (s + 1), (s + 1) % 2, r)
                        centre(g, par, s, tiles[s])
                if has(g, "batch"):
                    act.wait_ge(iv_done, g * 4)
                    until(act, parts_done, g * 5 - 8)
                    nc.scalar.activation(rs[:, :], iv[:, :], ACT.Sqrt).then_inc(rs_done, 1)
                if conv1:
                    for r in range(4):
                        relu0(g * 4 + 3, 1, r)
                    centre(g, par, 2, tiles[2])
                relus = [lambda n=n: relu(g, par, n, norms[n]) for n in range(len(norms))]
                centres = [lambda n=n: centre(g, par, n, tiles[n]) for n in range(3 if conv1 else 0, len(tiles))]
                ahead = [lambda r=r: relu0(g * 4 + 4, 0, r) for r in range(4)] if conv1 and has(g, "next") else []
                if conv1:
                    order = relus[:4] + centres[:1] + ahead[:1] + relus[4:5] + ahead[1:2] + relus[5:6] + centres[1:2] \
                        + relus[6:] + ahead[2:] + centres[2:]
                else:
                    order = relus + centres
                for work in order:
                    work()

            each_iteration(act, step)

        @block.vector
        def _(dve):
            count = [0]

            def chain(ins):
                count[0] += 1
                ins.then_inc(wsetup, 1)
                dve.wait_ge(wsetup, count[0])

            nc.vector.memset(onesC[:, :], 1.0 / P).then_inc(ones_set, 1)
            nc.vector.memset(ones_bf[:, :], 1.0).then_inc(ones_set, 1)
            nc.vector.memset(XT0[ONES:ONES + 32, :, :], 1.0)
            nc.vector.memset(TG[:, :, :], 0.0).then_inc(tg_clear, 1)
            dve.wait_ge(c0_in, 16)
            dve.wait_ge(gram_steps, 1)
            nc.vector.tensor_tensor(c0c[:, :], c0[:, :], bank[4][:, 0:NTAP], ALU.subtract).then_inc(gram_steps, 1)
            dve.wait_ge(w_in, 16)
            chain(nc.vector.tensor_reduce(wmean[:, :], wraw[:, :, :], AX.X, ALU.add))
            chain(nc.vector.tensor_scalar(wmean[:, :], wmean[:, :], 1.0 / P, None, ALU.mult))
            mean = wmean[:, :].unsqueeze(2).broadcast_to([P, 16, P])
            chain(nc.vector.tensor_tensor(wraw[:, :, :], wraw[:, :, :], mean, ALU.subtract))
            chain(nc.vector.tensor_copy(wc[:, 0], wraw[:, :, :]))
            nc.vector.tensor_tensor(wc[:, 1], wraw[:, :, :], wc[:, 0].bitcast(F32), ALU.subtract)
            dve.wait_ge(const_in, 80)
            chain(nc.vector.tensor_reduce(w0m[:, 0:1], w0[:, 0, :], AX.X, ALU.add))
            chain(nc.vector.tensor_scalar(w0m[:, 1:2], w0m[:, 0:1], w0k[:, 0:1], 1.0 / P, ALU.mult, ALU.mult))
            chain(nc.vector.tensor_scalar(w0t[:, 0, :], w0[:, 0, :], w0m[:, 1:2], None, ALU.subtract))
            chain(nc.vector.tensor_tensor(w0t[:, 0, :], w0t[:, 0, :], w0[:, 1, :], ALU.mult))
            chain(nc.vector.tensor_copy(w0p[:, 0, :], w0t[:, 0, :]))
            chain(nc.vector.tensor_tensor(w0t[:, 1, :], w0t[:, 0, :], w0p[:, 0, :], ALU.subtract))
            chain(nc.vector.tensor_copy(w0p[:, 1, :], w0t[:, 1, :]))
            chain(nc.vector.tensor_tensor(w0p[:, 2, :], w0t[:, 1, :], w0p[:, 1, :], ALU.subtract))
            chain(nc.vector.tensor_scalar(w0t[:, 0, :], w0p[:, 0, :], w0k[:, 1:2], None, ALU.mult))
            chain(nc.vector.scalar_tensor_tensor(w0t[:, 1, :], w0p[:, 1, :], w0k[:, 2:3], w0t[:, 0, :], ALU.mult, ALU.add))
            chain(nc.vector.scalar_tensor_tensor(W0[:, :], w0p[:, 2, :], w0k[:, 3:4], w0t[:, 1, :], ALU.mult, ALU.add))
            nc.vector.tensor_copy(selB[:, :, :], selBf[:, :, :])
            chain(nc.vector.memset(selV[:, :, :].bitcast(F32), 0.0))
            for j in range(NTILE):
                nc.vector.memset(selV[:, j, j:j + 1].bitcast(F32), 1.0)
            nc.vector.memset(RS[:, :], 0.0)
            dve.wait_ge(gram_steps, 4)
            nc.vector.tensor_tensor(bc[:, :], cols[:, CB:CB + 3], bank[4][:, 16:19], ALU.subtract).then_inc(psetup, 1)

            def quadratic(i):
                for d in range(2):
                    dve.wait_ge(quad_done, i * 2 + (d + 1))
                    z = bank[2 + d][:, 0:STEP_T * NTAP].rearrange("p (t k) -> p t k", k=NTAP)
                    nc.vector.tensor_tensor(prod[:, d, :].rearrange("p (t k) -> p t k", k=K0), z[:, :, 0:K0],
                                            patches(xs, i, d), ALU.mult).then_inc(prod_done, 1)
                    dve.wait_ge(prod_done, i * 2 + (d + 1))
                    nc.vector.tensor_reduce(red[:, d, :], prod[:, d, :].rearrange("p (t k) -> p t k", k=K0), AX.X,
                                            ALU.add).then_inc(red_done, 1)
                    dve.wait_ge(red_done, i * 2 + (d + 1))
                    nc.vector.tensor_tensor(var0[:, bass.ds(i * (2 * STEP_T) + d * STEP_T, STEP_T)], red[:, d, :],
                                            z[:, :, K0], ALU.add).then_inc(var_ready, 1)

            def scale(m):
                c, k = divmod(m, NTAP)
                if m >= 3:
                    dve.wait_ge(rest_ready, m - 2)
                o = ps[:, m % 3, :].rearrange("p (r q) -> p r q", r=4)
                rq = rstd0[:, c * CH:(c + 1) * CH].rearrange("p (q r) -> p r q", r=4)
                if k < K0:
                    nc.vector.tensor_tensor(o, phases(c, k), rq, ALU.mult).then_inc(scaled, 1)
                else:
                    nc.vector.tensor_copy(o, rq).then_inc(scaled, 1)

            def inverse(c):
                part = slice(c * CH, (c + 1) * CH)
                dve.wait_ge(var_ready, (c + 1) * 2 * PAIRS)
                chain(nc.vector.tensor_scalar(rstd0[:, part], var0[:, part], 1.0 / (P - 1), EPS, ALU.mult, ALU.add))
                nc.vector.reciprocal(var0[:, part], rstd0[:, part]).then_inc(inv_ready, 1)
                dve.wait_ge(rstd_ready, c + 1)
                scale(c * NTAP)

            def rest(c, k):
                m = c * NTAP + k
                if k + 1 < NTAP:
                    scale(m + 1)
                dve.wait_ge(high_ready, m + 1)
                if m >= 2:
                    dve.wait_ge(low_ready, m - 1)
                nc.vector.tensor_tensor(rt[:, m % 2, :], ps[:, m % 3, :], S[:, m % SR, 0, :], ALU.subtract)\
                    .then_inc(rest_ready, 1)

            statistics(dve, quadratic, inverse, rest)
            def low0(clip, slot, r):
                dve.wait_ge(h0_high, clip * 4 + (r + 1))
                nc.vector.scalar_tensor_tensor(A0[:, slot, 1, r, 1:T1 + 1], P0[r % 2][:, :], 0.0,
                                               A0[:, slot, 0, r, 1:T1 + 1].bitcast(F32), ALU.max, ALU.subtract)\
                    .then_inc(h0_low, 1)

            def normalise(g, par, n, tile):
                at = norms_before(g) + n
                slot = n % NRING
                dve.wait_ge(spread, at + 1)
                until(dve, relu_done, norms_before(g) + max(n - NRING + 1, 0))
                nc.vector.tensor_tensor(N[:, slot, :], RB[norms_par(g, par, n)][:, :], Y[:, 1 - par, row_of(tile), :], ALU.mult)\
                    .then_inc(n_done, 1)

            def split(g, par, n, tile):
                level, s = tile
                if level == 3:
                    return
                at = norms_before(g) + n
                slot = n % NRING
                dve.wait_ge(relu_done, at + 1)
                if level == 1:
                    src = AF[:, slot, :].rearrange("p (r q) -> p r q", r=2)
                    hi, lo = (A1[:, part, :, s, 1:T2 + 1] for part in range(2))
                    until(dve, conv2_done, (g - 1) * 2)
                else:
                    src = AF[:, slot, :].rearrange("p (r s q) -> p r s q", r=2, s=2)
                    hi, lo = (A2[:, part, :, 2 * s:2 * s + 2, 1:T3 + 1] for part in range(2))
                    until(dve, conv3_done, g - 2)
                nc.vector.tensor_copy(hi, src).then_inc(ah_done, 1)
                dve.wait_ge(ah_done, splits_before(g) + n + 1)
                nc.vector.tensor_tensor(lo, src, hi.bitcast(F32), ALU.subtract).then_inc(al_done, 1)

            for r in range(4):
                low0(0, 0, r)

            def step(g, par):
                norms = tiles_of(g, norm_tiles, FULLN)
                conv1 = has(g, "conv1")
                batch = has(g, "batch")
                if conv1:
                    for r in range(4):
                        low0(g * 4 + 1, 1, r)
                if batch:
                    dve.wait_ge(var_done, convs_before(g))
                    nc.vector.tensor_scalar(vs[:, :], V[0:NTILE + 1, :], 1.0 / (P - 1), EPS, ALU.mult, ALU.add)\
                        .then_inc(vs_done, 1)
                for part, r in ((0, 0), (1, 1), (None, 2), (2, 3), (3, None)):
                    if conv1 and r is not None:
                        low0(g * 4 + 2, 0, r)
                    if batch and part is not None:
                        if part == 0:
                            dve.wait_ge(vs_done, g)
                        c = slice(part * P, (part + 1) * P)
                        nc.vector.reciprocal(iv[:, c], vs[:, c]).then_inc(iv_done, 1)
                if conv1:
                    low0(g * 4 + 3, 1, 0)
                if batch:
                    dve.wait_ge(rs_done, g)
                    until(dve, spread, norms_before(g))
                    nc.vector.tensor_copy(RS[0:NTILE + 1, :], rs[:, :]).then_inc(parts_done, 1)
                    dve.wait_ge(parts_done, g * 5 - 4)
                    nc.vector.tensor_tensor(rr[:, :], rs[:, :], RS[0:NTILE + 1, :], ALU.subtract).then_inc(parts_done, 1)
                if conv1:
                    low0(g * 4 + 3, 1, 1)
                if batch:
                    dve.wait_ge(parts_done, g * 5 - 3)
                    nc.vector.tensor_copy(mt[:, :], rr[:, :]).then_inc(parts_done, 1)
                    dve.wait_ge(parts_done, g * 5 - 2)
                    nc.vector.tensor_tensor(RS[64:64 + NTILE + 1, :], rr[:, :], mt[:, :], ALU.subtract)\
                        .then_inc(parts_done, 1)
                    nc.vector.tensor_copy(RS[32:32 + NTILE + 1, :], mt[:, :]).then_inc(parts_done, 1)
                if conv1:
                    low0(g * 4 + 3, 1, 2)
                    low0(g * 4 + 3, 1, 3)
                for n in range(9):
                    if n < len(norms):
                        normalise(g, par, n, norms[n])
                    if 0 <= n - 2 < len(norms):
                        split(g, par, n - 2, norms[n - 2])
                    if n >= 5 and conv1 and has(g, "next"):
                        low0(g * 4 + 4, 0, n - 5)

            def split_weights():
                dve.wait_ge(mlp_in, 32)
                nc.vector.memset(W3[:, :, :].bitcast(F32), 0.0)
                chain(nc.vector.tensor_copy(W1[:, 0], raw1))
                nc.vector.tensor_tensor(W1[:, 1], raw1, W1[:, 0].bitcast(F32), ALU.subtract)
                w3 = cols[:, CW3:CW3 + KC]
                chain(nc.vector.tensor_copy(W3[:, :, 0], w3))
                nc.vector.tensor_tensor(W3[:, :, 1], w3, W3[:, :, 0].bitcast(F32), ALU.subtract).then_inc(wsetup, 1)
                count[0] += 1

            each_iteration(dve, step, split_weights)

        @block.tensor
        def _(pe):
            pe.wait_ge(c0_in, 16)
            pe.wait_ge(ones_set, 1)
            nc.tensor.matmul(bank[4][:, 0:NTAP], onesC[:, :], c0[:, :], start=True, stop=True).then_inc(gram_steps, 1)
            pe.wait_ge(gram_steps, 2)
            nc.tensor.matmul(bank[5][0:NTAP, 0:NTAP], c0c[:, :], c0c[:, :], start=True, stop=True).then_inc(gram_steps, 1)
            pe.wait_ge(const_in, 80)
            nc.tensor.matmul(bank[4][:, 16:19], onesC[:, :], cols[:, CB:CB + 3], start=True, stop=True)\
                .then_inc(gram_steps, 1)
            pe.wait_ge(tg_in, 16 * (BLK + 1))

            def turn(i, d):
                waits_behind(pe, const_in, 80, (staged, i * 2 + (d + 1)), (xt0_ready, i * 2 + (d - 1)))
                for t in range(SBLK):
                    mm = nc.tensor.transpose(bank[d][0:BW, t * P:(t + 1) * P],
                                             xst[:, d, t * BLK * STR0:t * BLK * STR0 + BW], ident[:, :])
                mm.then_inc(turned, 1)

            def quad(i, d):
                pe.wait_ge(xt0_ready, i * 2 + (d + 1))
                until(pe, var_ready, i * 2 + (d - 1))
                for t in range(SBLK):
                    c = slice(t * BLK * NTAP, (t + 1) * BLK * NTAP)
                    mm = nc.tensor.matmul(bank[2 + d][:, c], XT0[0:BW + 1, d, t * P:(t + 1) * P],
                                          TG[:, :, :].rearrange("j t k -> j (t k)"), start=True, stop=True)
                mm.then_inc(quad_done, 1)

            def quad_behind_turn(i, last=False):
                turn(i, 1)
                quad(i, 0)
                if not last:
                    turn(i + 1, 0)
                quad(i, 1)

            turn(0, 0)
            quad_behind_turn(0)
            with pe.Fori(1, NSTEP // 2 - 1) as i:
                quad_behind_turn(i)
            quad_behind_turn(NSTEP // 2 - 1, True)

            def conv0(clip, r, slot):
                at = clip * 4 + r
                if r == 0:
                    pe.wait_ge(r_in[slot], clip * 12 + (48 - 12 * slot))
                until(pe, h0_low, at - 1)
                nc.tensor.matmul(P0[r % 2][:, :], W0[:, :], R[0:K0ROWS, slot, :].rearrange("p (e r q) -> p r e q", e=2 * CHUNKS, r=4)[:, r], start=True, stop=True)\
                    .then_inc(conv0_done, 1)

            def conv1(g, s, fill):
                clip = g * 4 + s
                pe.wait_ge(h0_pads, clip * 4 + 4)
                until(pe, y_done, left_before(g, s))
                n = 0
                for tap in range(8):
                    m, phase = divmod(tap, 4)
                    r = (phase + 2) % 4
                    o = m + (1 if r < 2 else 0)
                    for w, x in PASSES:
                        mm = nc.tensor.matmul(CONV[s % 2][:, :], wc[:, w, tap, :], A0[:, s % 2, x, r, o:o + T1],
                                              start=(n == 0), stop=(n == 23))
                        n += 1
                        if n == 24:
                            mm.then_inc(conv1_done, 1)
                        elif n in fill:
                            fill[n]()

            def conv_small(g, level, s, fill):
                tile = (level, s)
                until(pe, y_done, left_before(g, tiles_of(g, conv_tiles, FULL).index(tile)))
                n = 0
                first, buf, w = (8, A1, T2) if level == 2 else (12, A2, T3)
                dst = CONV[bank_of(tile)]
                cl = slice(2 * s, 2 * s + 2) if level == 2 else slice(0, 4)
                for tap in range(4):
                    m, phase = divmod(tap, 2)
                    psi = 1 - phase
                    o = m + (1 - psi)
                    for wp, x in PASSES:
                        mm = nc.tensor.matmul(dst[:, :], wc[:, wp, first + tap, :], buf[:, x, psi, cl, o:o + w],
                                              start=(n == 0), stop=(n == 11))
                        n += 1
                        if n in fill:
                            fill[n]()
                mm.then_inc(conv2_done if level == 2 else conv3_done, 1)

            def conv2(g, s, fill):
                norms = tiles_of(g, norm_tiles, FULLN)
                pe.wait_ge(a_pads, 2 * (splits_before(g) + norms.index((1, 2 * s + 1)) + 1))
                conv_small(g, 2, s, fill)

            def conv3(g, fill):
                norms = tiles_of(g, norm_tiles, FULLN)
                pe.wait_ge(a_pads, 2 * (splits_before(g) + norms.index((2, 1)) + 1))
                conv_small(g, 3, 0, fill)

            def variance(g, par, tile):
                tiles = tiles_of(g, conv_tiles, FULL)
                n = tiles.index(tile)
                at = convs_before(g) + n
                slot = n % RING
                pe.wait_ge(sql_done, at + 1)
                if n == 0:
                    until(pe, vs_done, g)
                nc.tensor.matmul(V[:, :], selV[:, row_of(tile), :], sqh[:, slot, :], start=(n == 0), stop=False)
                nc.tensor.matmul(V[:, :], selV[:, row_of(tile), :], sql[:, slot, :], start=False,
                                 stop=(n == len(tiles) - 1)).then_inc(var_done, 1)

            def bcast(g, par, n, tile):
                if n == 0:
                    pe.wait_ge(parts_done, g * 5)
                until(pe, n_done, norms_before(g) + (n - 1))
                nc.tensor.matmul(RB[norms_par(g, par, n)][:, :], selB[:, row_of(tile), :], RS[:, :], start=True, stop=True).then_inc(spread, 1)

            pe.wait_ge(psetup, 1)
            for r in range(4):
                conv0(0, r, 0)

            def step(g, par):
                tiles = tiles_of(g, conv_tiles, FULL)
                norms = tiles_of(g, norm_tiles, FULLN)
                conv1_on = has(g, "conv1")
                pending = list(enumerate(norms))

                def spread_next():
                    if pending:
                        n, tile = pending.pop(0)
                        bcast(g, par, n, tile)

                def patch(r):
                    if conv1_on and has(g, "next"):
                        conv0(g * 4 + 4, r, 0)

                def fills(s):
                    if s == 3:
                        return dict.fromkeys((1, 6, 12, 18), spread_next)
                    f = {1 + 5 * r: lambda r=r: conv0(g * 4 + (s + 1), r, (s + 1) % 4) for r in range(4)}
                    if s == 2:
                        f[20] = spread_next
                    return f

                in_conv3 = {2: spread_next, 4: lambda: patch(0), 9: lambda: patch(1), 10: spread_next}
                in_conv2 = {3: lambda: patch(2), 8: lambda: patch(3)}
                if conv1_on:
                    conv1(g, 0, fills(0))
                for tile in late(g - 1):
                    variance(g - 1, 1 - par, tile)
                if conv1_on:
                    conv1(g, 1, fills(1))
                    variance(g, par, (1, 0))
                    conv1(g, 2, fills(2))
                    variance(g, par, (1, 1))
                    conv1(g, 3, fills(3))
                else:
                    while pending:
                        spread_next()
                if has(g, "conv3"):
                    conv3(g, in_conv3)
                else:
                    for work in in_conv3.values():
                        work()
                if conv1_on:
                    variance(g, par, (1, 2))
                if has(g, "conv2"):
                    conv2(g, 0, in_conv2)
                    conv2(g, 1, {})
                else:
                    for work in in_conv2.values():
                        work()
                while pending:
                    spread_next()
                if conv1_on:
                    variance(g, par, (1, 3))

            each_iteration(pe, step)


MLP_ORDER = ((2, 0), (1, 0), (1, 1), (2, 1), (1, 2), (1, 3), (2, 2), (2, 3))
PASSES = ((0, 0), (0, 1), (1, 0))


def mlp_order(i):
    return [t for t in MLP_ORDER if t[0] == 2 or not isinstance(i, int) or i + 1 < NG]


def mlp_before(i):
    return i * 8 + KC


def mlp_steps(eng, step):
    step(0, 0)
    step(1, 1)
    with eng.Fori(1, NG // 2 - 2) as i:
        for d in range(2):
            step(i * 2 + d, d)
    for i in range(NG - 4, NG):
        step(i, i % 2)


class Half:

    def __init__(self, nc, ctx, i):
        self.rows = slice(i * B // 2, (i + 1) * B // 2)
        self.logits_in, self.steps, self.turned, self.ready = (
            ctx.enter_context(nc.semaphore(f"{name}{i}")) for name in ("logits_in", "imp_steps", "cs_turned", "csT_ready"))


def importance_buffers(sb, i):
    return [sb(f"{name}{i}", [B, width]) for name, width in
            (("imp", T3), ("impn", T3), ("isum", 2), ("ones", T3), ("cs", T3 + 1))]


def importance_add(nc, dve, half, buffers, LG):
    imp, impn, isum, ones, cs = buffers
    r = half.rows
    nc.vector.memset(ones[r, :], 1.0).then_inc(half.steps, 1)
    nc.vector.memset(cs[r, 0:1], 0.0).then_inc(half.steps, 1)
    dve.wait_ge(half.logits_in, 32)
    nc.vector.tensor_tensor(impn[r, :], LG[r, 0, :], LG[r, 1, :], ALU.add).then_inc(half.steps, 1)


def importance_sigmoid(nc, act, half, buffers, b3):
    imp, impn, isum, ones, cs = buffers
    act.wait_ge(half.steps, 3)
    nc.scalar.activation(imp[half.rows, :], impn[half.rows, :], ACT.Sigmoid, bias=b3[half.rows, :])\
        .then_inc(half.steps, 1)


def importance_cumulate(nc, dve, half, buffers):
    imp, impn, isum, ones, cs = buffers
    r = half.rows
    dve.wait_ge(half.steps, 4)
    nc.vector.tensor_scalar(impn[r, :], imp[r, :], TEMP, None, ALU.add).then_inc(half.steps, 1)
    dve.wait_ge(half.steps, 5)
    nc.vector.tensor_reduce(isum[r, 0:1], impn[r, :], AX.X, ALU.add).then_inc(half.steps, 1)
    dve.wait_ge(half.steps, 6)
    nc.vector.reciprocal(isum[r, 1:2], isum[r, 0:1]).then_inc(half.steps, 1)
    dve.wait_ge(half.steps, 7)
    nc.vector.tensor_scalar(imp[r, :], impn[r, :], isum[r, 1:2], float(D), ALU.mult, ALU.mult).then_inc(half.steps, 1)
    dve.wait_ge(half.steps, 8)
    nc.vector.tensor_tensor_scan(cs[r, 1:T3 + 1], ones[r, :], imp[r, :], 0.0, ALU.mult, ALU.add).then_inc(half.steps, 1)


def importance_turn(nc, pe, half, buffers, ident, banks):
    imp, impn, isum, ones, cs = buffers
    r = half.rows
    pe.wait_ge(half.steps, 9)
    for s in range(2):
        nc.tensor.transpose(banks[s][:, 0:B // 2], cs[r, 1 - s:1 - s + T3], ident[r, r]).then_inc(half.turned, 1)


def importance_out(nc, act, half, csT, banks):
    act.wait_ge(half.turned, 2)
    for s in range(2):
        nc.scalar.activation(csT[:, half.rows, s], banks[s][:, 0:B // 2], ACT.Copy).then_inc(half.ready, 1)


def pooling_weights(nc, pool, half, shared, E, steps, before, q, h, free=None):
    LG, b3, iota, csT, WM, wm_ready, halves = shared
    E1, E2, E3 = E
    c = csT[:, bass.ds(q * GS, GS), :].rearrange("p b s -> p (b s)")
    shape = [P, 2 * GS, D + 1]
    nc.gpsimd.tensor_tensor(E1[:, :, :], c.unsqueeze(2).broadcast_to(shape),
                            iota[:, :].unsqueeze(1).broadcast_to(shape), ALU.subtract).then_inc(steps, 1)
    waits_behind(pool, half.ready, 2, (steps, before + 1))
    nc.gpsimd.tensor_scalar(E2[:, :, :], E1[:, :, :], FAR, 0.0, ALU.min, ALU.max).then_inc(steps, 1)
    pool.wait_ge(steps, before + 2)
    nc.gpsimd.tensor_tensor(E3[:, :, :, :].rearrange("p b s n -> p (b s) n"), E2[:, :, 0:D], E2[:, :, 1:D + 1],
                            ALU.subtract).then_inc(steps, 1)
    pool.wait_ge(steps, before + 3)
    if free:
        free()
    nc.gpsimd.tensor_tensor(WM[:, h], E3[:, :, 0, :], E3[:, :, 1, :], ALU.subtract).then_inc(wm_ready, 1)


def pooling_buffers(sb, i):
    return [sb(f"{name}{i}", [P, *shape]) for name, shape in
            (("cs_less_n", (2 * GS, D + 1)), ("above", (2 * GS, D + 1)), ("steps_between", (GS, 2, D)))]


def importance_mlp(nc, a, outer, bank, F, cols, ident, shared, weights):
    LG, b3, iota, csT, WM, wm_ready, halves = shared
    R, W1, W3 = weights
    raw1, raw2 = raw_weights(R)
    with ExitStack() as ctx:
        def sb(name, shape, dt=F32):
            return ctx.enter_context(nc.sbuf_tensor(name, shape, dt))

        def sem(name):
            return outer.enter_context(nc.semaphore(name))

        W2 = sb("W2", [P, 2, KC, DM], F32R)
        Fp = sb("Fp", [P, 2, 2, DM], F32R)
        Z = sb("Z", [P, KC, DM])
        Z1 = sb("Z1", [P, 2, 2, KC, DM], F32R)
        Z2 = sb("Z2", [P, 2, KC, DM], F32R)
        Lrow = sb("Lrow", [2, B * T3])
        mlp_setup = sem("mlp_setup")
        f_high = sem("f_high")
        f_low = sem("f_low")
        z_sums = sem("z_sums")
        z_gelu = sem("z_gelu")
        z_high = sem("z_high")
        z_low = sem("z_low")
        logit_sums = sem("logit_sums")
        logit_rows = sem("logit_rows")
        imp_in = sem("imp_in")
        wm_steps = sem("wm_steps_mlp")
        half, buffers, E = halves[0], importance_buffers(sb, 0), pooling_buffers(sb, 0)

        block = ctx.enter_context(nc.Block())

        @block.sync
        def _(sp):
            for dst, name in ((b3[:, :], "b3"), (iota[:, :], "iota")):
                sp.dma_start(dst, a[name]).then_inc(imp_in, 16)
            for i, hf in enumerate(halves):
                sp.wait_ge(logit_rows, (i + 1) * NG // 2)
                for r in range(2):
                    src = Lrow[r:r + 1, i * B // 2 * T3:(i + 1) * B // 2 * T3].rearrange("p (b t) -> p b t", t=T3)
                    sp.dma_start(LG[hf.rows, r, :], src).then_inc(hf.logits_in, 16)
            sp.wait_ge(halves[1].logits_in, 32)

        @block.gpsimd
        def _(pool):
            pool.wait_ge(imp_in, 32)
            pool.wait_ge(half.ready, 2)
            for q in range(W):
                pooling_weights(nc, pool, half, shared, E, wm_steps, q * 3, q, q)

        @block.scalar
        def _(act):
            def gelu(n, at, layer, m):
                act.wait_ge(z_sums, n + 1)
                until(act, z_low, n - 3)
                b = CM1 + m if layer == 1 else CM2 + m
                nc.scalar.activation(Z[:, at, :], bank[at][:, :], ACT.Gelu, bias=cols[:, b:b + 1]).then_inc(z_gelu, 1)

            def logits(i, par):
                act.wait_ge(logit_sums, i * KC + KC)
                nc.scalar.activation(Lrow[:, bass.ds(i * DM, DM)], bank[4 + par][0:2, :], ACT.Copy).then_inc(logit_rows, 1)

            for m in range(KC):
                gelu(m, m, 1, m)

            def step(i, par):
                for j, (layer, m) in enumerate(mlp_order(i)):
                    gelu(mlp_before(i) + j, j % KC, layer, m)
                    if isinstance(i, int) and (i, j) == (NG - 3, 3):
                        act.wait_ge(imp_in, 32)
                        importance_sigmoid(nc, act, half, buffers, b3)
                    if isinstance(i, int) and (i, j) == (NG - 2, 1):
                        importance_out(nc, act, half, csT, bank[6:8])
                    if j == 1 and not (isinstance(i, int) and i == 0):
                        logits(i - 1, 1 - par)

            mlp_steps(act, step)
            logits(NG - 1, (NG - 1) % 2)

        @block.vector
        def _(dve):
            def split_f(i, par):
                nc.vector.tensor_copy(Fp[:, par, 0, :], F[:, bass.ds(i * DM, DM)]).then_inc(f_high, 1)
                dve.wait_ge(f_high, i + 1)
                nc.vector.tensor_tensor(Fp[:, par, 1, :], F[:, bass.ds(i * DM, DM)], Fp[:, par, 0, :].bitcast(F32),
                                        ALU.subtract).then_inc(f_low, 1)

            def split_z(n, at, hi, lo):
                dve.wait_ge(z_gelu, n + 1)
                nc.vector.tensor_copy(hi, Z[:, at, :]).then_inc(z_high, 1)
                dve.wait_ge(z_high, n + 1)
                nc.vector.tensor_tensor(lo, Z[:, at, :], hi.bitcast(F32), ALU.subtract).then_inc(z_low, 1)

            split_f(0, 0)
            nc.vector.tensor_copy(W2[:, 0], raw2).then_inc(mlp_setup, 1)
            dve.wait_ge(mlp_setup, 1)
            nc.vector.tensor_tensor(W2[:, 1], raw2, W2[:, 0].bitcast(F32), ALU.subtract).then_inc(mlp_setup, 1)
            split_f(1, 1)
            for m in range(KC):
                split_z(m, m, Z1[:, 0, 0, m, :], Z1[:, 0, 1, m, :])

            def step(i, par):
                for j, (layer, m) in enumerate(mlp_order(i)):
                    n = mlp_before(i) + j
                    if layer == 1:
                        split_z(n, j % KC, Z1[:, 1 - par, 0, m, :], Z1[:, 1 - par, 1, m, :])
                    else:
                        until(dve, logit_sums, i * KC + (m - 3))
                        split_z(n, j % KC, Z2[:, 0, m, :], Z2[:, 1, m, :])
                    if isinstance(i, int) and (i, j) == (NG - 3, 1):
                        importance_add(nc, dve, half, buffers, LG)
                    if isinstance(i, int) and (i, j) == (NG - 3, 6):
                        importance_cumulate(nc, dve, half, buffers)
                if not isinstance(i, int) or i + 2 < NG:
                    split_f(i + 2, par)

            mlp_steps(dve, step)

        @block.tensor
        def _(pe):
            def chunk(n, at, layer, m, par):
                until(pe, z_gelu, n - 3)
                k = 0
                depth = 1 if layer == 1 else KC
                for kc in range(depth):
                    for w, x in PASSES:
                        if layer == 1:
                            lhs, rhs = W1[:, w, m * P:(m + 1) * P], Fp[:, par, x, :]
                        else:
                            lhs, rhs = W2[:, w, kc, m * P:(m + 1) * P], Z1[:, par, x, kc, :]
                        mm = nc.tensor.matmul(bank[at][:, :], lhs, rhs, start=(k == 0), stop=(k == 3 * depth - 1))
                        k += 1
                mm.then_inc(z_sums, 1)

            def logits(i, par, m):
                pe.wait_ge(z_low, mlp_before(i) + mlp_order(i).index((2, m)) + 1)
                if m == 0:
                    until(pe, logit_rows, i - 1)
                for x in range(2):
                    mm = nc.tensor.matmul(bank[4 + par][:, :], W3[:, m, :], Z2[:, x, m, :], start=(m == 0 and x == 0),
                                          stop=(m == KC - 1 and x == 1))
                mm.then_inc(logit_sums, 1)

            pe.wait_ge(f_low, 1)
            for m in range(KC):
                chunk(m, m, 1, m, 0)
            pe.wait_ge(mlp_setup, 2)

            def step(i, par):
                order = mlp_order(i)
                for j, (layer, m) in enumerate(order):
                    n = mlp_before(i) + j
                    if j == 0:
                        pe.wait_ge(z_low, KC if isinstance(i, int) and i == 0 else i * 8 + 2)
                    if (layer, m) == (1, 0):
                        pe.wait_ge(f_low, i + 2)
                    chunk(n, j % KC, layer, m, par if layer == 2 else 1 - par)
                    if j == 0 and not (isinstance(i, int) and i == 0):
                        logits(i - 1, 1 - par, 3)
                    elif layer == 2 and m > 0:
                        logits(i, par, m - 1)
                    if isinstance(i, int) and (i, j) == (NG - 2, 0):
                        importance_turn(nc, pe, half, buffers, ident, bank[6:8])

            mlp_steps(pe, step)
            logits(NG - 1, (NG - 1) % 2, 3)


def pool_attend_experts(nc, a, outer, bank, F, cols, ident, shared, out):
    with ExitStack() as ctx:
        def sb(name, shape, dt=F32):
            return ctx.enter_context(nc.sbuf_tensor(name, shape, dt))

        def sem(name):
            return outer.enter_context(nc.semaphore(name))

        LG, b3, iota, csT, WM, wm_ready, halves = shared
        half, buffers, E = halves[1], importance_buffers(sb, 1), pooling_buffers(sb, 1)
        ROUNDS = NG // W
        route = sb("route", [1, B], I32)
        wattn = sb("wattn", [P, 3, P])
        bv = sb("bv", [P, P])
        bo = sb("bo", [P, D])
        wi = sb("wi", [P, P])
        wo = sb("wo", [P, D])
        wx = sb("wx", [P, 2, NE, EW])
        wsh = sb("wsh", [P, 2, EW])
        Fs = sb("Fs", [P, W, GS, T3])
        zero = sb("zero", [P, 2 * GS])
        FT = sb("FT", [P, W, GS, P])
        st = sb("st", [P, W, 3, GS, 6])
        mv = sb("mv", [P, W, 3, GS, 2])
        sd = sb("sd", [P, W, 3, 3, GS])
        Xn = sb("Xn", [P, W, 2, P])
        H0 = sb("H0", [P, W, GS, D])
        Xc = sb("Xc", [P, W, 2, GS, D])
        Xa = sb("Xa", [P, W, 2, GS, D])
        XT = sb("XT", [P, W, 2, 2, P])
        QK = sb("QK", [P, W, 2, 2, P])
        Vt = sb("Vt", [P, W, 2, P])
        mx = sb("mx", [P, W, 2, GS])
        PR = sb("PR", [P, W, GS, P])
        psum_ = sb("prob_sums", [P, W, 2, GS])
        PT = sb("PT", [P, W, GS, P])
        H1 = sb("H1", [P, W, GS, D])
        H1b = sb("H1b", [P, W, GS, D])
        GW = sb("GW", [P, W, GS, 2, EW])
        HF = sb("HF", [P, W, 3, GS, P])
        O = sb("O", [P, W, GS, D])

        tail_in = sem("tail_in")
        experts_sum = sem("experts_sum")
        f_staged = sem("f_staged")
        wm_steps = sem("wm_steps")
        f_turned = sem("f_turned")
        ft_ready = sem("ft_ready")
        pooled = sem("pooled")
        stats = [sem(f"stats{i}") for i in range(3)]
        moments = [sem(f"moments{i}") for i in range(3)]
        var_eps = [sem(f"var_eps{i}") for i in range(3)]
        root = [sem(f"root{i}") for i in range(3)]
        invroot = [sem(f"invroot{i}") for i in range(3)]
        centred = [sem(f"centred{i}") for i in range(2)]
        normed = [sem(f"normed{i}") for i in range(3)]
        norm_turned = [sem(f"norm_turned{i}") for i in range(3)]
        h0_ready = sem("h0_ready")
        xt_ready = [sem(f"xt_ready{i}") for i in range(2)]
        qkv_done = sem("qkv_done")
        qk_ready = sem("qk_ready")
        v_ready = sem("v_ready")
        qk_done = sem("qk_done")
        half_scores = sem("half_scores")
        half_hidden = sem("half_hidden")
        scores_done = sem("scores_done")
        max_done = sem("max_done")
        shift_ready = sem("shift_ready")
        probs_ready = sem("probs_ready")
        inv_sum = sem("inv_sum")
        probs_turned = sem("probs_turned")
        pt_ready = sem("pt_ready")
        attended = sem("attended")
        h1_ready = sem("h1_ready")
        h1b_ready = sem("h1b_ready")
        hidden_done = [sem(f"hidden_done{i}") for i in range(3)]
        hidden_ready = [sem(f"hidden_ready{i}") for i in range(3)]
        experts_in = [sem(f"experts_in{h}") for h in range(W)]
        out_done = sem("out_done")
        o_ready = sem("o_ready")
        stored = [sem(f"stored{h}") for h in range(W)]

        def rounds(steps):
            def one(k, parts):
                at = {"front": k + 1, "attention": k, "experts": k + -1}
                for part, step in steps:
                    if part == "once" and isinstance(k, int) and k == 0:
                        step()
                    elif part in parts:
                        for h in range(W):
                            step(at[part] * W + h, h)
            return one

        def each_round(eng, steps):
            one = rounds(steps)
            one(-1, ("front",))
            one(0, ("attention", "front"))
            with eng.Fori(1, ROUNDS - 1) as k:
                one(k, ("attention", "experts", "front"))
            one(ROUNDS - 1, ("attention", "experts"))
            one(ROUNDS, ("experts",))

        def att(h):
            return bank[h]

        def exp(h):
            return bank[W + h]

        block = ctx.enter_context(nc.Block())

        @block.sync
        def _(sp):
            for dst, name in ((wattn[:, :, :], "attn"), (bv[:, :], "bv"),
                              (bo[:, :], "bo"), (wi[:, :], "wi"), (wo[:, :], "wo"), (wx[:, :, :, :], "wr"),
                              (wsh[:, :, :], "ws"), (route[:, :], "route")):
                sp.dma_start(dst, a[name]).then_inc(tail_in, 16)
            sp.wait_ge(experts_sum, 3)

            def fetch(k, h):
                sp.wait_ge(hidden_ready[2], k * W + (h + 1))
                for c in range(GS):
                    e = sp.value_load(route[0:1, bass.ds(k * (W * GS) + (h * GS + c), 1)], min_val=0, max_val=NE - 1)
                    for l in range(2):
                        sp.dma_start(GW[:, h, c, l, :], wx[:, l, bass.ds(e, 1), :].rearrange("p o w -> p (o w)"))\
                            .then_inc(experts_in[h], 16)

            with sp.Fori(0, NG // W) as k:
                for h in range(W):
                    fetch(k, h)
                for h in range(W):
                    sp.wait_ge(o_ready, k * W + (h + 1 + 2 * W))
                    dst = out[bass.ds(k * (W * GS) + h * GS, GS)].rearrange("b c d -> c b d")
                    sp.dma_start(dst, O[:, h]).then_inc(stored[h], 16)
            for h in range(W):
                sp.wait_ge(stored[h], (ROUNDS + 1) * 16)

        @block.gpsimd
        def _(pool):
            nc.gpsimd.memset(H0[:, :, 0, 0:1], 0.0).then_inc(h1_ready, W)
            nc.gpsimd.memset(H1[:, :, 0, 0:1], 0.0).then_inc(o_ready, 2 * W)
            for h in range(W):
                nc.gpsimd.memset(O[:, h, 0, 0:1], 0.0).then_inc(stored[h], 16)
            nc.gpsimd.memset(Fs[:, :, 0, 0:1], 0.0).then_inc(f_turned, W)
            nc.gpsimd.memset(FT[:, :, 0, 0:1], 0.0).then_inc(pooled, W)
            nc.gpsimd.memset(HF[:, :, 0, 0, 0:1], 0.0).then_inc(hidden_ready[2], W)
            nc.gpsimd.memset(zero[:, :], 0.0).then_inc(wm_steps, 1)
            pool.wait_ge(wm_steps, 1)

            def stage(q, h):
                pool.wait_ge(f_turned, q + 1)
                src = F[:, bass.ds(q * DM, DM)].rearrange("p (b t) -> p b t", b=GS)
                nc.gpsimd.tensor_tensor(Fs[:, h], src, zero[:, 0:GS].unsqueeze(2).broadcast_to([P, GS, T3]), ALU.add)\
                    .then_inc(f_staged, 1)

            def weights(q, h):
                pooling_weights(nc, pool, half, shared, E, wm_steps, q * 3 + (1 - 3 * W), q, h,
                                lambda: pool.wait_ge(pooled, q + 1))

            for h in range(W):
                stage(h, h)
            for step in (stage, weights):
                for h in range(W):
                    step(W + h, h)
            pool.wait_ge(half.ready, 2)
            with pool.Fori(2, ROUNDS) as k:
                for step in (stage, weights):
                    for h in range(W):
                        step(k * W + h, h)

        @block.scalar
        def _(act):
            def root_of(norm, n):
                def f(q, h):
                    act.wait_ge(var_eps[norm], q + 1)
                    nc.scalar.activation(sd[:, h, norm, 1, 0:n], sd[:, h, norm, 0, 0:n], ACT.Sqrt).then_inc(root[norm], 1)
                return f

            def first(q, h):
                act.wait_ge(norm_turned[0], q + 1)
                nc.scalar.activation(H0[:, h].rearrange("p b n -> p (b n)"), att(h)[:, 0:GS * D], ACT.Relu,
                                     scale=cols[:, CG4:CG4 + 1], bias=cols[:, CN4:CN4 + 1]).then_inc(h0_ready, 1)

            def turned(i):
                def f(q, h):
                    act.wait_ge(norm_turned[1 + i], q + 1)
                    nc.scalar.activation(XT[:, h, i].rearrange("p a c -> p (a c)"), (att, exp)[i](h)[:, 0:2 * P], ACT.Copy)\
                        .then_inc(xt_ready[i], 1)
                return f

            def queries_keys(q, h):
                act.wait_ge(qk_done, q + 1)
                for i, b in ((0, CBQ), (1, CBK)):
                    nc.scalar.activation(QK[:, h, i].rearrange("p a c -> p (a c)"), att(h)[:, i * 2 * P:(i + 1) * 2 * P],
                                         ACT.Identity, bias=cols[:, b:b + 1]).then_inc(qk_ready, 1)

            def probs(q, h):
                act.wait_ge(shift_ready, q + 1)
                for c in range(GS):
                    nc.scalar.activation(PR[:, h, c, :], att(h)[:, c * P:(c + 1) * P], ACT.Exp, scale=D ** -0.5,
                                         bias=mx[:, h, 1, c:c + 1], accum_out=psum_[:, h, 0, c:c + 1])\
                        .then_inc(probs_ready, 1)

            def probs_t(q, h):
                act.wait_ge(probs_turned, q + 1)
                nc.scalar.activation(PT[:, h], att(h)[:, :].rearrange("p (b c) -> p b c", b=GS), ACT.Copy)\
                    .then_inc(pt_ready, 1)

            def hidden0(q, h):
                act.wait_ge(hidden_done[0], q + 1)
                nc.scalar.activation(HF[:, h, 0].rearrange("p b c -> p (b c)"), exp(h)[:, :], ACT.Relu,
                                     bias=cols[:, CBI:CBI + 1]).then_inc(hidden_ready[0], 1)

            def hidden(l):
                def f(q, h):
                    act.wait_ge(hidden_done[1 + l], q + 1)
                    for c in range(GS):
                        clip = (c % 2) * 2 + c // 2
                        ins = nc.scalar.activation(HF[:, h, 1 + l, c, :], exp(h)[:, c * P:(c + 1) * P], ACT.Relu,
                                                   bias=GW[:, h, clip, l, P:EW])
                    ins.then_inc(hidden_ready[1 + l], 1)
                return f

            Fr, A, E = "front", "attention", "experts"
            each_round(act, [(A, first), ("once", lambda: importance_sigmoid(nc, act, half, buffers, b3)),
                             (E, root_of(2, GS)), ("once", lambda: importance_out(nc, act, half, csT, bank[6:8])),
                             (E, turned(1)), (A, root_of(1, GS)), (E, hidden0), (A, turned(0)), (A, queries_keys),
                             (E, hidden(0)), (E, hidden(1)), (A, probs), (A, probs_t), (Fr, root_of(0, 2))])

        @block.vector
        def _(dve):
            def moments_of(norm, n, src, ready, unbias):
                def stat(q, h):
                    dve.wait_ge(ready, q + (1 if norm == 1 else 1 + W))
                    for j in range(n):
                        nc.vector.bn_stats(st[:, h, norm, j, :], src(h, j)).then_inc(stats[norm], 1)

                def aggr(q, h):
                    waits_behind(dve, tail_in, 128, (stats[norm], q * n + n))
                    for j in range(n):
                        nc.vector.bn_aggr(mv[:, h, norm, j, :], st[:, h, norm, j, :]).then_inc(moments[norm], 1)

                def eps(q, h):
                    dve.wait_ge(moments[norm], q * n + n)
                    nc.vector.tensor_scalar(sd[:, h, norm, 0, 0:n], mv[:, h, norm, 0:n, 1], unbias, EPS, ALU.mult, ALU.add)\
                        .then_inc(var_eps[norm], 1)

                def inv(q, h):
                    dve.wait_ge(root[norm], q + 1)
                    nc.vector.reciprocal(sd[:, h, norm, 2, 0:n], sd[:, h, norm, 1, 0:n]).then_inc(invroot[norm], 1)

                return [stat, aggr, eps, inv]

            def features(q, h):
                dve.wait_ge(f_turned, q + (1 + W))
                nc.vector.tensor_copy(FT[:, h], exp(h)[:, :].rearrange("p (b c) -> p b c", b=GS)).then_inc(ft_ready, 1)

            def norm_pooled(q, h):
                dve.wait_ge(invroot[0], q + 1)
                for j in range(2):
                    nc.vector.tensor_scalar(Xn[:, h, j, :], exp(h)[:, j * P:(j + 1) * P], mv[:, h, 0, j, 0:1],
                                            sd[:, h, 0, 2, j:j + 1], ALU.subtract, ALU.mult).then_inc(normed[0], 1)

            def layer_norm(i, src):
                def centre(q, h):
                    nc.vector.tensor_tensor(Xc[:, h, i], src(h), mv[:, h, 1 + i, :, 0:1].broadcast_to([P, GS, D]),
                                            ALU.subtract).then_inc(centred[i], 1)

                def scale(q, h):
                    dve.wait_ge(invroot[1 + i], q + 1)
                    dve.wait_ge(centred[i], q + 1)
                    nc.vector.tensor_tensor(Xa[:, h, i], Xc[:, h, i],
                                            sd[:, h, 1 + i, 2, :].unsqueeze(2).broadcast_to([P, GS, D]), ALU.mult)\
                        .then_inc(normed[1 + i], 1)
                return centre, scale

            def values(q, h):
                dve.wait_ge(qkv_done, q + 1)
                nc.vector.tensor_tensor(Vt[:, h], att(h)[:, 0:2 * P].rearrange("p (a c) -> p a c", a=2),
                                        bv[:, :].unsqueeze(1).broadcast_to([P, 2, P]), ALU.add).then_inc(v_ready, 1)

            def maxima(q, h):
                dve.wait_ge(scores_done, q + 1)
                nc.vector.tensor_reduce(mx[:, h, 0, :], att(h)[:, :].rearrange("p (b c) -> p b c", b=GS), AX.X, ALU.max)\
                    .then_inc(max_done, 1)

            def shift(q, h):
                dve.wait_ge(max_done, q + 1)
                nc.vector.tensor_scalar(mx[:, h, 1, :], mx[:, h, 0, :], -D ** -0.5, None, ALU.mult).then_inc(shift_ready, 1)

            def inv_sums(q, h):
                dve.wait_ge(probs_ready, q * GS + GS)
                nc.vector.reciprocal(psum_[:, h, 1, :], psum_[:, h, 0, :]).then_inc(inv_sum, 1)

            def residual(q, h):
                dve.wait_ge(attended, q + 1)
                dve.wait_ge(inv_sum, q + 1)
                for c in range(GS):
                    ins = nc.vector.scalar_tensor_tensor(H1[:, h, c, :], att(h)[:, c * D:(c + 1) * D],
                                                         psum_[:, h, 1, c:c + 1], H0[:, h, c, :], ALU.mult, ALU.add)
                ins.then_inc(h1_ready, 1)

            def with_bias(q, h):
                dve.wait_ge(h1_ready, q + (1 + W))
                nc.vector.tensor_tensor(H1b[:, h], H1[:, h], bo[:, :].unsqueeze(1).broadcast_to([P, GS, D]), ALU.add)\
                    .then_inc(h1b_ready, 1)

            def outputs(q, h):
                dve.wait_ge(out_done, q + 1)
                dve.wait_ge(h1b_ready, q + 1)
                dve.wait_ge(stored[h], (q + -h) * (16 // W) + 16)
                nc.vector.tensor_tensor(O[:, h].rearrange("p b d -> p (b d)"), exp(h)[:, 0:GS * D],
                                        H1b[:, h].rearrange("p b d -> p (b d)"), ALU.add).then_inc(o_ready, 1)

            def sum_experts(part):
                dve.wait_ge(tail_in, 128)
                if part < 2:
                    shared_part = wsh[:, part, :].unsqueeze(1).broadcast_to([P, NE, EW])
                    nc.vector.tensor_tensor(wx[:, part], wx[:, part], shared_part, ALU.add).then_inc(experts_sum, 1)
                else:
                    dve.wait_ge(experts_sum, 2)
                    mats = wx[:, :, :, 0:P].rearrange("p l e h -> p (l e) h")
                    nc.vector.tensor_tensor(mats, mats, ident[:, :].unsqueeze(1).broadcast_to([P, 2 * NE, P]), ALU.add)\
                        .then_inc(experts_sum, 1)

            n0 = moments_of(0, 2, lambda h, j: exp(h)[:, j * P:(j + 1) * P], pooled, P / (P - 1))
            n1 = moments_of(1, GS, lambda h, j: H0[:, h, j, :], h0_ready, 1.0)
            n2 = moments_of(2, GS, lambda h, j: H1[:, h, j, :], h1_ready, 1.0)
            c1, s1 = layer_norm(0, lambda h: H0[:, h])
            c2, s2 = layer_norm(1, lambda h: H1[:, h])
            Fr, A, E = "front", "attention", "experts"
            each_round(dve, [(A, n0[3]), ("once", lambda: importance_add(nc, dve, half, buffers, LG)),
                             (A, norm_pooled), (E, n2[0]), (E, n2[1]), (E, n2[2]), (E, c2), (E, n2[3]), (E, s2),
                             (A, n1[0]), ("once", lambda: importance_cumulate(nc, dve, half, buffers)), (A, n1[1]),
                             (A, n1[2]), (A, c1), (A, n1[3]), (A, s1), ("once", lambda: sum_experts(0)),
                             (E, with_bias), (A, values), ("once", lambda: sum_experts(1)), (A, maxima), (A, shift),
                             (E, outputs), (Fr, features), (Fr, n0[0]), (Fr, n0[1]), (Fr, n0[2]), (A, inv_sums),
                             ("once", lambda: sum_experts(2)), (A, residual)])

        @block.tensor
        def _(pe):
            def turn_features(q, h):
                pe.wait_ge(o_ready, q + 1)
                pe.wait_ge(f_staged, q + 1)
                for c in range(GS):
                    mm = nc.tensor.transpose(exp(h)[:, c * P:(c + 1) * P], Fs[:, h, c, :], ident[:, :])
                mm.then_inc(f_turned, 1)

            def pool_time(q, h):
                pe.wait_ge(ft_ready, q + 1)
                pe.wait_ge(wm_ready, q + 1)
                for c in range(GS):
                    pair, one = divmod(c, 2)
                    mm = nc.tensor.matmul(exp(h)[one * D:(one + 1) * D, pair * P:(pair + 1) * P], WM[:, h, c, :],
                                          FT[:, h, c, :], start=True, stop=True)
                mm.then_inc(pooled, 1)

            def turn_pooled(q, h):
                pe.wait_ge(h1_ready, q + 1)
                pe.wait_ge(normed[0], q * 2 + 2)
                for j in range(2):
                    mm = nc.tensor.transpose(att(h)[:, j * P:(j + 1) * P], Xn[:, h, j, :], ident[:, :])
                mm.then_inc(norm_turned[0], 1)

            def turn_normed(i):
                def f(q, h):
                    pe.wait_ge(normed[1 + i], q + 1)
                    for j in range(2):
                        src = Xa[:, h, i, 2 * j:2 * j + 2, :].rearrange("p b d -> p (b d)")
                        mm = nc.tensor.transpose((att, exp)[i](h)[:, j * P:(j + 1) * P], src, ident[:, :])
                    mm.then_inc(norm_turned[1 + i], 1)
                return f

            def queries_keys(q, h):
                pe.wait_ge(tail_in, 128)
                pe.wait_ge(xt_ready[0], q + 1)
                x = XT[:, h, 0].rearrange("p a c -> p (a c)")
                for i in range(2):
                    mm = nc.tensor.matmul(att(h)[:, i * 2 * P:(i + 1) * 2 * P], wattn[:, i, :], x, start=True, stop=True)
                mm.then_inc(qk_done, 1)

            def values(q, h):
                pe.wait_ge(qk_ready, q * 2 + 2)
                for j in range(2):
                    mm = nc.tensor.matmul(att(h)[:, j * P:(j + 1) * P], XT[:, h, 0, j, :], wattn[:, 2, :], start=True,
                                          stop=True)
                mm.then_inc(qkv_done, 1)

            def scores(one):
                def f(q, h):
                    if one == 0:
                        pe.wait_ge(v_ready, q + 1)
                    else:
                        pe.wait_ge(half_scores, q + 1)
                    r = slice(one * D, (one + 1) * D)
                    for pair in range(2):
                        c = 2 * pair + one
                        mm = nc.tensor.matmul(att(h)[:, c * P:(c + 1) * P], QK[r, h, 0, pair, :], QK[r, h, 1, pair, :],
                                              start=True, stop=True)
                    mm.then_inc((half_scores, scores_done)[one], 1)
                return f

            def turn_probs(q, h):
                pe.wait_ge(probs_ready, q * GS + GS)
                for c in range(GS):
                    mm = nc.tensor.transpose(att(h)[:, c * P:(c + 1) * P], PR[:, h, c, :], ident[:, :])
                mm.then_inc(probs_turned, 1)

            def attend(q, h):
                pe.wait_ge(pt_ready, q + 1)
                pe.wait_ge(v_ready, q + 1)
                for c in range(GS):
                    pair, one = divmod(c, 2)
                    mm = nc.tensor.matmul(att(h)[:, c * D:(c + 1) * D], PT[:, h, c, :],
                                          Vt[:, h, pair, one * D:(one + 1) * D], start=True, stop=True)
                mm.then_inc(attended, 1)

            def hidden0(one):
                def f(q, h):
                    if one == 0:
                        pe.wait_ge(xt_ready[1], q + 1)
                    else:
                        pe.wait_ge(half_hidden, q + 1)
                    r = slice(one * D, (one + 1) * D)
                    nc.tensor.matmul(exp(h)[:, one * 2 * P:(one + 1) * 2 * P], wi[r, :],
                                     XT[r, h, 1].rearrange("p a c -> p (a c)"), start=True, stop=True)\
                        .then_inc((half_hidden, hidden_done[0])[one], 1)
                return f

            def hidden(l):
                def f(q, h):
                    pe.wait_ge(hidden_ready[l], q + 1)
                    if l == 0:
                        fetched(q, h)
                    for c in range(GS):
                        clip = (c % 2) * 2 + c // 2
                        mm = nc.tensor.matmul(exp(h)[:, c * P:(c + 1) * P], GW[:, h, clip, l, 0:P],
                                              HF[:, h, l, c, :], start=True, stop=True)
                    mm.then_inc(hidden_done[1 + l], 1)
                return f

            def outputs(q, h):
                pe.wait_ge(hidden_ready[2], q + (1 + W))
                for c in range(GS):
                    clip = (c % 2) * 2 + c // 2
                    mm = nc.tensor.matmul(exp(h)[:, clip * D:(clip + 1) * D], HF[:, h, 2, c, :], wo[:, :], start=True,
                                          stop=True)
                mm.then_inc(out_done, 1)

            def fetched(q, h):
                pe.wait_ge(experts_in[h], (q + -h) * (2 * GS * 16 // W) + 2 * GS * 16)

            Fr, A, E = "front", "attention", "experts"
            each_round(pe, [(A, turn_pooled), (E, turn_normed(1)), (E, hidden0(0)),
                            ("once", lambda: importance_turn(nc, pe, half, buffers, ident, bank[6:8])),
                            (E, hidden0(1)), (A, turn_normed(0)), (A, queries_keys), (A, values), (E, hidden(0)),
                            (A, scores(0)), (E, hidden(1)), (A, scores(1)), (E, outputs),
                            ("once", lambda: pe.wait_ge(half.ready, 2)), (Fr, turn_features), (Fr, pool_time),
                            (A, turn_probs), (A, attend)])


def raw_weights(R):
    flat = R[:, :, :].bitcast(F32).rearrange("p s t -> p (s t)")
    return flat[:, 0:DM], flat[:, DM:DM + KC * DM].rearrange("p (k n) -> p k n", k=KC)


def bank_of(tile):
    return 2 if tile[0] == 3 else tile[1] % 2


def left_before(g, n):
    bank = bank_of(tiles_of(g, conv_tiles, FULL)[n])
    for back in range(4):
        tiles = FULL if not isinstance(g, int) else conv_tiles(g - back) if g >= back else []
        for m in reversed(range(n if back == 0 else len(tiles))):
            if bank_of(tiles[m]) == bank:
                return convs_before(g - back) + (m + 1)
    return 0


def late(g):
    return [t for t in tiles_of(g, conv_tiles, FULL) if t[0] != 1] if not isinstance(g, int) or g >= 0 else []


def row_of(tile):
    return {1: ROW1, 2: ROW2, 3: ROW3}[tile[0]] + tile[1]


def summed_before(g, n):
    return convs_before(g) + max(n - RING + 1, 0)


def norms_par(g, par, n):
    return (norms_before(g) + n) % 2 if isinstance(g, int) else (NTILE * par + norms_before(3) - NTILE * 3 + n) % 2


def splits_before(g):
    if isinstance(g, int):
        return sum(len([t for t in norm_tiles(i) if t[0] != 3]) for i in range(g))
    return g * 6 + (10 - 18)


def patches(xs, i, d):
    w = STEP_T * STR0
    first = xs[:, bass.ds(i * (2 * w) + d * w, w + STR0)]
    return bass.AP(first.tensor, first.offset, [(XW, P), (STR0, STEP_T), (1, K0)])


def kernel(**x):
    import numpy as np
    import concourse.bacc as bacc
    from concourse.bass_utils import run_bass_kernel_spmd

    x = {k.replace("L0_", ""): np.asarray(v) for k, v in x.items()}
    f = np.float32

    def tap_major(w):
        return w.transpose(1, 2, 0)

    rows = np.zeros((K0ROWS, 2, P), f)
    kind = np.zeros((K0ROWS, 4), f)
    for q in range(3):
        for part in range(3):
            r = ROWS * q + NTAP * part
            rows[r:r + K0, 0] = x["tok_conv0_w"][:, 0, :].T
            rows[r + K0, 0] = x["tok_conv0_b"]
            rows[r:r + NTAP, 1] = x["tok_n0_w"]
            kind[r:r + NTAP, 0] = 1
        rows[ROWS * q + 3 * NTAP, 0] = x["tok_n0_b"]
        rows[ROWS * q + 3 * NTAP, 1] = 1
        kind[ROWS * q:ROWS * (q + 1), 1 + q] = 1
    sel = np.zeros((96, NTILE, P), f)
    for j in range(NTILE):
        sel[[j, 32 + j, 64 + j], j] = 1
    two = lambda v: np.concatenate([v, v])
    arrays = {
        "xpad": np.pad(x["x"][:, 0, :], ((0, 0), (3, 3)), mode="reflect"),
        "c0": np.concatenate([x["tok_conv0_w"][:, 0, :], x["tok_conv0_b"][:, None]], 1),
        "w0": rows, "w0k": kind, "selB": sel, "ident": np.eye(P, dtype=f),
        "wconv": np.concatenate([tap_major(x[f"tok_conv{i}_w"]) for i in (1, 2, 3)], 1),
        "cols": np.stack([x[f"tok_conv{i}_b"] for i in (1, 2, 3)] + [x[f"tok_n{i}_w"] for i in (1, 2, 3)]
                         + [x[f"tok_n{i}_b"] for i in (1, 2, 3)] + [x["tok_n4_w"], x["tok_n4_b"]]
                         + list(x["tok_mlp_b1"].reshape(KC, P)) + list(x["tok_mlp_b2"].reshape(KC, P))
                         + list(x["tok_mlp_w3"].reshape(KC, P)) + [two(x["attn_bq"]), two(x["attn_bk"]), x["ffn_bi"]], 1),
    }
    def pair(m):
        z = np.zeros((2, D, 2, D), f)
        z[0, :, 0] = z[1, :, 1] = m
        return z.reshape(P, P)

    arrays.update({
        "mlp1": x["tok_mlp_w1"], "mlp2": x["tok_mlp_w2"].reshape(KC, P, DM).transpose(1, 0, 2),
        "b3": np.repeat(x["tok_mlp_b3"][:, None], B, 0),
        "iota": np.tile(np.append(np.arange(D), FAR).astype(f), (P, 1)),
        "attn": np.stack([pair(x[f"attn_W{c}"]) for c in "qkv"], 1),
        "bv": np.tile(two(x["attn_bv"]), (P, 1)), "bo": np.tile(x["ffn_bo"], (P, 1)),
        "wi": two(x["ffn_Wi"].T), "wo": x["ffn_Wo"].T,
        "wr": np.concatenate([x["ffn_Wr"].transpose(3, 0, 1, 2), x["ffn_br"].transpose(2, 0, 1)[..., None]], 3),
        "ws": np.concatenate([x["ffn_Ws"].transpose(3, 0, 1, 2), x["ffn_bs"].transpose(2, 0, 1)[..., None]], 3)[:, :, 0],
        "route": x["ffn_route_id"][None, :],
    })
    arrays = {k: np.ascontiguousarray(v) for k, v in arrays.items()}
    nc = bacc.Bacc("TRN2", target_bir_lowering=False, num_devices=1)
    aps = {k: nc.dram_tensor("in_" + k, v.shape, mybir.dt.from_np(v.dtype), kind="ExternalInput").ap() for k, v in arrays.items()}
    out = nc.dram_tensor("out", (B, P, D), F32, kind="ExternalOutput").ap()
    audio_kernel(nc, aps, out)
    r = run_bass_kernel_spmd(nc, [{"in_" + k: v for k, v in arrays.items()}], core_ids=[0])
    return r.results[0]["out"]
```
